# Optimizing a Trainium2 kernel written in Bass

```python
import numpy as np
import jax
import jax.numpy as jnp

def _softmax(x, axis=-1):
    return jax.nn.softmax(x, axis=axis)

def _gelu(x):
    return jax.nn.gelu(x, approximate=True)

def _silu(x):
    return jax.nn.silu(x)

def _sigmoid(x):
    return jax.nn.sigmoid(x)

def _layernorm(x, axis=-1, eps=1e-05):
    m = jnp.mean(x, axis=axis, keepdims=True)
    v = jnp.var(x, axis=axis, keepdims=True)
    return (x - m) / jnp.sqrt(v + eps)

def _scatter_add(tgt, idx, src, axis=0):
    return tgt.at[idx].add(src)

def _segment_sum(src, seg, n):
    return jax.ops.segment_sum(src, seg, n)
kernel_name = 'mk_decoder_preln_d2_seqx_r8_a08e44'

def setup_inputs(seed: int=0):
    np.random.seed(seed)
    _w = jnp.asarray

    def _rec_inputs():
        import jax
        import jax.numpy as jnp
        _rk = jax.random.key(seed)
        x = -0.0002928 + 1 * jax.random.normal(jax.random.fold_in(_rk, 1), (4, 256, 128), jnp.float32)
        _lenS = 256 - jax.random.randint(jax.random.fold_in(_rk, 7), (4,), 0, max(1, 256 // 4) + 1, jnp.int32)
        _lenS2 = 256 - jax.random.randint(jax.random.fold_in(_rk, 8), (4,), 0, max(1, 256 // 4) + 1, jnp.int32)
        _ctx_1024P = jax.random.normal(jax.random.fold_in(_rk, 11), (4, 16, 128), jnp.float32)
        _ctx_1024c = jax.random.dirichlet(jax.random.fold_in(_rk, 511), 0.3 * jnp.ones((16,), jnp.float32), (4, 256))
        _ctx_1024t = jnp.einsum('bsk,bkd->bsd', _ctx_1024c, _ctx_1024P)
        _ctx_1024t = _ctx_1024t * jax.lax.rsqrt(jnp.mean(jnp.square(_ctx_1024t)) + 1e-12) * 0.953939
        ctx_1024 = -1.39393e-06 + 0.999914 * (_ctx_1024t + 0.3 * jax.random.normal(jax.random.fold_in(_rk, 611), (4, 256, 128), jnp.float32))
        _validS = jnp.arange(256)[None, :] < _lenS[:, None]
        _validS2 = jnp.arange(256)[None, :] < _lenS2[:, None]
        _causal = jnp.tril(jnp.ones((256, 256), dtype=bool))
        mask_BxS2_bf0 = jnp.logical_not(jnp.ones((4, 256), dtype=bool))
        return (x, ctx_1024, mask_BxS2_bf0)
    x, ctx_1024, mask_BxS2_bf0 = _rec_inputs()

    def _L0_attn_setup():
        import jax, jax.numpy as jnp
        import numpy as np
        B, S, D, H = (2, 256, 128, 16)
        HD = D // H
        EPS = 1e-05
        key = jax.random.key(seed)
        kx, kq, kk, kv, kb = jax.random.split(key, 5)
        sc = 0.02
        return {'x': jax.random.normal(kx, (B, S, D), dtype=jnp.float32), 'Wq': jax.random.normal(kq, (D, D), dtype=jnp.float32) * sc, 'Wk': jax.random.normal(kk, (D, D), dtype=jnp.float32) * sc, 'Wv': jax.random.normal(kv, (D, D), dtype=jnp.float32) * sc, 'rel_bias_table': jax.random.normal(kb, (2 * S - 1, H), dtype=jnp.float32) * sc, 'ln_gamma': jnp.ones((D,), dtype=jnp.float32), 'ln_beta': jnp.zeros((D,), dtype=jnp.float32)}
    _L0_attn_all = _L0_attn_setup()
    _L0_attn_in = {k: v for k, v in _L0_attn_all.items() if k in ('Wq', 'Wk', 'Wv', 'rel_bias_table', 'ln_gamma', 'ln_beta')}
    del _L0_attn_all

    def _L0_xattn_setup():
        import jax, jax.numpy as jnp
        import numpy as np
        DIM = 128
        HEADS = 16
        DIM_HEAD = 64
        INNER = HEADS * DIM_HEAD
        B, N = (2, 256)
        SCALE = DIM_HEAD ** (-0.5)
        key = jax.random.key(seed)
        ks = jax.random.split(key, 9)
        s_in = 1.0 / np.sqrt(DIM)
        s_inner = 1.0 / np.sqrt(INNER)
        return {'q': jax.random.normal(ks[0], (B, N, DIM), jnp.float32), 'k': jax.random.normal(ks[1], (B, N, DIM), jnp.float32), 'v': jax.random.normal(ks[2], (B, N, DIM), jnp.float32), 'Wq': jax.random.normal(ks[3], (DIM, INNER), jnp.float32) * s_in, 'Wk': jax.random.normal(ks[4], (DIM, INNER), jnp.float32) * s_in, 'Wv': jax.random.normal(ks[5], (DIM, INNER), jnp.float32) * s_in, 'Wo': jax.random.normal(ks[6], (INNER, DIM), jnp.float32) * s_inner, 'bo': jax.random.normal(ks[7], (DIM,), jnp.float32) * s_inner, 'mask': jnp.zeros((B, N), dtype=bool)}
    _L0_xattn_all = _L0_xattn_setup()
    _L0_xattn_in = {k: v for k, v in _L0_xattn_all.items() if k in ('Wq', 'Wk', 'Wv', 'Wo', 'bo')}
    del _L0_xattn_all

    def _L0_ffn_setup():
        import jax, jax.numpy as jnp
        import numpy as np
        B, S, D_MODEL, D_HIDDEN = (4, 256, 128, 512)

        def act_quant(x):
            scale = 127.0 / jnp.clip(jnp.max(jnp.abs(x), axis=-1, keepdims=True), 1e-05)
            return jnp.clip(jnp.round(x * scale), -128, 127) / scale

        def weight_quant(w):
            scale = 1.0 / jnp.clip(jnp.mean(jnp.abs(w)), 1e-05)
            return jnp.clip(jnp.round(w * scale), -1, 1) / scale

        def bit_linear(x, w):
            xq = x + jax.lax.stop_gradient(act_quant(x) - x)
            wq = w + jax.lax.stop_gradient(weight_quant(w) - w)
            return jnp.einsum('bsd,hd->bsh', xq, wq)

        def depthwise_conv1d(x_bcl, w, b):
            y = jax.lax.conv_general_dilated(x_bcl, w, window_strides=(1,), padding=[(1, 1)], dimension_numbers=('NCH', 'OIH', 'NCH'), feature_group_count=x_bcl.shape[1])
            return y + b[None, :, None]
        key = jax.random.key(seed)
        ks = jax.random.split(key, 5)
        lim1 = 1.0 / np.sqrt(D_MODEL)
        lim2 = 1.0 / np.sqrt(D_HIDDEN)
        limc = 1.0 / np.sqrt(3.0)
        return {'x': jax.random.normal(ks[0], (B, S, D_MODEL), dtype=jnp.float32), 'w1': jax.random.uniform(ks[1], (D_HIDDEN, D_MODEL), jnp.float32, -lim1, lim1), 'conv_w': jax.random.uniform(ks[2], (D_HIDDEN, 1, 3), jnp.float32, -limc, limc), 'conv_b': jax.random.uniform(ks[3], (D_HIDDEN,), jnp.float32, -limc, limc), 'w2': jax.random.uniform(ks[4], (D_MODEL, D_HIDDEN), jnp.float32, -lim2, lim2)}
    _L0_ffn_all = _L0_ffn_setup()
    _L0_ffn_in = {k: v for k, v in _L0_ffn_all.items() if k in ('w1', 'conv_w', 'conv_b', 'w2')}
    del _L0_ffn_all

    def _L1_attn_setup():
        import jax, jax.numpy as jnp
        import numpy as np
        D_IN = 128
        D_OUT = 128
        H = 16
        G = 4
        LF = 2
        HEAD_OUT = D_OUT // H
        DQ = HEAD_OUT // LF
        B, T = (2, 256)

        def _alibi_bias(T, dtype):
            slopes = jnp.asarray(2.0 ** (-8.0 * np.arange(1, H + 1) / H), dtype=dtype)
            pos = jnp.arange(T)
            rel = (pos[None, :] - pos[:, None]).astype(dtype)
            return slopes[:, None, None] * rel[None, :, :]
        key = jax.random.key(seed)
        ks = jax.random.split(key, 7)
        s = 0.02
        return {'x': jax.random.normal(ks[0], (B, T, D_IN), dtype=jnp.float32), 'Wq': jax.random.normal(ks[1], (D_IN, D_OUT // LF), dtype=jnp.float32) * s, 'Wk': jax.random.normal(ks[2], (D_IN, D_OUT // LF // G), dtype=jnp.float32) * s, 'Wv': jax.random.normal(ks[3], (D_IN, D_OUT // G), dtype=jnp.float32) * s, 'Wp': jax.random.normal(ks[4], (D_OUT, D_OUT), dtype=jnp.float32) * s, 'bp': jnp.zeros((D_OUT,), dtype=jnp.float32)}
    _L1_attn_all = _L1_attn_setup()
    _L1_attn_in = {k: v for k, v in _L1_attn_all.items() if k in ('Wq', 'Wk', 'Wv', 'Wp', 'bp')}
    del _L1_attn_all

    def _L1_xattn_setup():
        import math
        import jax, jax.numpy as jnp
        import numpy as np
        D_MODEL, N_HEADS, D_K = (128, 16, 64)
        B, S = (4, 512)
        key = jax.random.key(seed)
        ks = jax.random.split(key, 11)
        scale = 1.0 / math.sqrt(D_MODEL)
        hd = N_HEADS * D_K
        return {'query': jax.random.normal(ks[0], (B, S, D_MODEL), jnp.float32), 'key': jax.random.normal(ks[1], (B, S, D_MODEL), jnp.float32), 'value': jax.random.normal(ks[2], (B, S, D_MODEL), jnp.float32), 'Wq': jax.random.normal(ks[3], (hd, D_MODEL), jnp.float32) * scale, 'bq': jnp.zeros((hd,), jnp.float32), 'Wk': jax.random.normal(ks[4], (hd, D_MODEL), jnp.float32) * scale, 'bk': jnp.zeros((hd,), jnp.float32), 'Wv': jax.random.normal(ks[5], (hd, D_MODEL), jnp.float32) * scale, 'bv': jnp.zeros((hd,), jnp.float32), 'Wo': jax.random.normal(ks[6], (D_MODEL, hd), jnp.float32) * scale, 'bo': jnp.zeros((D_MODEL,), jnp.float32)}
    _L1_xattn_all = _L1_xattn_setup()
    _L1_xattn_in = {k: v for k, v in _L1_xattn_all.items() if k in ('Wq', 'bq', 'Wk', 'bk', 'Wv', 'bv', 'Wo', 'bo')}
    del _L1_xattn_all

    def _L1_ffn_setup():
        import jax, jax.numpy as jnp
        import numpy as np
        E = 8
        TOP_K = 2
        ROUTE_SCALE = 1.0
        ALPHA = 1.702
        LIMIT = 7.0
        D = 128
        F = 128
        B, S = (2, 128)

        def swiglu(h):
            g = jnp.minimum(h[..., ::2], LIMIT)
            l = jnp.clip(h[..., 1::2], -LIMIT, LIMIT)
            return g * jax.nn.sigmoid(ALPHA * g) * (l + 1.0)
        if __name__ == '__main__':
            out = reference(**setup_inputs())
            print(out.shape, out.dtype)
        key = jax.random.key(seed)
        ks = jax.random.split(key, 16)
        sd = 1.0 / np.sqrt(D)
        sf = 1.0 / np.sqrt(F)
        return {'x': jax.random.normal(ks[0], (B, S, D), jnp.float32), 'gate_w': jax.random.normal(ks[1], (E, D), jnp.float32) * sd, 'gate_b': jax.random.normal(ks[2], (E,), jnp.float32) * 0.01, 'w1': jax.random.normal(ks[3], (E, 2 * F, D), jnp.float32) * sd, 'b1': jax.random.normal(ks[4], (E, 2 * F), jnp.float32) * 0.01, 'w3': jax.random.normal(ks[5], (E, 2 * F, D), jnp.float32) * sd, 'b3': jax.random.normal(ks[6], (E, 2 * F), jnp.float32) * 0.01, 'w2': jax.random.normal(ks[7], (E, D, F), jnp.float32) * sf, 'b2': jax.random.normal(ks[8], (E, D), jnp.float32) * 0.01, 'sw1': jax.random.normal(ks[9], (2 * F, D), jnp.float32) * sd, 'sb1': jax.random.normal(ks[10], (2 * F,), jnp.float32) * 0.01, 'sw3': jax.random.normal(ks[11], (2 * F, D), jnp.float32) * sd, 'sb3': jax.random.normal(ks[12], (2 * F,), jnp.float32) * 0.01, 'sw2': jax.random.normal(ks[13], (D, F), jnp.float32) * sf, 'sb2': jax.random.normal(ks[14], (D,), jnp.float32) * 0.01}
    _L1_ffn_all = _L1_ffn_setup()
    _L1_ffn_in = {k: v for k, v in _L1_ffn_all.items() if k in ('gate_w', 'gate_b', 'w1', 'b1', 'w3', 'b3', 'w2', 'b2', 'sw1', 'sb1', 'sw3', 'sb3', 'sw2', 'sb2')}
    del _L1_ffn_all
    return {'x': x, 'ctx_1024': ctx_1024, 'mask_BxS2_bf0': mask_BxS2_bf0, 'L0_attn_Wq': _L0_attn_in['Wq'], 'L0_attn_Wk': _L0_attn_in['Wk'], 'L0_attn_Wv': _L0_attn_in['Wv'], 'L0_attn_rel_bias_table': _L0_attn_in['rel_bias_table'], 'L0_attn_ln_gamma': _L0_attn_in['ln_gamma'], 'L0_attn_ln_beta': _L0_attn_in['ln_beta'], 'L0_xattn_Wq': _L0_xattn_in['Wq'], 'L0_xattn_Wk': _L0_xattn_in['Wk'], 'L0_xattn_Wv': _L0_xattn_in['Wv'], 'L0_xattn_Wo': _L0_xattn_in['Wo'], 'L0_xattn_bo': _L0_xattn_in['bo'], 'L0_ffn_w1': _L0_ffn_in['w1'], 'L0_ffn_conv_w': _L0_ffn_in['conv_w'], 'L0_ffn_conv_b': _L0_ffn_in['conv_b'], 'L0_ffn_w2': _L0_ffn_in['w2'], 'L1_attn_Wq': _L1_attn_in['Wq'], 'L1_attn_Wk': _L1_attn_in['Wk'], 'L1_attn_Wv': _L1_attn_in['Wv'], 'L1_attn_Wp': _L1_attn_in['Wp'], 'L1_attn_bp': _L1_attn_in['bp'], 'L1_xattn_Wq': _L1_xattn_in['Wq'], 'L1_xattn_bq': _L1_xattn_in['bq'], 'L1_xattn_Wk': _L1_xattn_in['Wk'], 'L1_xattn_bk': _L1_xattn_in['bk'], 'L1_xattn_Wv': _L1_xattn_in['Wv'], 'L1_xattn_bv': _L1_xattn_in['bv'], 'L1_xattn_Wo': _L1_xattn_in['Wo'], 'L1_xattn_bo': _L1_xattn_in['bo'], 'L1_ffn_gate_w': _L1_ffn_in['gate_w'], 'L1_ffn_gate_b': _L1_ffn_in['gate_b'], 'L1_ffn_w1': _L1_ffn_in['w1'], 'L1_ffn_b1': _L1_ffn_in['b1'], 'L1_ffn_w3': _L1_ffn_in['w3'], 'L1_ffn_b3': _L1_ffn_in['b3'], 'L1_ffn_w2': _L1_ffn_in['w2'], 'L1_ffn_b2': _L1_ffn_in['b2'], 'L1_ffn_sw1': _L1_ffn_in['sw1'], 'L1_ffn_sb1': _L1_ffn_in['sb1'], 'L1_ffn_sw3': _L1_ffn_in['sw3'], 'L1_ffn_sb3': _L1_ffn_in['sb3'], 'L1_ffn_sw2': _L1_ffn_in['sw2'], 'L1_ffn_sb2': _L1_ffn_in['sb2']}

def reference(x, ctx_1024, mask_BxS2_bf0, L0_attn_Wq, L0_attn_Wk, L0_attn_Wv, L0_attn_rel_bias_table, L0_attn_ln_gamma, L0_attn_ln_beta, L0_xattn_Wq, L0_xattn_Wk, L0_xattn_Wv, L0_xattn_Wo, L0_xattn_bo, L0_ffn_w1, L0_ffn_conv_w, L0_ffn_conv_b, L0_ffn_w2, L1_attn_Wq, L1_attn_Wk, L1_attn_Wv, L1_attn_Wp, L1_attn_bp, L1_xattn_Wq, L1_xattn_bq, L1_xattn_Wk, L1_xattn_bk, L1_xattn_Wv, L1_xattn_bv, L1_xattn_Wo, L1_xattn_bo, L1_ffn_gate_w, L1_ffn_gate_b, L1_ffn_w1, L1_ffn_b1, L1_ffn_w3, L1_ffn_b3, L1_ffn_w2, L1_ffn_b2, L1_ffn_sw1, L1_ffn_sb1, L1_ffn_sw3, L1_ffn_sb3, L1_ffn_sw2, L1_ffn_sb2):
    import jax
    import jax.numpy as jnp

    def _L0_attn_ref(x, Wq, Wk, Wv, rel_bias_table, ln_gamma, ln_beta):
        import jax, jax.numpy as jnp
        import numpy as np
        B, S, D, H = (2, 256, 128, 16)
        HD = D // H
        EPS = 1e-05
        bs, seq_len, d_model = x.shape
        scale = d_model ** (-0.5)
        q = jnp.einsum('bsd,ed->bse', x, Wq).reshape(bs, seq_len, H, HD).transpose(0, 2, 1, 3)
        k = jnp.einsum('bsd,ed->bse', x, Wk).reshape(bs, seq_len, H, HD).transpose(0, 2, 1, 3)
        v = jnp.einsum('bsd,ed->bse', x, Wv).reshape(bs, seq_len, H, HD).transpose(0, 2, 1, 3)
        attn = jax.nn.softmax(jnp.einsum('bhqd,bhkd->bhqk', q, k) * scale, axis=-1)
        idx = jnp.arange(seq_len)[:, None] - jnp.arange(seq_len)[None, :] + (seq_len - 1)
        rel_bias = rel_bias_table[idx]
        rel_bias = rel_bias.transpose(2, 0, 1)[None]
        attn = attn + rel_bias
        out = jnp.einsum('bhqk,bhkd->bhqd', attn, v)
        out = out.transpose(0, 2, 1, 3).reshape(bs, seq_len, d_model)
        mu = jnp.mean(out, axis=-1, keepdims=True)
        var = jnp.var(out, axis=-1, keepdims=True)
        out = (out - mu) * jax.lax.rsqrt(var + EPS)
        return out * ln_gamma + ln_beta

    def _L0_xattn_ref(q, k, v, Wq, Wk, Wv, Wo, bo, mask):
        import jax, jax.numpy as jnp
        import numpy as np
        DIM = 128
        HEADS = 16
        DIM_HEAD = 64
        INNER = HEADS * DIM_HEAD
        B, N = (2, 256)
        SCALE = DIM_HEAD ** (-0.5)
        b, n, _ = q.shape
        h, d = (HEADS, DIM_HEAD)

        def split_heads(x):
            return x.reshape(b, n, h, d).transpose(0, 2, 1, 3)
        qh = split_heads(q @ Wq)
        kh = split_heads(k @ Wk)
        vh = split_heads(v @ Wv)
        dots = jnp.einsum('bhid,bhjd->bhij', qh, kh) * SCALE
        mask_value = -jnp.finfo(dots.dtype).max
        dots = jnp.where(mask[:, None, None, :], mask_value, dots)
        causal = jnp.triu(jnp.ones((n, n), dtype=bool), k=1)
        dots = jnp.where(causal[None, None, :, :], mask_value, dots)
        attn = jax.nn.softmax(dots, axis=-1)
        out = jnp.einsum('bhij,bhjd->bhid', attn, vh)
        out = out.transpose(0, 2, 1, 3).reshape(b, n, h * d)
        return out @ Wo + bo

    def _L0_ffn_ref(x, w1, conv_w, conv_b, w2):
        import jax, jax.numpy as jnp
        import numpy as np
        B, S, D_MODEL, D_HIDDEN = (4, 256, 128, 512)

        def act_quant(x):
            scale = 127.0 / jnp.clip(jnp.max(jnp.abs(x), axis=-1, keepdims=True), 1e-05)
            return jnp.clip(jnp.round(x * scale), -128, 127) / scale

        def weight_quant(w):
            scale = 1.0 / jnp.clip(jnp.mean(jnp.abs(w)), 1e-05)
            return jnp.clip(jnp.round(w * scale), -1, 1) / scale

        def bit_linear(x, w):
            xq = x + jax.lax.stop_gradient(act_quant(x) - x)
            wq = w + jax.lax.stop_gradient(weight_quant(w) - w)
            return jnp.einsum('bsd,hd->bsh', xq, wq)

        def depthwise_conv1d(x_bcl, w, b):
            y = jax.lax.conv_general_dilated(x_bcl, w, window_strides=(1,), padding=[(1, 1)], dimension_numbers=('NCH', 'OIH', 'NCH'), feature_group_count=x_bcl.shape[1])
            return y + b[None, :, None]
        h = bit_linear(x, w1)
        h = depthwise_conv1d(h.transpose(0, 2, 1), conv_w, conv_b)
        h = h.transpose(0, 2, 1)
        h = jax.nn.silu(h)
        return bit_linear(h, w2)

    def _L1_attn_ref(x, Wq, Wk, Wv, Wp, bp):
        import jax, jax.numpy as jnp
        import numpy as np
        D_IN = 128
        D_OUT = 128
        H = 16
        G = 4
        LF = 2
        HEAD_OUT = D_OUT // H
        DQ = HEAD_OUT // LF
        B, T = (2, 256)

        def _alibi_bias(T, dtype):
            slopes = jnp.asarray(2.0 ** (-8.0 * np.arange(1, H + 1) / H), dtype=dtype)
            pos = jnp.arange(T)
            rel = (pos[None, :] - pos[:, None]).astype(dtype)
            return slopes[:, None, None] * rel[None, :, :]
        b, t, _ = x.shape
        q = x @ Wq
        k = jnp.tile(x @ Wk, (1, 1, G))
        v = jnp.tile(x @ Wv, (1, 1, G))
        q = q.reshape(b, t, H, DQ).transpose(0, 2, 1, 3)
        k = k.reshape(b, t, H, DQ).transpose(0, 2, 1, 3)
        v = v.reshape(b, t, H, HEAD_OUT).transpose(0, 2, 1, 3)
        scores = jnp.einsum('bhqd,bhkd->bhqk', q, k)
        causal = jnp.triu(jnp.ones((t, t), dtype=bool), k=1)
        scores = jnp.where(causal, -jnp.inf, scores)
        scores = (scores + _alibi_bias(t, scores.dtype)) / jnp.sqrt(jnp.asarray(DQ, scores.dtype))
        w = jax.nn.softmax(scores, axis=-1)
        ctx = jnp.einsum('bhqk,bhkd->bqhd', w, v).reshape(b, t, D_OUT)
        return ctx @ Wp + bp

    def _L1_xattn_ref(query, key, value, Wq, bq, Wk, bk, Wv, bv, Wo, bo):
        import math
        import jax, jax.numpy as jnp
        import numpy as np
        D_MODEL, N_HEADS, D_K = (128, 16, 64)
        B, S = (4, 512)
        b, s, _ = query.shape
        q = (query @ Wq.T + bq).reshape(b, s, N_HEADS, D_K)
        k = (key @ Wk.T + bk).reshape(b, s, N_HEADS, D_K)
        v = (value @ Wv.T + bv).reshape(b, s, N_HEADS, D_K)
        inv_sqrt_dk = 1.0 / math.sqrt(D_K)
        scores = jnp.einsum('bshd,bsgd->bshg', q, k) * inv_sqrt_dk
        attn = jax.nn.softmax(scores, axis=-1)
        out = jnp.einsum('bshg,bsgd->bshd', attn, v)
        out = jnp.transpose(out, (0, 2, 1, 3)).reshape(b, -1, N_HEADS * D_K)
        return out @ Wo.T + bo

    def _L1_ffn_ref(x, gate_w, gate_b, w1, b1, w3, b3, w2, b2, sw1, sb1, sw3, sb3, sw2, sb2):
        import jax, jax.numpy as jnp
        import numpy as np
        E = 8
        TOP_K = 2
        ROUTE_SCALE = 1.0
        ALPHA = 1.702
        LIMIT = 7.0
        D = 128
        F = 128
        B, S = (2, 128)

        def swiglu(h):
            g = jnp.minimum(h[..., ::2], LIMIT)
            l = jnp.clip(h[..., 1::2], -LIMIT, LIMIT)
            return g * jax.nn.sigmoid(ALPHA * g) * (l + 1.0)
        if __name__ == '__main__':
            out = reference(**setup_inputs())
            print(out.shape, out.dtype)
        inp_shape = x.shape
        xt = x.reshape(-1, D)
        logits = xt @ gate_w.T
        scores = jax.nn.softmax(logits.astype(jnp.float32), axis=-1)
        biased = scores + gate_b.astype(jnp.float32)
        idx = jax.lax.top_k(biased, TOP_K)[1]
        weights = (jnp.take_along_axis(scores, idx, axis=-1) * ROUTE_SCALE).astype(x.dtype)
        cw = jnp.sum(jax.nn.one_hot(idx, E, dtype=x.dtype) * weights[..., None], axis=1)
        h1 = jnp.einsum('td,efd->etf', xt, w1) + b1[:, None, :]
        h3 = jnp.einsum('td,efd->etf', xt, w3) + b3[:, None, :]
        a = swiglu(h1 * h3)
        y = jnp.einsum('etf,edf->etd', a, w2) + b2[:, None, :]
        routed = jnp.einsum('te,etd->td', cw, y)
        sh = swiglu((xt @ sw1.T + sb1) * (xt @ sw3.T + sb3))
        shared = sh @ sw2.T + sb2
        return (routed + shared).reshape(inp_shape)
    x = x + _L0_attn_ref(_layernorm(x, axis=-1), L0_attn_Wq, L0_attn_Wk, L0_attn_Wv, L0_attn_rel_bias_table, L0_attn_ln_gamma, L0_attn_ln_beta)
    x = x + _L0_xattn_ref(_layernorm(x, axis=-1), ctx_1024, ctx_1024, L0_xattn_Wq, L0_xattn_Wk, L0_xattn_Wv, L0_xattn_Wo, L0_xattn_bo, mask_BxS2_bf0)
    x = x + _L0_ffn_ref(_layernorm(x, axis=-1), L0_ffn_w1, L0_ffn_conv_w, L0_ffn_conv_b, L0_ffn_w2)
    x = x + _L1_attn_ref(_layernorm(x, axis=-1), L1_attn_Wq, L1_attn_Wk, L1_attn_Wv, L1_attn_Wp, L1_attn_bp)
    x = x + _L1_xattn_ref(_layernorm(x, axis=-1), ctx_1024, ctx_1024, L1_xattn_Wq, L1_xattn_bq, L1_xattn_Wk, L1_xattn_bk, L1_xattn_Wv, L1_xattn_bv, L1_xattn_Wo, L1_xattn_bo)
    x = x + _L1_ffn_ref(_layernorm(x, axis=-1), L1_ffn_gate_w, L1_ffn_gate_b, L1_ffn_w1, L1_ffn_b1, L1_ffn_w3, L1_ffn_b3, L1_ffn_w2, L1_ffn_b2, L1_ffn_sw1, L1_ffn_sb1, L1_ffn_sw3, L1_ffn_sb3, L1_ffn_sw2, L1_ffn_sb2)
    return x

_drawn_inputs = setup_inputs


def setup_inputs(seed=0):
    import zlib

    import numpy as np

    out = dict(_drawn_inputs(seed))
    spreads = {'L0_attn_ln_gamma': (1.0, 0.2),
     'L0_attn_ln_beta': (0.0, 0.1),
     'L1_attn_bp': (0.0, 0.1),
     'L1_xattn_bq': (0.0, 0.1),
     'L1_xattn_bk': (0.0, 0.1),
     'L1_xattn_bv': (0.0, 0.1),
     'L1_xattn_bo': (0.0, 0.1)}
    factors = {'L0_attn_Wq': 8.0,
     'L0_attn_Wk': 8.0,
     'L1_attn_Wq': 8.0,
     'L1_attn_Wk': 8.0,
     'L1_attn_Wv': 2.678,
     'L1_ffn_b1': 23.318,
     'L1_ffn_b3': 22.735,
     'L1_ffn_b2': 29.102,
     'L1_ffn_sb1': 8.0,
     'L1_ffn_sb3': 8.0,
     'L1_ffn_sb2': 8.0}
    for name, (base, spread) in spreads.items():
        noise = np.random.default_rng([zlib.crc32(name.encode()), seed]).standard_normal(out[name].shape)
        drawn = base * np.exp(spread * noise) if base else spread * noise
        out[name] = jnp.asarray(drawn.astype(out[name].dtype))
    for name, factor in factors.items():
        out[name] = (out[name] * factor).astype(out[name].dtype)
    return out
```

```python
from contextlib import ExitStack

import concourse.bass as bass
from concourse import mybir
from concourse.alu_op_type import AluOpType as ALU

ACT = mybir.ActivationFunctionType
AX = mybir.AxisListType.X
F32 = mybir.dt.float32
BF16 = mybir.dt.bfloat16

B, S, D = 4, 256, 128
P = 128
NB = 2
PASSES = B // NB
SB = S // P
TT = NB * SB
TOK = NB * S
H = 16
U = NB * H
HID = 512
HC = HID // P
E, F = 8, 128
EPS = 1e-5
BIG = 1e30
MAGIC = 1.5 * 2.0 ** 23
Q4 = 4
TW = S + P


class Stage:

    def __init__(self, nc, name):
        self.nc, self.name, self.ctx, self.sems = nc, name, ExitStack(), []
        self.chained = 0

    def sb(self, name, shape, dt=F32):
        return self.ctx.enter_context(self.nc.sbuf_tensor(f"{self.name}_{name}", shape, dt))

    def psum_banks(self):
        return [self.ctx.enter_context(self.nc.psum_tensor(f"{self.name}_bank{i}", [P, 512], F32)) for i in range(8)]

    def sem(self, name):
        s = self.ctx.enter_context(self.nc.semaphore(f"{self.name}_{name}"))
        self.sems.append(s)
        return s

    def close(self):
        nums = sorted(s.num for s in self.sems)
        while nums:
            n = 1
            while n < len(nums) and nums[n] == nums[0] + n:
                n += 1
            self.nc.vector.sem_clear(range(nums[0], nums[0] + n))
            nums = nums[n:]
        self.nc.all_engine_barrier()
        self.ctx.close()


class Chain:

    def __init__(self, eng, sem):
        self.eng, self.sem, self.n = eng, sem, 0

    def __call__(self, ins):
        self.n += 1
        ins.then_inc(self.sem, 1)
        self.eng.wait_ge(self.sem, self.n)


def bcast(ap, n, width):
    return ap.unsqueeze(2).broadcast_to([ap.shape[0], n, width])



class Norm:

    def __init__(self, st, w, tag=""):
        self.w = w
        self.stats = st.sb(f"bn{tag}", [P, TT, 6])
        self.mv = st.sb(f"mv{tag}", [P, TT, 2])
        self.ve = st.sb(f"ve{tag}", [P, TT])
        self.rstd = st.sb(f"rstd{tag}", [P, TT])
        self.s_var = st.sem(f"var_ready{tag}")
        self.s_rstd = st.sem(f"rstd_ready{tag}")

    def vector_stats(self, dve, link, src):
        for t in range(TT):
            ins = dve.bn_stats(self.stats[:, t, :], src[:, t, :])
            if t == TT - 1:
                link(ins)
            else:
                ins.then_inc(link.sem, 1)
                link.n += 1
        for t in range(TT):
            ins = dve.bn_aggr(self.mv[:, t, :], self.stats[:, t, :])
            if t == TT - 1:
                link(ins)
            else:
                ins.then_inc(link.sem, 1)
                link.n += 1
        dve.tensor_scalar(self.ve[:], self.mv[:, :, 1], EPS, None, ALU.add).then_inc(self.s_var, 1)

    def gpsimd_rstd(self, pool):
        pool.wait_ge(self.s_var, 1)
        pool.tensor_tensor(self.rstd[:], self.ve[:], self.w["minus_half"][:, 0:TT], ALU.pow).then_inc(self.s_rstd, 1)

    def vector_apply(self, dve, out, src, s_done):
        dve.wait_ge(self.s_rstd, 1)
        for t in range(TT):
            dve.tensor_scalar(out[:, t, :], src[:, t, :], self.mv[:, t, 0:1], self.rstd[:, t:t + 1],
                              ALU.subtract, ALU.mult).then_inc(s_done, 1)


def tensor_transpose_tiles(pe, w, bank, src, s_src, s_done):
    for t in range(TT):
        pe.wait_ge(s_src, t + 1)
        ins = pe.transpose(bank[:, t * P:(t + 1) * P], src[:, t, :], w["ident"][:])
    ins.then_inc(s_done, 1)



class Attention:

    def __init__(self, st, w, *, causal, lse, scale, heads_per_out, q, k, values, out_rows):
        self.st, self.w, self.causal, self.lse, self.scale = st, w, causal, lse, scale
        self.HG, self.q, self.k, self.values, self.rows = heads_per_out, q, k, values, out_rows
        self.W = 3 * P if causal else 2 * S
        self.nmax = st.sb("nmax", [P, NB, SB, H])
        self.zsum = st.sb("zsum", [P, NB, SB, H]) if lse else None
        self.lnz = st.sb("lnz", [P, SB, H]) if lse else None
        self.shift = st.sb("shift", [P, SB, H])
        self.rest = st.sb("rest", [P, SB, H])
        self.parts = st.sb("parts", [P, NB, SB, P], BF16)
        self.shiftT = st.sb("shiftT", [P, NB, S], BF16)
        self.expT = st.sb("expT", [P, 3, self.W])
        self.s_s = st.sem("max_scores_ready")
        self.s_mx = st.sem("max_done")
        self.s_lse = st.sem("sum_done")
        self.s_ln = st.sem("log_ready")
        self.s_parts = st.sem("shift_parts_ready")
        self.s_tp = st.sem("shift_transposed")
        self.s_shT = st.sem("shiftT_ready")
        self.s_e = st.sem("exp_scores_ready")
        self.s_p = st.sem("exp_ready")
        self.s_pv = st.sem("exp_used")
        self.s_og = st.sem("out_evicted")
        self.s_zero = st.sem("parts_zeroed")

    def tensor_S(self, pe, u, bank):
        b, h = divmod(u, H)
        if u >= 2:
            pe.wait_ge(self.s_lse if self.lse else self.s_mx, u - 1)
        if self.causal:
            pe.matmul(bank[:, 0:P], self.q(b, h, 0, P), self.k(b, h, 0, P), start=True, stop=False, skip_group_check=True)
            pe.matmul(bank[:, P:3 * P], self.q(b, h, P, P), self.k(b, h, 0, S), start=False, stop=False, skip_group_check=True)
            for c in (0, 2 * P):
                ins = pe.matmul(bank[:, c:c + P], self.w["ident_bf"][:], self.w["mask_q"][:], start=False, stop=True, skip_group_check=True)
        else:
            for c in range(SB):
                ins = pe.matmul(bank[:, c * S:(c + 1) * S], self.q(b, h, c * P, P), self.k(b, h, 0, S),
                                start=(c == 0), stop=True, skip_group_check=True)
        ins.then_inc(self.s_s, 1)

    def tensor_shift(self, pe, b, bank):
        pe.wait_ge(self.s_parts, b + 1)
        if b:
            pe.wait_ge(self.s_shT, b)
        view = bank[:, 0:P].bitcast(BF16)
        for c in range(SB):
            ins = pe.transpose(view[:, c * P:(c + 1) * P], self.parts[:, b, c, :], self.w["ident_bf"][:])
        ins.then_inc(self.s_tp, 1)

    def tensor_E(self, pe, u, bank):
        b, h = divmod(u, H)
        if h == 0:
            pe.wait_ge(self.s_shT, b + 1)
        if u >= 2:
            pe.wait_ge(self.s_p, u - 1)
        sel = self.w["sel"][:, h, :]
        sh = self.shiftT[:, b, :]
        second = P if self.causal else 0
        pe.matmul(bank[:, 0:S], sel, sh, start=True, stop=False, skip_group_check=True)
        pe.matmul(bank[:, S:self.W], sel, sh[:, second:S], start=False, stop=False, skip_group_check=True)
        pe.matmul(bank[:, 0:S], self.k(b, h, 0, P), self.q(b, h, 0, S), start=False, stop=not self.causal, skip_group_check=True)
        ins = pe.matmul(bank[:, S:self.W], self.k(b, h, P, P), self.q(b, h, second, S - second), start=False, stop=not self.causal, skip_group_check=True)
        if self.causal:
            for c in (0, S):
                ins = pe.matmul(bank[:, c:c + P], self.w["ident_bf"][:], self.w["mask_k"][:], start=False, stop=True, skip_group_check=True)
        ins.then_inc(self.s_e, 1)

    def tensor_PV(self, pe, u, bank, extra=None):
        b, h = divmod(u, H)
        g, j = divmod(u, self.HG)
        pe.wait_ge(self.s_p, u + 1)
        if j == 0 and g >= 2:
            pe.wait_ge(self.s_og, g - 1)
        r = j * self.rows
        second = P if self.causal else 0
        e = self.expT[:, u % 3, :]
        pe.matmul(bank[r:r + self.rows, 0:S], self.values(b, h, 0), e[:, 0:S], start=True, stop=False, skip_group_check=True)
        ins = pe.matmul(bank[r:r + self.rows, second:S], self.values(b, h, 1), e[:, S:self.W], start=False, stop=extra is None, skip_group_check=True)
        if extra is not None:
            for c in range(SB):
                lhsT, rhs = extra(b, h, c)
                ins = pe.matmul(bank[r:r + self.rows, 0:S], lhsT, rhs, start=False, stop=(c == 1), skip_group_check=True)
        ins.then_inc(self.s_pv, 1)

    def vector_max(self, dve, u, bank):
        b, h = divmod(u, H)
        dve.wait_ge(self.s_s, u + 1)
        if self.causal:
            dve.tensor_reduce(self.nmax[:, b, 0, h:h + 1], bank[:, 0:P], AX, ALU.max, negate=True)
            dve.tensor_reduce(self.nmax[:, b, 1, h:h + 1], bank[:, P:3 * P], AX, ALU.max, negate=True).then_inc(self.s_mx, 1)
        else:
            dve.tensor_reduce(self.nmax[:, b, :, h], bank[:, :].rearrange("p (c k) -> p c k", c=SB), AX, ALU.max,
                              negate=True).then_inc(self.s_mx, 1)

    def vector_parts(self, dve, link, b):
        dve.wait_ge(self.s_mx, H * (b + 1))
        src = self.nmax[:, b, :, :]
        if self.lse:
            dve.wait_ge(self.s_ln, b + 1)
            link(dve.tensor_tensor(self.shift[:], src, self.lnz[:], ALU.subtract))
            src = self.shift[:]
        if b == 0:
            dve.wait_ge(self.s_zero, 1)
        hi, mid, lo = (self.parts[:, b, :, i * H:(i + 1) * H] for i in range(3))
        link(dve.tensor_copy(hi, src))
        link(dve.tensor_tensor(self.rest[:], src, hi, ALU.subtract))
        link(dve.tensor_copy(mid, self.rest[:]))
        dve.tensor_tensor(lo, self.rest[:], mid, ALU.subtract).then_inc(self.s_parts, 1)

    def vector_shiftT(self, dve, b, bank):
        dve.wait_ge(self.s_tp, b + 1)
        dve.tensor_copy(self.shiftT[:, b, :], bank[:, 0:P].bitcast(BF16)).then_inc(self.s_shT, 1)

    def scalar_sum(self, act, u, bank):
        b, h = divmod(u, H)
        act.wait_ge(self.s_mx, u + 1)
        act.activation(bank[:, 0:P], bank[:, 0:P], ACT.Exp, bias=self.nmax[:, b, 0, h:h + 1], scale=self.scale,
                       accum_out=self.zsum[:, b, 0, h:h + 1])
        act.activation(bank[:, P:3 * P], bank[:, P:3 * P], ACT.Exp, bias=self.nmax[:, b, 1, h:h + 1], scale=self.scale,
                       accum_out=self.zsum[:, b, 1, h:h + 1]).then_inc(self.s_lse, 1)

    def scalar_log(self, act, b):
        act.wait_ge(self.s_lse, H * (b + 1))
        if b:
            act.wait_ge(self.s_parts, b)
        act.activation(self.lnz[:], self.zsum[:, b, :, :], ACT.Ln).then_inc(self.s_ln, 1)

    def scalar_exp(self, act, u, bank):
        act.wait_ge(self.s_e, u + 1)
        if u >= 3:
            act.wait_ge(self.s_pv, u - 2)
        act.activation(self.expT[:, u % 3, :], bank[:, 0:self.W], ACT.Exp, scale=self.scale).then_inc(self.s_p, 1)


def split_columns(part_of):
    runs = []
    for i, x in enumerate(part_of):
        if runs and runs[-1][0] == x and runs[-1][1] + runs[-1][2] == i:
            runs[-1][2] += 1
        else:
            runs.append([x, i, 1])
    return runs


Q_PARTS = (0, 0, 0, 1, 1, 2)
K_PARTS = (0, 1, 2, 0, 1, 0)


def rel_attention(nc, w, x, ctx, x_dram, ctx_dram, it):
    st = Stage(nc, "l0a")
    HD = D // H
    SW = 64
    xn = st.sb("xn", [P, TT, D])
    xT = st.sb("xT", [P, TOK])
    sp_ = st.sb("split", [P, 2, 3, 2 * D], BF16)
    sr = st.sb("rest_qk", [P, 2, 2 * D])
    stack = st.sb("stack", [P, 2, 2, H, SW], BF16)
    qkT = st.sb("qkT", [P, H // 2, 2, TOK], BF16)
    vals = st.sb("vals", [P, TT, H, 64])
    xb = st.sb("x_beta", [P, TT, D])
    y = st.sb("y", [P, TT, D])
    osb = st.sb("o", [P, 2, S])
    rz = st.sb("rz", [P, 2 * Q4])
    tmp = st.sb("tmp", [P, 2 * Q4, HD])
    norm, norm2 = Norm(st, w), Norm(st, w, "2")
    s_chain = st.sem("dve_chain")
    s_x, s_ctx = st.sem("x_loaded"), st.sem("ctx_loaded")
    s_xn = st.sem("xn_ready")
    s_xTp = st.sem("x_transposed")
    s_xT = st.sem("xT_ready")
    s_qkv = st.sem("qkv_ready")
    s_split = st.sem("parts_ready")
    s_v = st.sem("values_ready")
    s_stq = st.sem("q_stack_ready")
    s_stk = st.sem("k_stack_ready")
    s_init = st.sem("buffers_set")
    s_stT = st.sem("stack_transposed")
    s_qkT = st.sem("qkT_ready")
    s_ob = st.sem("o_transposed")
    s_fin = st.sem("o_finished")
    s_y = st.sem("y_normalized")
    s_xb = st.sem("x_beta_ready")
    bank = st.psum_banks()
    SBK, EBK, OBK, G0, G1 = bank[0:2], bank[2:4], bank[4:6], bank[6], bank[7]

    def at(part, b, h, t0, n):
        r = SW * (h % 2)
        return qkT[r:r + SW, h // 2, part, b * S + t0:b * S + t0 + n]

    a = Attention(st, w, causal=False, lse=False, scale=float(D) ** -0.5, heads_per_out=Q4,
                  q=lambda b, h, t0, n: at(0, b, h, t0, n), k=lambda b, h, t0, n: at(1, b, h, t0, n),
                  values=lambda b, h, c: vals[:, b * SB + c, h, 0:32], out_rows=32)

    def bias_term(b, h, c):
        return vals[:, b * SB + c, h, 32:64], w["toeplitz"][:, h, (1 - c) * P:(1 - c) * P + S]

    GROUPS = U // Q4
    def copy_stack(dve, t):
        for i in range(4):
            n = 4 * t + i
            dve.wait_ge(s_stT, n + 1)
            dve.tensor_copy(qkT[:, 2 * i:2 * i + 2, :, t * P:(t + 1) * P],
                            bank[6 + n % 2][:, 0:256].bitcast(BF16).rearrange("p (a q k) -> p a q k", a=2, q=2)
                            ).then_inc(s_qkT, 1)

    with nc.Block() as block:

        @block.sync
        def _(sp):
            sp.dma_start(x[:], x_dram[bass.ts(it, NB)].rearrange("b (c p) d -> p (b c) d", p=P)).then_inc(s_x, 16)
            sp.dma_start(ctx[:], ctx_dram[bass.ts(it, NB)].rearrange("b (c p) d -> p (b c) d", p=P)).then_inc(s_ctx, 16)
            sp.wait_ge(s_ctx, 16)

        @block.gpsimd
        def _(pool):
            pool.wait_ge(s_x, 16)
            w.loaded(pool, "l0a")
            pool.memset(stack[:, :, :, :, 6 * HD:SW], 0.0).then_inc(s_init, 1)
            pool.memset(a.parts[:], 0.0).then_inc(a.s_zero, 1)
            norm.gpsimd_rstd(pool)
            pool.wait_ge(s_init, 3)
            pool.tensor_tensor(xb[:], x[:], w["beta"][:].unsqueeze(1).broadcast_to([P, TT, D]), ALU.add).then_inc(s_xb, 1)
            for t in range(TT):
                pool.wait_ge(s_split, t + 1)
                if t >= 2:
                    pool.wait_ge(s_stT, 4 * (t - 1))
                for part, i, n in split_columns(Q_PARTS):
                    out = stack[:, t % 2, 0, :, i * HD:(i + n) * HD].rearrange("p h (n d) -> p h n d", n=n)
                    src = sp_[:, t % 2, part, 0:D].rearrange("p (h d) -> p h d", h=H).unsqueeze(2).broadcast_to([P, H, n, HD])
                    ins = pool.tensor_copy(out, src)
                ins.then_inc(s_stq, 1)
            norm2.gpsimd_rstd(pool)

        @block.scalar
        def _(act):
            act.wait_ge(s_xTp, 1)
            act.activation(xT[:], G0[:, :], ACT.Copy).then_inc(s_xT, 1)
            act.wait_ge(s_init, 3)
            for t in range(TT):
                act.wait_ge(s_split, t + 1)
                v = EBK[t % 2][:, 2 * D:3 * D].rearrange("p (h d) -> p h d", h=H)
                act.activation(vals[:, t, :, 0:HD], v, ACT.Copy)
                act.activation(vals[:, t, :, 48:48 + HD], v, ACT.Copy).then_inc(s_v, 1)
                if t >= 2:
                    act.wait_ge(s_stT, 4 * (t - 1))
                for part, i, n in split_columns(K_PARTS):
                    ins = act.activation(stack[:, t % 2, 1, :, i * HD:(i + n) * HD],
                                         sp_[:, t % 2, part, D:2 * D].rearrange("p (h d) -> p h d", h=H), ACT.Copy)
                ins.then_inc(s_stk, 1)
            for n in range(U + 2):
                if n < U:
                    a.scalar_exp(act, n, EBK[n % 2])
                if n % Q4 == 0 and n:
                    g = n // Q4 - 1
                    act.wait_ge(a.s_pv, n)
                    if g >= 2:
                        act.wait_ge(s_ob, g - 1)
                    act.activation(osb[:, g % 2, :], OBK[g % 2][:, 0:S], ACT.Copy).then_inc(a.s_og, 1)

        @block.vector
        def _(dve):
            link = Chain(dve, s_chain)
            dve.wait_ge(s_x, 16)
            norm.vector_stats(dve, link, x)
            w.loaded(dve, "l0a")
            dve.memset(vals[:], 0.0).then_inc(s_init, 1)
            dve.wait_ge(s_init, 2)
            dve.memset(vals[:, :, :, HD:HD + 1], 1.0).then_inc(s_init, 1)
            norm.vector_apply(dve, xn, x, s_xn)
            for t in range(TT):
                dve.wait_ge(s_qkv, t + 1)
                if t >= 2:
                    dve.wait_ge(s_stq, t - 1)
                    dve.wait_ge(s_stk, t - 1)
                qk = EBK[t % 2][:, 0:2 * D]
                hi, mid, lo = (sp_[:, t % 2, i, :] for i in range(3))
                link(dve.tensor_copy(hi, qk))
                link(dve.tensor_tensor(sr[:, t % 2, :], qk, hi, ALU.subtract))
                link(dve.tensor_copy(mid, sr[:, t % 2, :]))
                dve.tensor_tensor(lo, sr[:, t % 2, :], mid, ALU.subtract).then_inc(s_split, 1)
                if t:
                    copy_stack(dve, t - 1)
            copy_stack(dve, TT - 1)
            for u in range(H):
                a.vector_max(dve, u, SBK[u % 2])
            a.vector_parts(dve, link, 0)
            for n in range(U + 3):
                b, h = divmod(n, H)
                if h == 0 and b < NB:
                    a.vector_shiftT(dve, b, G0)
                if n + H < U:
                    a.vector_max(dve, n + H, SBK[n % 2])
                if h == H - 1 and b + 1 < NB:
                    a.vector_parts(dve, link, b + 1)
                if n >= Q4 + 2 and (n - 2) % Q4 == 0:
                    g = (n - 2) // Q4 - 1
                    b2, hg = divmod(g, H // Q4)
                    dve.wait_ge(s_ob, g + 1)
                    if g:
                        dve.wait_ge(s_fin, g)
                    o = G1[:, 0:SB * P].rearrange("p (c r) -> p c r", r=32)
                    link(dve.reciprocal(rz[:], o[:, :, HD]))
                    link(dve.tensor_tensor(tmp[:], o[:, :, 0:HD], bcast(rz[:], 2 * Q4, HD), ALU.mult))
                    dst = y[:, b2 * SB:(b2 + 1) * SB, hg * 32:(hg + 1) * 32].rearrange("p c (j d) -> p c j d", d=HD)
                    for c in range(SB):
                        ins = dve.tensor_tensor(dst[:, c], o[:, c * Q4:(c + 1) * Q4, 16:16 + HD],
                                                tmp[:, c * Q4:(c + 1) * Q4, :], ALU.add)
                    ins.then_inc(s_fin, 1)
            dve.wait_ge(s_fin, GROUPS)
            norm2.vector_stats(dve, link, y)
            norm2.vector_apply(dve, xn, y, s_y)
            dve.wait_ge(s_y, TT)
            dve.wait_ge(s_xb, 1)
            link(dve.tensor_tensor(y[:], xn[:], w["gamma"][:].unsqueeze(1).broadcast_to([P, TT, D]), ALU.mult))
            link(dve.tensor_tensor(x[:], y[:], xb[:], ALU.add))

        @block.tensor
        def _(pe):
            tensor_transpose_tiles(pe, w, G0, xn, s_xn, s_xTp)
            w.loaded(pe, "l0a")
            pe.wait_ge(s_xT, 1)
            for t in range(TT + 1):
                if t < TT:
                    if t >= 2:
                        pe.wait_ge(s_split, t - 1)
                        pe.wait_ge(s_v, t - 1)
                    pe.matmul(EBK[t % 2][:, 0:3 * D], xT[:, t * P:(t + 1) * P], w["l0a_qkv"][:], start=True, stop=True).then_inc(s_qkv, 1)
                if t:
                    pe.wait_ge(s_stq, t)
                    pe.wait_ge(s_stk, t)
                    for i in range(4):
                        n = 4 * (t - 1) + i
                        if n >= 2:
                            pe.wait_ge(s_qkT, n - 1)
                        out = bank[6 + n % 2][:, 0:256].bitcast(BF16)
                        for hp in (2 * i, 2 * i + 1):
                            for part in range(2):
                                c = ((hp % 2) * 2 + part) * P
                                ins = pe.transpose(out[:, c:c + P], stack[:, (t - 1) % 2, part, 2 * hp:2 * hp + 2, :], w["ident_bf"][:])
                        ins.then_inc(s_stT, 1)
            pe.wait_ge(s_qkT, 4 * TT)
            for u in range(H):
                a.tensor_S(pe, u, SBK[u % 2])
            for n in range(U + 3):
                b, h = divmod(n, H)
                if h == 0 and b < NB:
                    a.tensor_shift(pe, b, G0)
                if n < U:
                    a.tensor_E(pe, n, EBK[n % 2])
                if n + H < U:
                    a.tensor_S(pe, n + H, SBK[n % 2])
                if 1 <= n <= U:
                    a.tensor_PV(pe, n - 1, OBK[(n - 1) // Q4 % 2], extra=bias_term)
                if n >= Q4 + 2 and (n - 2) % Q4 == 0:
                    g = (n - 2) // Q4 - 1
                    pe.wait_ge(a.s_og, g + 1)
                    if g:
                        pe.wait_ge(s_fin, g)
                    for c in range(SB):
                        ins = pe.transpose(G1[:, c * P:(c + 1) * P], osb[:, g % 2, c * P:(c + 1) * P], w["ident"][:])
                    ins.then_inc(s_ob, 1)
    st.close()

def cross_attention(nc, w, x, ctx):
    st = Stage(nc, "l0x")
    HD = 64
    HP = H // 2
    xn = st.sb("xn", [P, TT, D])
    xT = st.sb("xT", [P, 2, TOK])
    qT = st.sb("qT", [P, HP, TOK])
    kT = st.sb("kT", [P, HP, TOK])
    vals = st.sb("vals", [P, TT, H * HD])
    oT = st.sb("oT", [P, HP, TOK])
    xb = st.sb("x_bias", [P, TT, D])
    norm = Norm(st, w)
    s_chain = st.sem("dve_chain")
    s_xn = st.sem("xn_ready")
    s_tp = st.sem("transposed")
    s_xT = st.sem("xT_ready")
    s_xb = st.sem("x_bias_ready")
    s_pr = st.sem("projected")
    s_pa = st.sem("projection_by_scalar")
    s_pv = st.sem("projection_by_vector")
    s_wo = st.sem("product_ready")
    s_x = st.sem("x_updated")
    bank = st.psum_banks()
    SBK, EBK, OBK, G0, G1 = bank[0:2], bank[2:4], bank[4:6], bank[6], bank[7]

    def at(buf, b, h, t0, n):
        r = HD * (h % 2)
        return buf[r:r + HD, h // 2, b * S + t0:b * S + t0 + n]

    a = Attention(st, w, causal=True, lse=True, scale=1.0, heads_per_out=2,
                  q=lambda b, h, t0, n: at(qT, b, h, t0, n), k=lambda b, h, t0, n: at(kT, b, h, t0, n),
                  values=lambda b, h, c: vals[:, b * SB + c, h * HD:(h + 1) * HD], out_rows=HD)

    jobs = [("k", c, 0) for c in range(HP)] + [("v", t, i) for t in range(TT) for i in range(2)] + [("q", c, 0) for c in range(HP)]
    GROUPS = U // 2

    def destination(job):
        kind, c, i = job
        if kind == "k":
            return kT[:, c, :], 1.0
        if kind == "q":
            return qT[:, c, :], float(HD) ** -0.5
        return vals[:, c, i * 512:(i + 1) * 512], 1.0

    with nc.Block() as block:

        @block.gpsimd
        def _(pool):
            w.loaded(pool, "l0x")
            pool.tensor_tensor(xb[:], x[:], w["l0x_bo"][:].unsqueeze(1).broadcast_to([P, TT, D]), ALU.add).then_inc(s_xb, 1)
            pool.memset(a.parts[:], 0.0).then_inc(a.s_zero, 1)
            norm.gpsimd_rstd(pool)

        @block.scalar
        def _(act):
            act.wait_ge(s_tp, 1)
            act.activation(xT[:, 1, :], G0[:, :], ACT.Copy).then_inc(s_xT, 1)
            for n in range(0, len(jobs), 2):
                if jobs[n] == ("q", 0, 0):
                    act.wait_ge(s_tp, 2)
                    act.activation(xT[:, 0, :], G1[:, :], ACT.Copy).then_inc(s_xT, 1)
                out, scale = destination(jobs[n])
                act.wait_ge(s_pr, n + 1)
                act.activation(out, bank[n % 4][:, :], ACT.Copy, scale=scale).then_inc(s_pa, 1)
            for u in range(H):
                a.scalar_sum(act, u, SBK[u % 2])
            a.scalar_log(act, 0)
            for n in range(U + 1):
                b, h = divmod(n, H)
                if n < U:
                    a.scalar_exp(act, n, EBK[n % 2])
                if n + H < U:
                    a.scalar_sum(act, n + H, SBK[n % 2])
                if n % 2 == 0 and n:
                    g = n // 2 - 1
                    b2, c = divmod(g, HP)
                    act.wait_ge(a.s_pv, n)
                    act.activation(oT[:, c, b2 * S:(b2 + 1) * S], OBK[g % 2][:, 0:S], ACT.Copy).then_inc(a.s_og, 1)
                if h == H - 1 and b + 1 < NB:
                    a.scalar_log(act, b + 1)

        @block.vector
        def _(dve):
            link = Chain(dve, s_chain)
            norm.vector_stats(dve, link, x)
            norm.vector_apply(dve, xn, x, s_xn)
            for n in range(1, len(jobs), 2):
                out, scale = destination(jobs[n])
                dve.wait_ge(s_pr, n + 1)
                if scale == 1.0:
                    ins = dve.tensor_copy(out, bank[n % 4][:, :])
                else:
                    ins = dve.tensor_scalar(out, bank[n % 4][:, :], scale, None, ALU.mult)
                ins.then_inc(s_pv, 1)
            for u in range(H):
                a.vector_max(dve, u, SBK[u % 2])
            a.vector_parts(dve, link, 0)
            for n in range(U + 1):
                b, h = divmod(n, H)
                if h == 0 and b < NB:
                    a.vector_shiftT(dve, b, G0)
                if n + H < U:
                    a.vector_max(dve, n + H, SBK[n % 2])
                if h == H - 1 and b + 1 < NB:
                    a.vector_parts(dve, link, b + 1)
            dve.wait_ge(s_xb, 1)
            for t in range(TT):
                dve.wait_ge(s_wo, t + 1)
                dve.tensor_tensor(x[:, t, :], bank[t % 4][:, 0:D], xb[:, t, :], ALU.add).then_inc(s_x, 1)

        @block.tensor
        def _(pe):
            w.loaded(pe, "l0x")
            for t in range(TT):
                ins = pe.transpose(G0[:, t * P:(t + 1) * P], ctx[:, t, :], w["ident"][:])
            ins.then_inc(s_tp, 1)
            pe.wait_ge(s_xT, 1)
            for n, (kind, c, i) in enumerate(jobs):
                if (kind, c) == ("q", 0):
                    tensor_transpose_tiles(pe, w, G1, xn, s_xn, s_tp)
                    pe.wait_ge(s_xT, 2)
                if n >= 4:
                    pe.wait_ge(s_pv if n % 2 else s_pa, n // 2 - 1)
                out = bank[n % 4][:, :]
                if kind == "v":
                    ins = pe.matmul(out, xT[:, 1, c * P:(c + 1) * P], w["l0x_v"][:, i * 512:(i + 1) * 512], start=True, stop=True)
                else:
                    ins = pe.matmul(out, w[f"l0x_{kind}"][:, c * P:(c + 1) * P], xT[:, int(kind == "k"), :], start=True, stop=True)
                ins.then_inc(s_pr, 1)
            pe.wait_ge(s_pa, len(jobs) // 2)
            pe.wait_ge(s_pv, len(jobs) // 2)
            for u in range(H):
                a.tensor_S(pe, u, SBK[u % 2])
            for n in range(U + 1):
                b, h = divmod(n, H)
                if h == 0 and b < NB:
                    a.tensor_shift(pe, b, G0)
                if n < U:
                    a.tensor_E(pe, n, EBK[n % 2])
                if n + H < U:
                    a.tensor_S(pe, n + H, SBK[n % 2])
                if 1 <= n <= U:
                    a.tensor_PV(pe, n - 1, OBK[(n - 1) // 2 % 2])
            pe.wait_ge(a.s_og, GROUPS)
            for t in range(TT):
                for c in range(HP):
                    ins = pe.matmul(bank[t % 4][:, 0:D], oT[:, c, t * P:(t + 1) * P], w["l0x_o"][:, c, :],
                                    start=(c == 0), stop=(c == HP - 1))
                ins.then_inc(s_wo, 1)
    st.close()


def weight_levels(nc, w, dram):
    st = Stage(nc, "wq")
    raw = st.sb("raw", [P, 2, HID])
    psum_bank = st.psum_banks()
    part = st.sb("part", [P, 2])
    scale = st.sb("scale", [P, 2])
    r = st.sb("r", [P, 2, HID])
    s_raw, s_part, s_sum, s_chain, s_done = (st.sem(n) for n in ("raw_loaded", "part_ready", "sum_ready", "dve_chain", "done"))
    with nc.Block() as block:

        @block.sync
        def _(sp):
            sp.dma_start(raw[:, 0, :], dram["ffn_w1T"]).then_inc(s_raw, 16)
            sp.dma_start(raw[:, 1, :], dram["ffn_w2T"]).then_inc(s_raw, 16)
            sp.wait_ge(s_raw, 32)

        @block.vector
        def _(dve):
            link = Chain(dve, s_chain)
            dve.wait_ge(s_raw, 32)
            dve.tensor_reduce(part[:], raw[:], AX, ALU.add, apply_absolute_value=True).then_inc(s_part, 1)
            dve.wait_ge(s_sum, 1)
            mean = w["ffn_wmean"]
            link(dve.tensor_scalar(mean[:], psum_bank[0][:, 0:2], 1.0 / (HID * D), EPS, ALU.mult, ALU.max))
            link(dve.reciprocal(scale[:], mean[:]))
            for i in range(2):
                link(dve.tensor_scalar(r[:, i, :], raw[:, i, :], scale[:, i:i + 1], MAGIC, ALU.mult, ALU.add))
            link(dve.tensor_scalar(r[:], r[:], MAGIC, 1.0, ALU.subtract, ALU.min))
            dve.tensor_scalar(w["ffn_q"][:], r[:], -1.0, None, ALU.max).then_inc(s_done, 1)

        @block.tensor
        def _(pe):
            w.loaded(pe, "const")
            pe.wait_ge(s_part, 1)
            pe.matmul(psum_bank[0][:, 0:2], w["ones"][:], part[:], start=True, stop=True).then_inc(s_sum, 1)
    st.close()


def quantized_ffn(nc, w, x):
    st = Stage(nc, "ffn")
    xn = st.sb("xn", [P, TT, D])
    r = st.sb("r", [P, TT, HID])
    xq = st.sb("xq", [P, TT, D], BF16)
    xqT = st.sb("xqT", [P, TOK], BF16)
    amax = st.sb("amax", [P, 2, TT])
    inv = st.sb("inv", [P, 2, TT])
    scale = st.sb("scale", [P, 2, TT])
    dg = st.sb("diag", [P, TT, P])
    rowinv = st.sb("rowinv", [P, TOK])
    hp = st.sb("h", [P, HC, NB, S + 2])
    y = st.sb("conv", [P, HC, TOK])
    q2 = st.sb("q2", [P, TT, HID], BF16)
    q2T = st.sb("q2T", [P, HC, TOK], BF16)
    norm = Norm(st, w)
    names = ("dve_chain", "xn_ready", "diag_ready", "rowsum_ready", "rowinv_ready", "xq_ready", "xq_transposed", "xqT_ready",
             "hidden_ready", "hidden_scaled", "conv_ready", "act_ready", "act_transposed", "q2_ready", "q2_transposed", "q2T_ready",
             "product_ready", "x_updated", "inv_ready", "pads_zero", "act_read")
    (s_chain, s_xn, s_dg, s_rs, s_ri, s_xq, s_xqt, s_xqT, s_h, s_hs, s_cv, s_ac, s_act, s_q2, s_q2t, s_q2T,
     s_pr, s_x, s_inv, s_pad, s_rd) = (st.sem(n) for n in names)
    bank = st.psum_banks()

    def tokens(ap):
        return ap.rearrange("p (b s) -> p b s", b=NB)

    with nc.Block() as block:

        @block.gpsimd
        def _(pool):
            norm.gpsimd_rstd(pool)
            pool.memset(hp[:, :, :, 0:1], 0.0).then_inc(s_pad, 1)
            pool.memset(hp[:, :, :, S + 1:S + 2], 0.0).then_inc(s_pad, 1)
            pool.wait_ge(s_inv, 1)
            for t in range(TT):
                ins = pool.tensor_tensor(dg[:, t, :], w["ident"][:], inv[:, 0, t:t + 1].broadcast_to([P, P]), ALU.mult)
            ins.then_inc(s_dg, 1)

        @block.scalar
        def _(act):
            act.wait_ge(s_rs, 1)
            act.activation(rowinv[:], bank[0][:, :], ACT.Copy).then_inc(s_ri, 1)
            for c in range(HC):
                act.wait_ge(s_cv, c + 1)
                act.activation(y[:, c, :], y[:, c, :], ACT.Silu).then_inc(s_ac, 1)
            for c in range(HC):
                act.wait_ge(s_q2t, c + 1)
                act.activation(q2T[:, c, :], bank[c][:, 0:TOK // 2].bitcast(BF16), ACT.Copy).then_inc(s_q2T, 1)

        @block.vector
        def _(dve):
            link = Chain(dve, s_chain)

            def levels(i, t0, t1, src_of, out, width, s_done):
                a, n, s = amax[:, i, t0:t1], inv[:, i, t0:t1], scale[:, i, t0:t1]
                link(dve.tensor_scalar(a, a, EPS, None, ALU.max))
                link(dve.tensor_scalar(n, a, 1.0 / 127.0, None, ALU.mult))
                link(dve.reciprocal(s, a))
                link(dve.tensor_scalar(s, s, 127.0, None, ALU.mult))
                for t in range(t0, t1):
                    ins = dve.tensor_scalar(r[:, t, 0:width], src_of(t), scale[:, i, t:t + 1], 127.0, ALU.mult, ALU.min)
                    if i:
                        ins.then_inc(s_rd, 1)
                        dve.wait_ge(s_rd, t + 1)
                    else:
                        link(ins)
                link(dve.tensor_scalar(r[:, t0:t1, 0:width], r[:, t0:t1, 0:width], -128.0, MAGIC, ALU.max, ALU.add))
                dve.tensor_scalar(out, r[:, t0:t1, 0:width], MAGIC, None, ALU.subtract).then_inc(s_done, 1)

            norm.vector_stats(dve, link, x)
            norm.vector_apply(dve, xn, x, s_xn)
            dve.wait_ge(s_xn, TT)
            link(dve.tensor_reduce(amax[:, 0, :], xn[:], AX, ALU.max, apply_absolute_value=True))
            levels(0, 0, TT, lambda t: xn[:, t, :], xq[:], D, s_xq)
            dve.wait_ge(s_xq, 1)
            link(dve.tensor_scalar(inv[:, 0, :], inv[:, 0, :], w["ffn_wmean"][:, 0:1], None, ALU.mult))
            dve.tensor_copy(scale[:, 0, :], inv[:, 0, :]).then_inc(s_inv, 1)
            dve.wait_ge(s_xqt, 1)
            dve.tensor_copy(xqT[:], bank[1][:, 0:TOK // 2].bitcast(BF16)).then_inc(s_xqT, 1)
            dve.wait_ge(s_ri, 1)
            dve.wait_ge(s_pad, 2)
            w.loaded(dve, "ffn")
            cw = w["ffn_conv"]
            for c in range(HC):
                dve.wait_ge(s_h, c + 1)
                link(dve.tensor_tensor(hp[:, c, :, 1:S + 1], tokens(bank[2 + c][:, :]), tokens(rowinv[:]), ALU.mult))
                v = tokens(y[:, c, :])
                link(dve.tensor_scalar(v, hp[:, c, :, 1:S + 1], cw[:, c, 1:2], cw[:, c, 3:4], ALU.mult, ALU.add))
                link(dve.scalar_tensor_tensor(v, hp[:, c, :, 0:S], cw[:, c, 0:1], v, ALU.mult, ALU.add))
                dve.scalar_tensor_tensor(v, hp[:, c, :, 2:S + 2], cw[:, c, 2:3], v, ALU.mult, ALU.add).then_inc(s_cv, 1)
            for t in range(TT):
                dve.wait_ge(s_act, t + 1)
                link(dve.tensor_reduce(amax[:, 1, t:t + 1], bank[4 + t][:, :], AX, ALU.max, apply_absolute_value=True))
                levels(1, t, t + 1, lambda t: bank[4 + t][:, :], q2[:, t, :], HID, s_q2)
            dve.wait_ge(s_q2, TT)
            link(dve.tensor_scalar(inv[:, 1, :], inv[:, 1, :], w["ffn_wmean"][:, 1:2], None, ALU.mult))
            for t in range(TT):
                dve.wait_ge(s_pr, t + 1)
                dve.scalar_tensor_tensor(x[:, t, :], bank[4 + t][:, 0:D], inv[:, 1, t:t + 1], x[:, t, :], ALU.mult, ALU.add).then_inc(s_x, 1)

        @block.tensor
        def _(pe):
            pe.wait_ge(s_xq, 1)
            for t in range(TT):
                ins = pe.transpose(bank[1][:, 0:TOK // 2].bitcast(BF16)[:, t * P:(t + 1) * P], xq[:, t, :], w["ident_bf"][:])
            ins.then_inc(s_xqt, 1)
            pe.wait_ge(s_dg, 1)
            for t in range(TT):
                ins = pe.matmul(bank[0][:, t * P:(t + 1) * P], w["ones"][:], dg[:, t, :], start=(t == 0), stop=True, skip_group_check=True)
            ins.then_inc(s_rs, 1)
            pe.wait_ge(s_xqT, 1)
            for c in range(HC):
                pe.matmul(bank[2 + c][:, :], w["ffn_q"][:, 0, c * P:(c + 1) * P], xqT[:], start=True, stop=True).then_inc(s_h, 1)
            pe.wait_ge(s_ac, HC)
            for t in range(TT):
                for c in range(HC):
                    ins = pe.transpose(bank[4 + t][:, c * P:(c + 1) * P], y[:, c, t * P:(t + 1) * P], w["ident"][:])
                ins.then_inc(s_act, 1)
            pe.wait_ge(s_q2, TT)
            for c in range(HC):
                for t in range(TT):
                    ins = pe.transpose(bank[c][:, 0:TOK // 2].bitcast(BF16)[:, t * P:(t + 1) * P], q2[:, t, c * P:(c + 1) * P], w["ident_bf"][:])
                ins.then_inc(s_q2t, 1)
            pe.wait_ge(s_q2T, HC)
            for t in range(TT):
                for c in range(HC):
                    ins = pe.matmul(bank[4 + t][:, 0:D], q2T[:, c, t * P:(t + 1) * P], w["ffn_q"][:, 1, c * P:(c + 1) * P],
                                    start=(c == 0), stop=(c == HC - 1))
                ins.then_inc(s_pr, 1)
    st.close()


def alibi_attention(nc, w, x):
    st = Stage(nc, "l1a")
    HK, DQ, DV = 4, 4, 8
    NQ, NV = H * DQ, HK * DV
    W = NQ + HK * DQ + NV
    SW = 32
    xn = st.sb("xn", [P, TT, D])
    xT = st.sb("xT", [P, TOK])
    NQK = NQ + HK * DQ
    sp_ = st.sb("split", [P, 2, 3, NQK], BF16)
    sr = st.sb("rest_qk", [P, 2, NQK])
    stack = st.sb("stack", [P, TT, H + HK, SW], BF16)
    qkT = st.sb("qkT", [P, 5, TOK], BF16)
    vals = st.sb("vals", [P, TT, HK, 32])
    xb = st.sb("x_bias", [P, TT, D])
    y = st.sb("y", [P, TT, D])
    yT = st.sb("yT", [P, TOK])
    osb = st.sb("o", [P, 2, S])
    rz = st.sb("rz", [P, 2 * Q4])
    norm = Norm(st, w)
    s_chain = st.sem("dve_chain")
    s_xn = st.sem("xn_ready")
    s_xTp = st.sem("x_transposed")
    s_xT = st.sem("xT_ready")
    s_qkv = st.sem("qkv_ready")
    s_split = st.sem("parts_ready")
    s_v = st.sem("values_ready")
    s_stq = st.sem("q_stack_ready")
    s_stk = st.sem("k_stack_ready")
    s_init = st.sem("buffers_set")
    s_stT = st.sem("stack_transposed")
    s_qkT = st.sem("qkT_ready")
    s_ob = st.sem("o_transposed")
    s_fin = st.sem("o_finished")
    s_xb = st.sem("x_bias_ready")
    s_yT = st.sem("yT_ready")
    s_yTp = st.sem("y_transposed")
    s_wp = st.sem("product_ready")
    s_x = st.sem("x_updated")
    bank = st.psum_banks()
    SBK, EBK, OBK, G0, G1 = bank[0:2], bank[2:4], bank[4:6], bank[6], bank[7]

    def at(group, b, h, t0, n):
        r = SW * (h % HK)
        return qkT[r:r + SW, group, b * S + t0:b * S + t0 + n]

    a = Attention(st, w, causal=True, lse=False, scale=float(DQ) ** -0.5, heads_per_out=Q4,
                  q=lambda b, h, t0, n: at(h // HK, b, h, t0, n), k=lambda b, h, t0, n: at(4, b, h, t0, n),
                  values=lambda b, h, c: vals[:, b * SB + c, h % HK, :], out_rows=32)
    GROUPS = U // Q4
    with nc.Block() as block:

        @block.gpsimd
        def _(pool):
            w.loaded(pool, "l1a")
            pool.memset(stack[:, :, :, 6 * DQ + 6:SW], 0.0).then_inc(s_init, 1)
            pool.memset(a.parts[:], 0.0).then_inc(a.s_zero, 1)
            for t in range(TT):
                pool.tensor_copy(stack[:, t, 0:H, 6 * DQ:6 * DQ + 6], w["alibi_q"][:, t % SB, :, :])
                ins = pool.tensor_copy(stack[:, t, H:H + HK, 6 * DQ:6 * DQ + 6],
                                       w["alibi_k"][:, t % SB, :].unsqueeze(1).broadcast_to([P, HK, 6]))
            ins.then_inc(s_init, 1)
            norm.gpsimd_rstd(pool)
            pool.tensor_tensor(xb[:], x[:], w["l1a_bp"][:].unsqueeze(1).broadcast_to([P, TT, D]), ALU.add).then_inc(s_xb, 1)
            for t in range(TT):
                pool.wait_ge(s_split, t + 1)
                for part, i, n in split_columns(Q_PARTS):
                    out = stack[:, t, 0:H, i * DQ:(i + n) * DQ].rearrange("p h (n d) -> p h n d", n=n)
                    src = sp_[:, t % 2, part, 0:NQ].rearrange("p (h d) -> p h d", h=H).unsqueeze(2).broadcast_to([P, H, n, DQ])
                    ins = pool.tensor_copy(out, src)
                ins.then_inc(s_stq, 1)

        @block.scalar
        def _(act):
            act.wait_ge(s_xTp, 1)
            act.activation(xT[:], G0[:, :], ACT.Copy).then_inc(s_xT, 1)
            act.wait_ge(s_init, 4)
            for t in range(TT):
                act.wait_ge(s_split, t + 1)
                act.activation(vals[:, t, :, 0:DV], EBK[t % 2][:, NQK:W].rearrange("p (h d) -> p h d", h=HK), ACT.Copy).then_inc(s_v, 1)
                for part, i, n in split_columns(K_PARTS):
                    ins = act.activation(stack[:, t, H:H + HK, i * DQ:(i + n) * DQ],
                                         sp_[:, t % 2, part, NQ:NQK].rearrange("p (h d) -> p h d", h=HK), ACT.Copy)
                ins.then_inc(s_stk, 1)
            for n in range(U + 2):
                if n < U:
                    a.scalar_exp(act, n, EBK[n % 2])
                if n % Q4 == 0 and n:
                    g = n // Q4 - 1
                    act.wait_ge(a.s_pv, n)
                    if g >= 2:
                        act.wait_ge(s_ob, g - 1)
                    act.activation(osb[:, g % 2, :], OBK[g % 2][:, 0:S], ACT.Copy).then_inc(a.s_og, 1)
            act.wait_ge(s_yTp, 1)
            act.activation(yT[:], G0[:, :], ACT.Copy).then_inc(s_yT, 1)

        @block.vector
        def _(dve):
            link = Chain(dve, s_chain)
            norm.vector_stats(dve, link, x)
            dve.memset(vals[:], 0.0).then_inc(s_init, 1)
            dve.wait_ge(s_init, 3)
            dve.memset(vals[:, :, :, DV:DV + 1], 1.0).then_inc(s_init, 1)
            norm.vector_apply(dve, xn, x, s_xn)
            for t in range(TT):
                dve.wait_ge(s_qkv, t + 1)
                if t >= 2:
                    dve.wait_ge(s_stq, t - 1)
                    dve.wait_ge(s_stk, t - 1)
                qk = EBK[t % 2][:, 0:NQK]
                hi, mid, lo = (sp_[:, t % 2, i, :] for i in range(3))
                link(dve.tensor_copy(hi, qk))
                link(dve.tensor_tensor(sr[:, t % 2, :], qk, hi, ALU.subtract))
                link(dve.tensor_copy(mid, sr[:, t % 2, :]))
                dve.tensor_tensor(lo, sr[:, t % 2, :], mid, ALU.subtract).then_inc(s_split, 1)
            for g in range(5):
                dve.wait_ge(s_stT, g + 1)
                dve.tensor_copy(qkT[:, g, :], bank[6 + g % 2][:, 0:TOK // 2].bitcast(BF16)).then_inc(s_qkT, 1)
            for u in range(H):
                a.vector_max(dve, u, SBK[u % 2])
            a.vector_parts(dve, link, 0)
            for n in range(U + 3):
                b, h = divmod(n, H)
                if h == 0 and b < NB:
                    a.vector_shiftT(dve, b, G0)
                if n + H < U:
                    a.vector_max(dve, n + H, SBK[n % 2])
                if h == H - 1 and b + 1 < NB:
                    a.vector_parts(dve, link, b + 1)
                if n >= Q4 + 2 and (n - 2) % Q4 == 0:
                    g = (n - 2) // Q4 - 1
                    b2, hg = divmod(g, H // Q4)
                    dve.wait_ge(s_ob, g + 1)
                    if g:
                        dve.wait_ge(s_fin, g)
                    o = G1[:, 0:SB * P].rearrange("p (c r) -> p c r", r=32)
                    link(dve.reciprocal(rz[:], o[:, :, DV]))
                    dst = y[:, b2 * SB:(b2 + 1) * SB, hg * 32:(hg + 1) * 32].rearrange("p c (j d) -> p c j d", d=DV)
                    for c in range(SB):
                        ins = dve.tensor_tensor(dst[:, c], o[:, c * Q4:(c + 1) * Q4, 0:DV],
                                                bcast(rz[:, c * Q4:(c + 1) * Q4], Q4, DV), ALU.mult)
                    ins.then_inc(s_fin, 1)
            dve.wait_ge(s_xb, 1)
            for t in range(TT):
                dve.wait_ge(s_wp, t + 1)
                dve.tensor_tensor(x[:, t, :], bank[t % 4][:, 0:D], xb[:, t, :], ALU.add).then_inc(s_x, 1)

        @block.tensor
        def _(pe):
            tensor_transpose_tiles(pe, w, G0, xn, s_xn, s_xTp)
            w.loaded(pe, "l1a")
            pe.wait_ge(s_xT, 1)
            for t in range(TT):
                if t >= 2:
                    pe.wait_ge(s_v, t - 1)
                pe.matmul(EBK[t % 2][:, 0:W], xT[:, t * P:(t + 1) * P], w["l1a_qkv"][:], start=True, stop=True).then_inc(s_qkv, 1)
            pe.wait_ge(s_init, 4)
            for g in range(5):
                if g >= 2:
                    pe.wait_ge(s_qkT, g - 1)
                for t in range(TT):
                    pe.wait_ge(s_stq, t + 1)
                    pe.wait_ge(s_stk, t + 1)
                    ins = pe.transpose(bank[6 + g % 2][:, 0:TOK // 2].bitcast(BF16)[:, t * P:(t + 1) * P],
                                       stack[:, t, g * HK:(g + 1) * HK, :], w["ident_bf"][:])
                ins.then_inc(s_stT, 1)
            pe.wait_ge(s_qkT, 5)
            for u in range(H):
                a.tensor_S(pe, u, SBK[u % 2])
            for n in range(U + 3):
                b, h = divmod(n, H)
                if h == 0 and b < NB:
                    a.tensor_shift(pe, b, G0)
                if n < U:
                    a.tensor_E(pe, n, EBK[n % 2])
                if n + H < U:
                    a.tensor_S(pe, n + H, SBK[n % 2])
                if 1 <= n <= U:
                    a.tensor_PV(pe, n - 1, OBK[(n - 1) // Q4 % 2])
                if n >= Q4 + 2 and (n - 2) % Q4 == 0:
                    g = (n - 2) // Q4 - 1
                    pe.wait_ge(a.s_og, g + 1)
                    if g:
                        pe.wait_ge(s_fin, g)
                    for c in range(SB):
                        ins = pe.transpose(G1[:, c * P:(c + 1) * P], osb[:, g % 2, c * P:(c + 1) * P], w["ident"][:])
                    ins.then_inc(s_ob, 1)
            pe.wait_ge(s_fin, GROUPS)
            for t in range(TT):
                ins = pe.transpose(G0[:, t * P:(t + 1) * P], y[:, t, :], w["ident"][:])
            ins.then_inc(s_yTp, 1)
            pe.wait_ge(s_yT, 1)
            for t in range(TT):
                pe.matmul(bank[t % 4][:, 0:D], yT[:, t * P:(t + 1) * P], w["l1a_p"][:], start=True, stop=True).then_inc(s_wp, 1)
    st.close()


def head_attention(nc, w, x, ctx, v_dram):
    st = Stage(nc, "l1x")
    HD = 64
    assert NB == 2
    GT = P // H
    NG = S // GT
    GB = 4
    NU = NB * NG // GB
    UB = NU // NB
    J = 8
    xn = st.sb("xn", [P, TT, D])
    xT = st.sb("xT", [P, 2, TOK])
    qT = st.sb("qT", [P, S, H])
    kT = st.sb("kT", [P, S, H])
    vt = st.sb("v_tokens", [P, 2, H * HD])
    vg = st.sb("v_groups", [P, NB * NG, HD])
    oT = st.sb("oT", [P, NB, J, H, S // 16])
    xb = st.sb("x_bias", [P, TT, D])
    nmax = st.sb("nmax", [P, NB, NG])
    zsum = st.sb("zsum", [P, NB, NG])
    lnz = st.sb("lnz", [P, NG])
    shift = st.sb("shift", [P, NG])
    rest = st.sb("rest", [P, NG])
    parts = st.sb("parts", [P, NB, P], BF16)
    shiftT = st.sb("shiftT", [P, NB, P], BF16)
    expT = st.sb("expT", [P, 3, GB * P])
    norm = Norm(st, w)
    names = ("dve_chain", "xn_ready", "transposed", "xT_ready", "x_bias_ready", "v_projected", "v_biased", "v_stored", "v_regrouped",
             "heads_projected", "heads_by_scalar", "heads_by_vector", "max_scores_ready", "max_done", "sum_done", "log_ready",
             "parts_set", "parts_ready", "shift_transposed", "shiftT_ready", "exp_scores_ready", "exp_ready", "exp_used",
             "out_evicted", "product_ready", "x_updated")
    (s_chain, s_xn, s_tp, s_xT, s_xb, s_vp, s_vb, s_vs, s_vg, s_pr, s_pa, s_pv, s_s, s_mx, s_lse, s_ln, s_ps, s_parts, s_shp, s_shT,
     s_e, s_p, s_used, s_og, s_wo, s_x) = (st.sem(n) for n in names)
    bank = st.psum_banks()
    SBK, EBK, OBK, G0, G1 = bank[0:2], bank[2:4], bank[4:6], bank[6], bank[7]
    jobs = [(kind, c) for kind in "kq" for c in range(H // 2)]

    def group(buf, n, i):
        u, q = divmod(n, UB)
        g = q * GB + i
        return buf[HD * u:HD * (u + 1), g * GT:(g + 1) * GT, :].rearrange("p t h -> p (t h)")

    with nc.Block() as block:

        @block.sync
        def _(sp):
            for t in range(TT):
                sp.wait_ge(s_vb, 2 * t + 2)
                sp.dma_start(v_dram[t * P:(t + 1) * P, :], vt[:, t % 2, :]).then_inc(s_vs, 16)
                sp.wait_ge(s_vs, 16 * (t + 1))
                src = v_dram[t * P:(t + 1) * P, :].rearrange("(g t) (h d) -> (t h) g d", t=GT, d=HD)
                sp.dma_start(vg[:, t * (P // GT):(t + 1) * (P // GT), :], src).then_inc(s_vg, 16)
            sp.wait_ge(s_vg, 16 * TT)

        @block.gpsimd
        def _(pool):
            w.loaded(pool, "l1x")
            pool.tensor_tensor(xb[:], x[:], w["l1x_bo"][:].unsqueeze(1).broadcast_to([P, TT, D]), ALU.add).then_inc(s_xb, 1)
            for u in range(NB):
                pool.memset(parts[:, u, 3 * NG + GT:P], 0.0)
                ins = pool.tensor_copy(parts[:, u, 3 * NG:3 * NG + GT], w["other_token"][:])
            ins.then_inc(s_ps, 1)
            norm.gpsimd_rstd(pool)

        @block.scalar
        def _(act):
            act.wait_ge(s_tp, 1)
            act.activation(xT[:, 1, :], G0[:, :], ACT.Copy).then_inc(s_xT, 1)
            w.loaded(act, "l1x")
            for n in range(0, len(jobs), 2):
                if jobs[n] == ("q", 0):
                    act.wait_ge(s_tp, 2)
                    act.activation(xT[:, 0, :], G1[:, :], ACT.Copy).then_inc(s_xT, 1)
                kind, c = jobs[n]
                buf, bias = (qT, "l1x_bq") if kind == "q" else (kT, "l1x_bk")
                act.wait_ge(s_pr, n + 1)
                for i in range(2):
                    h = 2 * c + i
                    ins = act.activation(buf[:, :, h], bank[n % 4][:, i * S:(i + 1) * S], ACT.Identity,
                                         bias=w[bias][:, h:h + 1], scale=float(HD) ** -0.5 if kind == "q" else 1.0)
                ins.then_inc(s_pa, 1)

            def row_sums(n):
                u, q = divmod(n, UB)
                act.wait_ge(s_mx, n + 1)
                for i in range(GB):
                    part = SBK[n % 2][:, i * P:(i + 1) * P]
                    g = q * GB + i
                    ins = act.activation(part, part, ACT.Exp, bias=nmax[:, u, g:g + 1], accum_out=zsum[:, u, g:g + 1])
                ins.then_inc(s_lse, 1)

            def logs(u):
                act.wait_ge(s_lse, UB * (u + 1))
                if u:
                    act.wait_ge(s_parts, u)
                act.activation(lnz[:], zsum[:, u, :], ACT.Ln).then_inc(s_ln, 1)

            for n in range(UB):
                row_sums(n)
            logs(0)
            for n in range(NU + 1):
                if n < NU:
                    act.wait_ge(s_e, n + 1)
                    if n >= 3:
                        act.wait_ge(s_used, n - 2)
                    act.activation(expT[:, n % 3, :], EBK[n % 2][:, :], ACT.Exp).then_inc(s_p, 1)
                if n + UB < NU:
                    row_sums(n + UB)
                if n % UB == UB - 1 and n // UB + 1 < NB:
                    logs(n // UB + 1)

        @block.vector
        def _(dve):
            link = Chain(dve, s_chain)
            w.loaded(dve, "l1x")
            for i in range(2 * TT):
                t, half = divmod(i, 2)
                dve.wait_ge(s_vp, i + 1)
                if t >= 2 and half == 0:
                    dve.wait_ge(s_vs, 16 * (t - 1))
                dve.tensor_tensor(vt[:, t % 2, half * 512:(half + 1) * 512], bank[4 + i % 2][:, :],
                                  w["l1x_bv"][:, half * 512:(half + 1) * 512], ALU.add).then_inc(s_vb, 1)
            norm.vector_stats(dve, link, x)
            norm.vector_apply(dve, xn, x, s_xn)
            for n in range(1, len(jobs), 2):
                kind, c = jobs[n]
                buf, bias = (qT, "l1x_bq") if kind == "q" else (kT, "l1x_bk")
                dve.wait_ge(s_pr, n + 1)
                for i in range(2):
                    h = 2 * c + i
                    ins = dve.tensor_scalar(buf[:, :, h], bank[n % 4][:, i * S:(i + 1) * S],
                                            float(HD) ** -0.5 if kind == "q" else 1.0, w[bias][:, h:h + 1], ALU.mult, ALU.add)
                ins.then_inc(s_pv, 1)

            def maxima(n):
                u, q = divmod(n, UB)
                dve.wait_ge(s_s, n + 1)
                dve.tensor_reduce(nmax[:, u, q * GB:(q + 1) * GB], SBK[n % 2][:, :].rearrange("p (g k) -> p g k", g=GB), AX, ALU.max,
                                  negate=True).then_inc(s_mx, 1)

            def split(u):
                dve.wait_ge(s_ln, u + 1)
                link(dve.tensor_tensor(shift[:], nmax[:, u, :], lnz[:], ALU.subtract))
                hi, mid, lo = (parts[:, u, i * NG:(i + 1) * NG] for i in range(3))
                link(dve.tensor_copy(hi, shift[:]))
                link(dve.tensor_tensor(rest[:], shift[:], hi, ALU.subtract))
                link(dve.tensor_copy(mid, rest[:]))
                dve.tensor_tensor(lo, rest[:], mid, ALU.subtract).then_inc(s_parts, 1)

            for n in range(UB):
                maxima(n)
            split(0)
            for n in range(NU + 2):
                u = n // UB
                if n % UB == 0 and u < NB:
                    dve.wait_ge(s_shp, u + 1)
                    dve.tensor_copy(shiftT[:, u, :], G0[:, 0:P // 2].bitcast(BF16)).then_inc(s_shT, 1)
                if n + UB < NU:
                    maxima(n + UB)
                if n % UB == UB - 1 and u + 1 < NB:
                    split(u + 1)
                if n >= 2:
                    m = n - 2
                    u2, q = divmod(m, UB)
                    dve.wait_ge(s_used, m + 1)
                    out = oT[:, u2, :, :, 2 * q:2 * q + 2].rearrange("p j h s -> p s j h")
                    for s in range(2):
                        ins = dve.tensor_copy(out[:, s], OBK[m % 2][:, s * P:(s + 1) * P].rearrange("p (j h) -> p j h", j=J))
                    ins.then_inc(s_og, 1)
            dve.wait_ge(s_xb, 1)
            for t in range(TT):
                dve.wait_ge(s_wo, t + 1)
                dve.tensor_tensor(x[:, t, :], bank[t % 4][:, 0:D], xb[:, t, :], ALU.add).then_inc(s_x, 1)

        @block.tensor
        def _(pe):
            w.loaded(pe, "l1x")
            for t in range(TT):
                ins = pe.transpose(G0[:, t * P:(t + 1) * P], ctx[:, t, :], w["ident"][:])
            ins.then_inc(s_tp, 1)
            pe.wait_ge(s_xT, 1)
            for i in range(2 * TT):
                t, half = divmod(i, 2)
                if i >= 2:
                    pe.wait_ge(s_vb, i - 1)
                pe.matmul(bank[4 + i % 2][:, :], xT[:, 1, t * P:(t + 1) * P], w["l1x_v"][:, half * 512:(half + 1) * 512],
                          start=True, stop=True).then_inc(s_vp, 1)
            for n, (kind, c) in enumerate(jobs):
                if (kind, c) == ("q", 0):
                    tensor_transpose_tiles(pe, w, G1, xn, s_xn, s_tp)
                    pe.wait_ge(s_xT, 2)
                if n >= 4:
                    pe.wait_ge(s_pv if n % 2 else s_pa, n // 2 - 1)
                for i in range(2):
                    for u in range(NB):
                        h = 2 * c + i
                        ins = pe.matmul(bank[n % 4][HD * u:HD * (u + 1), i * S:(i + 1) * S], w[f"l1x_{kind}"][:, h * HD:(h + 1) * HD],
                                        xT[:, int(kind == "k"), u * S:(u + 1) * S], start=(i == 0), stop=True, skip_group_check=True)
                ins.then_inc(s_pr, 1)
            pe.wait_ge(s_pa, len(jobs) // 2)
            pe.wait_ge(s_pv, len(jobs) // 2)

            def scores_for_max(n):
                if n >= 2:
                    pe.wait_ge(s_lse, n - 1)
                out = SBK[n % 2]
                pe.matmul(out[:, :], w["same_token"][:], w["other_token4"][:], start=True, stop=False, skip_group_check=True)
                for i in range(GB):
                    ins = pe.matmul(out[:, i * P:(i + 1) * P], group(qT, n, i), group(kT, n, i), start=False, stop=True, skip_group_check=True)
                ins.then_inc(s_s, 1)

            def scores_for_exp(n):
                u, q = divmod(n, UB)
                if n >= 2:
                    pe.wait_ge(s_p, n - 1)
                out = EBK[n % 2]
                for i in range(GB):
                    pe.matmul(out[:, i * P:(i + 1) * P], w["sel_group"][:, q * GB + i, :], shiftT[:, u, :], start=(i == 0), stop=False,
                              skip_group_check=True)
                for i in range(GB):
                    ins = pe.matmul(out[:, i * P:(i + 1) * P], group(kT, n, i), group(qT, n, i), start=False, stop=True, skip_group_check=True)
                ins.then_inc(s_e, 1)

            def weighted_values(n):
                u, q = divmod(n, UB)
                pe.wait_ge(s_p, n + 1)
                if q == 0:
                    pe.wait_ge(s_vg, 16 * TT)
                if n >= 2:
                    pe.wait_ge(s_og, n - 1)
                for i in range(GB):
                    r = HD * (i % 2)
                    ins = pe.matmul(OBK[n % 2][r:r + HD, (i // 2) * P:(i // 2 + 1) * P], vg[:, u * NG + q * GB + i, :],
                                    expT[:, n % 3, i * P:(i + 1) * P], start=(i < 2), stop=True, skip_group_check=True)
                ins.then_inc(s_used, 1)

            for n in range(UB):
                scores_for_max(n)
            for n in range(NU + 1):
                u = n // UB
                if n % UB == 0 and u < NB:
                    pe.wait_ge(s_ps, 1)
                    pe.wait_ge(s_parts, u + 1)
                    pe.transpose(G0[:, 0:P // 2].bitcast(BF16), parts[:, u, :], w["ident_bf"][:]).then_inc(s_shp, 1)
                if n < NU:
                    if n % UB == 0:
                        pe.wait_ge(s_shT, u + 1)
                    scores_for_exp(n)
                if n + UB < NU:
                    scores_for_max(n + UB)
                if n:
                    weighted_values(n - 1)
            pe.wait_ge(s_og, NU)
            for t in range(TT):
                u, c = divmod(t, SB)
                for j in range(J):
                    ins = pe.matmul(bank[t % 4][:, 0:D], oT[:, u, j, c * J:(c + 1) * J, :].rearrange("p h s -> p (h s)"),
                                    w["l1x_o"][:, j, :], start=(j == 0), stop=(j == J - 1))
                ins.then_inc(s_wo, 1)
    st.close()


def expert_ffn(nc, w, x):
    st = Stage(nc, "moe")
    NE = E + 1
    ALPHA, LIMIT = 1.702, 7.0
    xn = st.sb("xn", [P, TT, D])
    xT = st.sb("xT", [P, TOK])
    logit = st.sb("logit", [P, TT, E])
    small = st.sb("small", [P, 2, TT])
    score = st.sb("score", [P, TT, E])
    biased = st.sb("biased", [P, TT, E])
    above = st.sb("above", [P, TT, E, E])
    equal = st.sb("equal", [P, TT, E, E])
    rank = st.sb("rank", [P, TT, E])
    cw = st.sb("expert_weight", [P, TT, NE])
    cwT = st.sb("expert_weightT", [NE, TOK])
    h1 = st.sb("h1", [P, 2, TOK])
    hh = st.sb("h13", [P, 2, TOK])
    g = st.sb("gate", [P, 2, TOK])
    sg = st.sb("sigmoid", [P, 2, TOK])
    act_in = st.sb("l1g", [P, 2, TOK])
    a = st.sb("a", [P, 2, TOK])
    norm = Norm(st, w)
    names = ("dve_chain", "xn_ready", "transposed", "xT_ready", "logits_ready", "shifted_ready", "exp_ready", "cw_ready", "cw_transposed",
             "cwT_ready", "bias_ready", "x_seeded", "hidden_ready", "h1_ready", "h13_ready", "gate_ready", "sigmoid_ready", "lg_ready",
             "a_ready", "y_ready", "y_added")
    (s_chain, s_xn, s_tp, s_xT, s_lg, s_sh, s_ex, s_cw, s_cwp, s_cwT, s_b, s_xs, s_h, s_h1, s_hh, s_g, s_sg, s_l, s_a, s_y,
     s_ya) = (st.sem(n) for n in names)
    bank = st.psum_banks()
    G0, G1 = bank[6], bank[7]

    def pair(n):
        return bank[2 * (n % 3)], bank[2 * (n % 3) + 1]

    with nc.Block() as block:

        @block.gpsimd
        def _(pool):
            pool.memset(cw[:, :, E:NE], 1.0).then_inc(s_cw, 1)
            norm.gpsimd_rstd(pool)
            for e in range(NE):
                pool.wait_ge(s_l, e + 1)
                pool.wait_ge(s_sg, e + 1)
                if e >= 2:
                    pool.wait_ge(s_y, e - 1)
                pool.tensor_tensor(a[:, e % 2, :], act_in[:, e % 2, :], sg[:, e % 2, :], ALU.mult).then_inc(s_a, 1)

        @block.scalar
        def _(act):
            act.wait_ge(s_tp, 1)
            act.activation(xT[:], G0[:, :], ACT.Copy).then_inc(s_xT, 1)
            act.wait_ge(s_sh, 1)
            act.activation(score[:], logit[:], ACT.Exp).then_inc(s_ex, 1)
            w.loaded(act, "moe")

            def sigmoid(e):
                act.wait_ge(s_g, e + 1)
                if e >= 2:
                    act.wait_ge(s_a, e - 1)
                act.activation(sg[:, e % 2, :], g[:, e % 2, :], ACT.Sigmoid, scale=ALPHA).then_inc(s_sg, 1)

            for n in range(2 * NE):
                e, part = divmod(n, 2)
                act.wait_ge(s_h, n + 1)
                if n >= 2:
                    act.wait_ge(s_hh, n - 1)
                act.activation(h1[:, n % 2, :], pair(n)[0][:, :], ACT.Identity, bias=w["moe_b1"][:, e, part:part + 1]).then_inc(s_h1, 1)
                if part:
                    sigmoid(e)

        @block.vector
        def _(dve):
            link = Chain(dve, s_chain)
            norm.vector_stats(dve, link, x)
            norm.vector_apply(dve, xn, x, s_xn)
            dve.wait_ge(s_lg, 1)
            lg = G1[:, 0:TT * E].rearrange("p (t e) -> p t e", t=TT)
            link(dve.tensor_reduce(small[:, 0, :], lg, AX, ALU.max, negate=True))
            dve.tensor_tensor(logit[:], lg, bcast(small[:, 0, :], TT, E), ALU.add).then_inc(s_sh, 1)
            dve.wait_ge(s_ex, 1)
            w.loaded(dve, "moe")
            link(dve.tensor_reduce(small[:, 1, :], score[:], AX, ALU.add))
            link(dve.reciprocal(small[:, 0, :], small[:, 1, :]))
            link(dve.tensor_tensor(score[:], score[:], bcast(small[:, 0, :], TT, E), ALU.mult))
            link(dve.tensor_tensor(biased[:], score[:], w["moe_gate_b"][:].unsqueeze(1).broadcast_to([P, TT, E]), ALU.add))
            for t in range(TT):
                mine = bcast(biased[:, t, :], E, E)
                theirs = biased[:, t, :].unsqueeze(1).broadcast_to([P, E, E])
                dve.tensor_tensor(above[:, t], theirs, mine, ALU.is_gt)
                ins = dve.tensor_tensor(equal[:, t], theirs, mine, ALU.is_equal)
            link(ins)
            link(dve.tensor_tensor(equal[:], equal[:], w["before"][:].unsqueeze(1).broadcast_to([P, TT, E * E]).rearrange("p t (e f) -> p t e f", e=E), ALU.mult))
            link(dve.tensor_tensor(above[:], above[:], equal[:], ALU.add))
            link(dve.tensor_reduce(rank[:], above[:], AX, ALU.add))
            dve.wait_ge(s_cw, 1)
            dve.scalar_tensor_tensor(cw[:, :, 0:E], rank[:], 2.0, score[:], ALU.is_lt, ALU.mult).then_inc(s_cw, 1)
            dve.wait_ge(s_cwp, 1)
            dve.tensor_copy(cwT[:], G0[0:NE, :]).then_inc(s_cwT, 1)
            dve.wait_ge(s_b, 1)
            dve.tensor_tensor(x[:], x[:], G1[:, :].rearrange("p (t d) -> p t d", t=TT), ALU.add).then_inc(s_xs, 1)

            def add_expert(e):
                dve.wait_ge(s_y, e + 1)
                if e:
                    dve.wait_ge(s_ya, e)
                else:
                    dve.wait_ge(s_xs, 1)
                for t in range(TT):
                    ins = dve.scalar_tensor_tensor(x[:, t, :], bank[6 + e % 2][:, t * P:(t + 1) * P], cw[:, t, e:e + 1], x[:, t, :],
                                                   ALU.mult, ALU.add)
                ins.then_inc(s_ya, 1)

            for n in range(2 * NE):
                e, part = divmod(n, 2)
                dve.wait_ge(s_h1, n + 1)
                if n >= 2:
                    dve.wait_ge(s_g if part == 0 else s_l, n // 2)
                dve.scalar_tensor_tensor(hh[:, n % 2, :], pair(n)[1][:, :], w["moe_b3"][:, e, part:part + 1], h1[:, n % 2, :],
                                         ALU.add, ALU.mult).then_inc(s_hh, 1)
                dve.wait_ge(s_hh, n + 1)
                if part == 0:
                    if e >= 2:
                        dve.wait_ge(s_sg, e - 1)
                    dve.tensor_scalar(g[:, e % 2, :], hh[:, 0, :], LIMIT, None, ALU.min).then_inc(s_g, 1)
                else:
                    link(dve.tensor_scalar(hh[:, 1, :], hh[:, 1, :], LIMIT, -LIMIT, ALU.min, ALU.max))
                    if e >= 2:
                        dve.wait_ge(s_a, e - 1)
                    dve.scalar_tensor_tensor(act_in[:, e % 2, :], hh[:, 1, :], 1.0, g[:, e % 2, :], ALU.add, ALU.mult).then_inc(s_l, 1)
                    if e:
                        add_expert(e - 1)
            add_expert(NE - 1)

        @block.tensor
        def _(pe):
            tensor_transpose_tiles(pe, w, G0, xn, s_xn, s_tp)
            pe.wait_ge(s_xT, 1)
            w.loaded(pe, "moe")
            for t in range(TT):
                ins = pe.matmul(G1[:, t * E:(t + 1) * E], xT[:, t * P:(t + 1) * P], w["moe_gateT"][:], start=(t == 0), stop=True,
                                skip_group_check=True)
            ins.then_inc(s_lg, 1)

            def hidden(n):
                e, part = divmod(n, 2)
                if n >= 3:
                    pe.wait_ge(s_hh, n - 2)
                for out, name in zip(pair(n), ("moe_w1", "moe_w3")):
                    ins = pe.matmul(out[:, :], w[name][:, e, part, :], xT[:], start=True, stop=True)
                ins.then_inc(s_h, 1)

            def expert_out(e):
                pe.wait_ge(s_a, e + 1)
                if e >= 2:
                    pe.wait_ge(s_ya, e - 1)
                for t in range(TT):
                    ins = pe.matmul(bank[6 + e % 2][:, t * P:(t + 1) * P], a[:, e % 2, t * P:(t + 1) * P], w["moe_w2"][:, e, :],
                                    start=(t == 0), stop=True, skip_group_check=True)
                ins.then_inc(s_y, 1)

            for n in range(3):
                hidden(n)
            pe.wait_ge(s_cw, 2)
            for t in range(TT):
                ins = pe.transpose(G0[0:NE, t * P:(t + 1) * P], cw[:, t, :], w["ident"][:])
            ins.then_inc(s_cwp, 1)
            pe.wait_ge(s_cwT, 1)
            for t in range(TT):
                ins = pe.matmul(G1[:, t * P:(t + 1) * P], cwT[:, t * P:(t + 1) * P], w["moe_b2"][:], start=(t == 0), stop=True,
                                skip_group_check=True)
            ins.then_inc(s_b, 1)
            pe.wait_ge(s_xs, 1)
            for n in range(3, 2 * NE):
                hidden(n)
                if n % 2 and n >= 3:
                    expert_out((n - 3) // 2)
            expert_out(NE - 1)
    st.close()



class Weights(dict):

    def __init__(self):
        super().__init__()
        self.groups = {}

    def loaded(self, eng, group):
        sem, count = self.groups[group]
        eng.wait_ge(sem, count)


def setup(nc, ctx, dram):
    w = Weights()

    def sb(name, shape, dt=F32):
        t = ctx.enter_context(nc.sbuf_tensor(f"w_{name}", shape, dt))
        w[name] = t
        return t

    loads = {
        "const": [("ident", [P, P]), ("mask_q32", [P, P]), ("mask_k32", [P, P]), ("sel32", [P, H]), ("minus_half", [P, 8]), ("ones", [P, P]), ("group32", [P, 32]),
                  ("same_token32", [P, P]), ("other_rows32", [P, P]), ("other_token", [P, 8])],
        "l0x": [("l0x_q", [P, H * 64]), ("l0x_k", [P, H * 64]), ("l0x_v", [P, H * 64]), ("l0x_o", [P, H // 2, D]), ("l0x_bo", [P, D])],
        "ffn": [("ffn_conv", [P, HC, 4])],
        "l1a": [("l1a_qkv", [P, 112]), ("l1a_p", [P, D]), ("l1a_bp", [P, D]), ("alibi_q", [P, SB, H, 6]), ("alibi_k", [P, SB, 6])],
        "l1x": [("l1x_q", [P, H * 64]), ("l1x_k", [P, H * 64]), ("l1x_v", [P, H * 64]), ("l1x_o", [P, 8, D]), ("l1x_bq1", [P, H]),
                ("l1x_bk", [P, H]), ("l1x_bv", [P, H * 64]), ("l1x_bo", [P, D])],
        "moe": [("moe_w1", [P, E + 1, 2, F]), ("moe_w3", [P, E + 1, 2, F]), ("moe_w2", [P, E + 1, D]), ("moe_b1", [P, E + 1, 2]),
                ("moe_b3", [P, E + 1, 2]), ("moe_b2", [E + 1, D]), ("moe_gateT", [P, E]), ("moe_gate_b", [P, E]), ("before", [P, E * E])],
        "l0a": [("l0a_qkv", [P, 3 * D]), ("gamma", [P, D]), ("beta", [P, D]), ("toeplitz", [P, H, TW])],
    }
    todo = []
    for g, items in loads.items():
        sem = ctx.enter_context(nc.semaphore(f"loaded_{g}"))
        for name, shape in items:
            t = sb(name, shape)
            src = dram[name]
            if len(src.shape) == 1:
                src = src.unsqueeze(0).broadcast_to([P, src.shape[0]])
            todo.append((t, src, sem))
        w.groups[g] = (sem, 16 * len(items))
    sb("ident_bf", [P, P], BF16)
    sb("mask_q", [P, P], BF16)
    sb("mask_k", [P, P], BF16)
    sb("sel", [P, H, P], BF16)
    sb("same_token", [P, P], BF16)
    sb("other_token4", [P, 4 * P], BF16)
    sb("sel_group", [P, 32, P], BF16)
    sb("l1x_bq", [P, H])
    sb("ffn_q", [P, 2, HID], BF16)
    sb("ffn_wmean", [P, 2])
    with nc.Block() as block:

        @block.sync
        def _(sp):
            for t, src, sem in todo:
                sp.dma_start(t[:], src).then_inc(sem, 16)

        @block.vector
        def _(dve):
            w.loaded(dve, "const")
            dve.tensor_copy(w["ident_bf"][:], w["ident"][:])
            dve.tensor_copy(w["mask_q"][:], w["mask_q32"][:])
            dve.tensor_copy(w["mask_k"][:], w["mask_k32"][:])
            dve.tensor_copy(w["sel"][:], bcast(w["sel32"][:], H, P))
            dve.tensor_copy(w["same_token"][:], w["same_token32"][:])
            dve.tensor_copy(w["other_token4"][:].rearrange("p (a k) -> p a k", a=4), w["other_rows32"][:].unsqueeze(1).broadcast_to([P, 4, P]))
            dve.tensor_tensor(w["sel_group"][:], bcast(w["group32"][:], 32, P), w["same_token32"][:].unsqueeze(1).broadcast_to([P, 32, P]), ALU.add)
            w.loaded(dve, "l1x")
            dve.tensor_scalar(w["l1x_bq"][:], w["l1x_bq1"][:], 0.125, None, ALU.mult)
    return w


def decoder(nc, dram, out):
    with ExitStack() as ctx:
        x = ctx.enter_context(nc.sbuf_tensor("x", [P, TT, D], F32))
        c = ctx.enter_context(nc.sbuf_tensor("ctx", [P, TT, D], F32))
        v_dram = nc.dram_tensor("l1x_values", (TOK, H * 64), F32, kind="Internal").ap()
        w = setup(nc, ctx, dram)
        weight_levels(nc, w, dram)
        with nc.Fori(0, PASSES) as it:
            rel_attention(nc, w, x, c, dram["x"], dram["ctx_1024"], it)
            cross_attention(nc, w, x, c)
            quantized_ffn(nc, w, x)
            alibi_attention(nc, w, x)
            head_attention(nc, w, x, c, v_dram)
            expert_ffn(nc, w, x)
            store(nc, w, x, out, it)


def store(nc, w, x, out, it):
    st = Stage(nc, "store")
    s_out = st.sem("out_stored")
    st.sem("unused")
    with nc.Block() as block:

        @block.sync
        def _(sp):
            w.loaded(sp, "moe")
            sp.dma_start(out[bass.ts(it, NB)].rearrange("b (c p) d -> p (b c) d", p=P), x[:]).then_inc(s_out, 16)
            sp.wait_ge(s_out, 16)
    st.close()



def _constants(np):
    r = np.arange(P)
    c = {"ident": np.eye(P), "mask_q32": np.where(r[None, :] > r[:, None], -BIG, 0.0),
         "mask_k32": np.where(r[:, None] > r[None, :], -BIG, 0.0), "minus_half": np.full((P, 8), -0.5), "ones": np.ones((P, P))}
    k = np.arange(P)
    c["sel32"] = (k[:, None] % H == np.arange(H)[None, :]) & (k[:, None] < 3 * H)
    c["group32"] = (k[:, None] % 32 == np.arange(32)[None, :]) & (k[:, None] < 96)
    c["same_token32"] = (k[:, None] - 96 == r[None, :] // H)
    c["other_rows32"] = np.where((k[:, None] >= 96) & (k[:, None] < 104) & (k[:, None] - 96 != r[None, :] // H), -BIG, 0.0)
    c["other_token"] = np.where(r[:, None] // H != np.arange(8)[None, :], -BIG, 0.0)
    c["before"] = np.broadcast_to((np.arange(E)[None, :] < np.arange(E)[:, None]).reshape(-1), (P, E * E))
    slopes = (2.0 ** (-8.0 * np.arange(1, H + 1) / H)).astype(np.float32)
    pos = np.arange(S).astype(np.float32).reshape(SB, P).T
    c["alibi_q"] = np.concatenate([np.broadcast_to(_parts(np, slopes), (P, SB, H, 3)), _parts(np, -slopes * pos[:, :, None])], -1)
    c["alibi_k"] = np.stack([pos] * 3 + [np.ones_like(pos)] * 3, -1)
    return {n: np.ascontiguousarray(v, np.float32) for n, v in c.items()}


def _parts(np, v):
    out = []
    for _ in range(3):
        m, e = np.frexp(v)
        h = np.ldexp(np.rint(m * 256.0) / 256.0, e).astype(np.float32)
        out.append(h)
        v = v - h
    return np.stack(out, -1)


def kernel(**inputs):
    import numpy as np
    import concourse.bacc as bacc
    from concourse.bass_utils import run_bass_kernel_spmd as run

    i = {k: np.asarray(v) for k, v in inputs.items()}
    a = {"x": i["x"], "ctx_1024": i["ctx_1024"]}
    a["l0a_qkv"] = np.concatenate([i["L0_attn_Wq"].T, i["L0_attn_Wk"].T, i["L0_attn_Wv"].T], 1)
    a["gamma"], a["beta"] = i["L0_attn_ln_gamma"], i["L0_attn_ln_beta"]
    a["toeplitz"] = i["L0_attn_rel_bias_table"][(np.arange(TW)[None, :] - np.arange(P)[:, None] + P - 1)].transpose(0, 2, 1)
    for n in "qkv":
        a[f"l0x_{n}"] = i[f"L0_xattn_W{n}"]
    a["l0x_o"] = i["L0_xattn_Wo"].reshape(H // 2, P, D).transpose(1, 0, 2)
    a["l0x_bo"] = i["L0_xattn_bo"]
    a["ffn_w1T"] = i["L0_ffn_w1"].T
    a["ffn_w2T"] = i["L0_ffn_w2"].T.reshape(HC, P, D).transpose(1, 0, 2).reshape(P, HID)
    a["ffn_conv"] = np.concatenate([i["L0_ffn_conv_w"][:, 0, :], i["L0_ffn_conv_b"][:, None]], 1).reshape(HC, P, 4).transpose(1, 0, 2)
    a["l1a_qkv"] = np.concatenate([i["L1_attn_Wq"], i["L1_attn_Wk"], i["L1_attn_Wv"]], 1)
    a["l1a_p"], a["l1a_bp"] = i["L1_attn_Wp"], i["L1_attn_bp"]
    for n in "qkv":
        a[f"l1x_{n}"] = i[f"L1_xattn_W{n}"].T
    for n in "qk":
        a[f"l1x_b{n}"] = np.tile(i[f"L1_xattn_b{n}"].reshape(H, 64).T, (2, 1))
    a["l1x_bq1"] = a.pop("l1x_bq")
    a["l1x_bv"], a["l1x_bo"] = i["L1_xattn_bv"], i["L1_xattn_bo"]
    a["l1x_o"] = i["L1_xattn_Wo"].reshape(D, 2, 8, 64).transpose(1, 3, 2, 0).reshape(P, 8, D)

    def experts(name):
        return np.concatenate([i["L1_ffn_" + name], i["L1_ffn_s" + name][None]], 0)

    for n in ("w1", "w3"):
        a["moe_" + n] = experts(n).reshape(E + 1, F, 2, D).transpose(3, 0, 2, 1)
    for n in ("b1", "b3"):
        a["moe_" + n] = experts(n).reshape(E + 1, F, 2).transpose(1, 0, 2)
    a["moe_w2"], a["moe_b2"] = experts("w2").transpose(2, 0, 1), experts("b2")
    a["moe_gateT"], a["moe_gate_b"] = i["L1_ffn_gate_w"].T, i["L1_ffn_gate_b"]
    a.update(_constants(np))
    a = {k: np.ascontiguousarray(v) for k, v in a.items()}

    nc = bacc.Bacc("TRN2", target_bir_lowering=False, num_devices=1)
    dram = {k: nc.dram_tensor(f"in_{k}", v.shape, mybir.dt.from_np(v.dtype), kind="ExternalInput").ap() for k, v in a.items()}
    out = nc.dram_tensor("out_x", (B, S, D), F32, kind="ExternalOutput").ap()
    decoder(nc, dram, out)
    r = run(nc, [{f"in_{k}": v for k, v in a.items()}], core_ids=[0])
    return r.results[0]["out_x"]
```

```python
from contextlib import ExitStack

import concourse.bass as bass
from concourse import mybir
from concourse.alu_op_type import AluOpType as ALU

ACT = mybir.ActivationFunctionType
AX = mybir.AxisListType.X
F32 = mybir.dt.float32
BF16 = mybir.dt.bfloat16
U8 = mybir.dt.uint8
U32 = mybir.dt.uint32

B, S, D = 4, 256, 128
P = 128
NB = 2
PASSES = B // NB
SB = S // P
TT = NB * SB
TOK = NB * S
H = 16
U = NB * H
HID = 512
HC = HID // P
E, F = 8, 128
EPS = 1e-5
BIG = 1e30
EXP_LN = "natural_log_exp_and_others"
MAGIC = 1.5 * 2.0 ** 23
Q4 = 4
EARLY = 4
LAG = 2
TW = S + P


class Stage:

    def __init__(self, nc, name):
        self.nc, self.name, self.ctx, self.sems = nc, name, ExitStack(), []
        self.chained = 0

    def sb(self, name, shape, dt=F32):
        return self.ctx.enter_context(self.nc.sbuf_tensor(f"{self.name}_{name}", shape, dt))

    def psum_banks(self):
        return [self.ctx.enter_context(self.nc.psum_tensor(f"{self.name}_bank{i}", [P, 512], F32)) for i in range(8)]

    def sem(self, name):
        s = self.ctx.enter_context(self.nc.semaphore(f"{self.name}_{name}"))
        self.sems.append(s)
        return s

    def close(self):
        nums = sorted(s.num for s in self.sems)
        while nums:
            n = 1
            while n < len(nums) and nums[n] == nums[0] + n:
                n += 1
            self.nc.vector.sem_clear(range(nums[0], nums[0] + n))
            nums = nums[n:]
        self.nc.all_engine_barrier()
        self.ctx.close()


class Chain:

    def __init__(self, eng, sem):
        self.eng, self.sem, self.n = eng, sem, 0

    def __call__(self, ins):
        self.n += 1
        ins.then_inc(self.sem, 1)
        self.eng.wait_ge(self.sem, self.n)


def bcast(ap, n, width):
    return ap.unsqueeze(2).broadcast_to([ap.shape[0], n, width])



class Norm:

    def __init__(self, st, w, tag=""):
        self.w = w
        self.stats = st.sb(f"bn{tag}", [P, TT, 6])
        self.mv = st.sb(f"mv{tag}", [P, TT, 2])
        self.ve = st.sb(f"ve{tag}", [P, TT])
        self.rstd = st.sb(f"rstd{tag}", [P, TT])
        self.s_var = st.sem(f"var_ready{tag}")
        self.s_rstd = st.sem(f"rstd_ready{tag}")

    def vector_stats(self, dve, link, src):
        for t in range(TT):
            ins = dve.bn_stats(self.stats[:, t, :], src[:, t, :])
            if t == TT - 1:
                link(ins)
            else:
                ins.then_inc(link.sem, 1)
                link.n += 1
        for t in range(TT):
            ins = dve.bn_aggr(self.mv[:, t, :], self.stats[:, t, :])
            if t == TT - 1:
                link(ins)
            else:
                ins.then_inc(link.sem, 1)
                link.n += 1
        dve.tensor_scalar(self.ve[:], self.mv[:, :, 1], EPS, None, ALU.add).then_inc(self.s_var, 1)

    def gpsimd_rstd(self, pool):
        pool.wait_ge(self.s_var, 1)
        pool.tensor_tensor(self.rstd[:], self.ve[:], self.w["minus_half"][:, 0:TT], ALU.pow).then_inc(self.s_rstd, 1)

    def vector_apply(self, dve, out, src, s_done):
        dve.wait_ge(self.s_rstd, 1)
        for t in range(TT):
            dve.tensor_scalar(out[:, t, :], src[:, t, :], self.mv[:, t, 0:1], self.rstd[:, t:t + 1],
                              ALU.subtract, ALU.mult).then_inc(s_done, 1)


def tensor_transpose_tiles(pe, w, bank, src, s_src, s_done):
    for t in range(TT):
        pe.wait_ge(s_src, t + 1)
        ins = pe.transpose(bank[:, t * P:(t + 1) * P], src[:, t, :], w["ident"][:])
    ins.then_inc(s_done, 1)



class Attention:

    def __init__(self, st, w, *, causal, lse, scale, heads_per_out, q, k, values, out_rows, ring, masks=None, extra=False):
        self.st, self.w, self.causal, self.lse, self.scale = st, w, causal, lse, scale
        self.masks, self.ring = masks, ring
        self.HG, self.q, self.k, self.values, self.rows = heads_per_out, q, k, values, out_rows
        self.W = 3 * P if causal else 2 * S
        self.nmax = st.sb("nmax", [P, NB, SB, H])
        self.zsum = st.sb("zsum", [P, NB, SB, H]) if lse else None
        self.lnz = st.sb("lnz", [P, SB, H]) if lse else None
        self.shift = st.sb("shift", [P, SB, H])
        self.rest = st.sb("rest", [P, SB, H])
        self.parts = st.sb("parts", [P, NB, SB, P], BF16)
        self.shiftT = st.sb("shiftT", [P, NB, S], BF16)
        self.expT = st.sb("expT", [P, ring, self.W])
        self.s_s = st.sem("max_scores_ready")
        self.s_mx = st.sem("max_done")
        self.s_lse = st.sem("sum_done")
        self.s_ln = st.sem("log_ready")
        self.s_parts = st.sem("shift_parts_ready")
        self.s_tp = st.sem("shift_transposed")
        self.s_shT = st.sem("shiftT_ready")
        self.s_e = st.sem("exp_scores_ready")
        self.s_p = st.sem("exp_ready")
        self.s_pv = st.sem("exp_used")
        self.s_sum = st.sem("group_summed") if extra else self.s_pv
        self.s_og = st.sem("out_evicted")
        self.s_zero = st.sem("parts_zeroed")

    def tensor_S(self, pe, u, bank):
        b, h = divmod(u, H)
        if u >= 2:
            pe.wait_ge(self.s_lse if self.lse else self.s_mx, u - 1)
        if self.causal:
            pe.matmul(bank[:, 0:P], self.q(b, h, 0, P), self.k(b, h, 0, P), start=True, stop=False, skip_group_check=True)
            pe.matmul(bank[:, P:3 * P], self.q(b, h, P, P), self.k(b, h, 0, S), start=False, stop=False, skip_group_check=True)
            if self.masks:
                ins = pe.matmul(bank[:, 0:3 * P], self.w["ident_bf"][:], self.masks[0][:, b, :], start=False, stop=True, skip_group_check=True)
            else:
                for c in (0, 2 * P):
                    ins = pe.matmul(bank[:, c:c + P], self.w["ident_bf"][:], self.w["mask_q"][:], start=False, stop=True, skip_group_check=True)
        else:
            for c in range(SB):
                ins = pe.matmul(bank[:, c * S:(c + 1) * S], self.q(b, h, c * P, P), self.k(b, h, 0, S),
                                start=(c == 0), stop=True, skip_group_check=True)
        ins.then_inc(self.s_s, 1)

    def tensor_shift(self, pe, b, bank):
        pe.wait_ge(self.s_parts, b + 1)
        if b:
            pe.wait_ge(self.s_shT, b)
        view = bank[:, 0:P].bitcast(BF16)
        for c in range(SB):
            ins = pe.transpose(view[:, c * P:(c + 1) * P], self.parts[:, b, c, :], self.w["ident_bf"][:])
        ins.then_inc(self.s_tp, 1)

    def tensor_E(self, pe, u, bank):
        b, h = divmod(u, H)
        if h == 0:
            pe.wait_ge(self.s_shT, b + 1)
        if u >= 2:
            pe.wait_ge(self.s_p, u - 1)
        sel = self.w["sel"][:, h, :]
        sh = self.shiftT[:, b, :]
        second = P if self.causal else 0
        pe.matmul(bank[:, 0:S], sel, sh, start=True, stop=False, skip_group_check=True)
        pe.matmul(bank[:, S:self.W], sel, sh[:, second:S], start=False, stop=False, skip_group_check=True)
        pe.matmul(bank[:, 0:S], self.k(b, h, 0, P), self.q(b, h, 0, S), start=False, stop=not self.causal, skip_group_check=True)
        ins = pe.matmul(bank[:, S:self.W], self.k(b, h, P, P), self.q(b, h, second, S - second), start=False, stop=not self.causal, skip_group_check=True)
        if self.masks:
            ins = pe.matmul(bank[:, 0:self.W], self.w["ident_bf"][:], self.masks[1][:, b, :], start=False, stop=True, skip_group_check=True)
        elif self.causal:
            for c in (0, S):
                ins = pe.matmul(bank[:, c:c + P], self.w["ident_bf"][:], self.w["mask_k"][:], start=False, stop=True, skip_group_check=True)
        ins.then_inc(self.s_e, 1)

    def tensor_PV(self, pe, g, bank, extra=None):
        pe.wait_ge(self.s_p, self.HG * (g + 1))
        if g >= 2:
            pe.wait_ge(self.s_og, g - 1)
        second = P if self.causal else 0
        units = range(self.HG * g, self.HG * (g + 1))

        def product(u, t0, lhsT, rhs, start, stop):
            r = u % self.HG * self.rows
            return pe.matmul(bank[r:r + self.rows, t0:S], lhsT, rhs, start=start, stop=stop, skip_group_check=True)

        for u in units:
            product(u, 0, self.values(*divmod(u, H), 0), self.expT[:, u % self.ring, 0:S], True, False)
        for u in units:
            ins = product(u, second, self.values(*divmod(u, H), 1), self.expT[:, u % self.ring, S:self.W], False, extra is None)
        ins.then_inc(self.s_pv, 1)
        if extra is not None:
            for c in range(SB):
                for u in units:
                    lhsT, rhs = extra(*divmod(u, H), c)
                    ins = product(u, 0, lhsT, rhs, False, c == 1)
            ins.then_inc(self.s_sum, 1)

    def vector_max(self, dve, u, bank):
        b, h = divmod(u, H)
        dve.wait_ge(self.s_s, u + 1)
        if self.causal:
            dve.tensor_reduce(self.nmax[:, b, 0, h:h + 1], bank[:, 0:P], AX, ALU.max, negate=True)
            dve.tensor_reduce(self.nmax[:, b, 1, h:h + 1], bank[:, P:3 * P], AX, ALU.max, negate=True).then_inc(self.s_mx, 1)
        else:
            dve.tensor_reduce(self.nmax[:, b, :, h], bank[:, :].rearrange("p (c k) -> p c k", c=SB), AX, ALU.max,
                              negate=True).then_inc(self.s_mx, 1)

    def vector_parts(self, dve, link, b):
        dve.wait_ge(self.s_mx, H * (b + 1))
        src = self.nmax[:, b, :, :]
        if self.lse:
            dve.wait_ge(self.s_ln, b + 1)
            link(dve.scalar_tensor_tensor(self.shift[:], src, BIG / 2, src, ALU.is_lt, ALU.mult))
            link(dve.tensor_tensor(self.shift[:], self.shift[:], self.lnz[:], ALU.subtract))
            src = self.shift[:]
        if b == 0:
            dve.wait_ge(self.s_zero, 1)
        hi, mid, lo = (self.parts[:, b, :, i * H:(i + 1) * H] for i in range(3))
        link(dve.tensor_copy(hi, src))
        link(dve.tensor_tensor(self.rest[:], src, hi, ALU.subtract))
        link(dve.tensor_copy(mid, self.rest[:]))
        dve.tensor_tensor(lo, self.rest[:], mid, ALU.subtract).then_inc(self.s_parts, 1)

    def vector_shiftT(self, dve, b, bank):
        dve.wait_ge(self.s_tp, b + 1)
        dve.tensor_copy(self.shiftT[:, b, :], bank[:, 0:P].bitcast(BF16)).then_inc(self.s_shT, 1)

    def scalar_sum(self, act, u, bank):
        b, h = divmod(u, H)
        act.wait_ge(self.s_mx, u + 1)
        act.activation(bank[:, 0:P], bank[:, 0:P], ACT.Exp, bias=self.nmax[:, b, 0, h:h + 1], scale=self.scale,
                       accum_out=self.zsum[:, b, 0, h:h + 1])
        act.activation(bank[:, P:3 * P], bank[:, P:3 * P], ACT.Exp, bias=self.nmax[:, b, 1, h:h + 1], scale=self.scale,
                       accum_out=self.zsum[:, b, 1, h:h + 1]).then_inc(self.s_lse, 1)

    def scalar_log(self, act, b):
        act.wait_ge(self.s_lse, H * (b + 1))
        if b:
            act.wait_ge(self.s_parts, b)
        act.activation(self.lnz[:], self.zsum[:, b, :, :], ACT.Ln).then_inc(self.s_ln, 1)

    def scalar_exp(self, act, u, bank):
        act.wait_ge(self.s_e, u + 1)
        if u >= self.ring:
            act.wait_ge(self.s_pv, (u - self.ring) // self.HG + 1)
        act.activation(self.expT[:, u % self.ring, :], bank[:, 0:self.W], ACT.Exp, scale=self.scale).then_inc(self.s_p, 1)


def ahead(n, units, early):
    b, h = divmod(n, units)
    if b + 1 >= NB:
        return range(0)
    done, now = (min(units, k * units // (units - early)) for k in (h, h + 1))
    return range(units * (b + 1) + done, units * (b + 1) + now)


def split_columns(part_of):
    runs = []
    for i, x in enumerate(part_of):
        if runs and runs[-1][0] == x and runs[-1][1] + runs[-1][2] == i:
            runs[-1][2] += 1
        else:
            runs.append([x, i, 1])
    return runs


Q_PARTS = (0, 0, 0, 1, 1, 2)
K_PARTS = (0, 1, 2, 0, 1, 0)


def rel_attention(nc, w, x, ctx, x_dram, ctx_dram, it):
    st = Stage(nc, "l0a")
    HD = D // H
    SW = 64
    xn = st.sb("xn", [P, TT, D])
    xT = st.sb("xT", [P, TOK])
    sp_ = st.sb("split", [P, 2, 3, 2 * D], BF16)
    sr = st.sb("rest_qk", [P, 2, 2 * D])
    stack = st.sb("stack", [P, 2, 2, H, SW], BF16)
    qkT = st.sb("qkT", [P, H // 2, 2, TOK], BF16)
    vals = st.sb("vals", [P, TT, H, 64])
    xb = st.sb("x_beta", [P, TT, D])
    y = st.sb("y", [P, TT, D])
    osb = st.sb("o", [P, 2, S])
    rz = st.sb("rz", [P, 2 * Q4])
    tmp = st.sb("tmp", [P, 2 * Q4, HD])
    norm, norm2 = Norm(st, w), Norm(st, w, "2")
    s_chain = st.sem("dve_chain")
    s_x, s_ctx = st.sem("x_loaded"), st.sem("ctx_loaded")
    s_xn = st.sem("xn_ready")
    s_xTp = st.sem("x_transposed")
    s_xT = st.sem("xT_ready")
    s_qkv = st.sem("qkv_ready")
    s_split = st.sem("parts_ready")
    s_v = st.sem("values_ready")
    s_stq = st.sem("q_stack_ready")
    s_stk = st.sem("k_stack_ready")
    s_init = st.sem("buffers_set")
    s_stT = st.sem("stack_transposed")
    s_qkT = st.sem("qkT_ready")
    s_ob = st.sem("o_transposed")
    s_fin = st.sem("o_finished")
    s_y = st.sem("y_normalized")
    s_xb = st.sem("x_beta_ready")
    bank = st.psum_banks()
    SBK, EBK, OBK, G0, G1 = bank[0:2], bank[2:4], bank[4:6], bank[6], bank[7]

    def at(part, b, h, t0, n):
        r = SW * (h % 2)
        return qkT[r:r + SW, h // 2, part, b * S + t0:b * S + t0 + n]

    a = Attention(st, w, causal=False, lse=False, scale=float(D) ** -0.5, heads_per_out=Q4,
                  q=lambda b, h, t0, n: at(0, b, h, t0, n), k=lambda b, h, t0, n: at(1, b, h, t0, n),
                  values=lambda b, h, c: vals[:, b * SB + c, h, 0:32], out_rows=32,
                  ring=8, extra=True)

    def bias_term(b, h, c):
        return vals[:, b * SB + c, h, 32:64], w["toeplitz"][:, h, (1 - c) * P:(1 - c) * P + S]

    GROUPS = U // Q4
    def copy_stack(dve, t):
        for i in range(4):
            n = 4 * t + i
            dve.wait_ge(s_stT, n + 1)
            dve.tensor_copy(qkT[:, 2 * i:2 * i + 2, :, t * P:(t + 1) * P],
                            bank[6 + n % 2][:, 0:256].bitcast(BF16).rearrange("p (a q k) -> p a q k", a=2, q=2)
                            ).then_inc(s_qkT, 1)

    with nc.Block() as block:

        @block.gpsimd
        def _(pool):
            pool.wait_ge(s_x, 16)
            w.loaded(pool, "l0a")
            pool.memset(stack[:, :, :, :, 6 * HD:SW], 0.0).then_inc(s_init, 1)
            pool.memset(a.parts[:], 0.0).then_inc(a.s_zero, 1)
            norm.gpsimd_rstd(pool)
            pool.wait_ge(s_init, 3)
            pool.tensor_tensor(xb[:], x[:], w["beta"][:].unsqueeze(1).broadcast_to([P, TT, D]), ALU.add).then_inc(s_xb, 1)
            for t in range(TT):
                pool.wait_ge(s_split, t + 1)
                if t >= 2:
                    pool.wait_ge(s_stT, 4 * (t - 1))
                for part, i, n in split_columns(Q_PARTS):
                    out = stack[:, t % 2, 0, :, i * HD:(i + n) * HD].rearrange("p h (n d) -> p h n d", n=n)
                    src = sp_[:, t % 2, part, 0:D].rearrange("p (h d) -> p h d", h=H).unsqueeze(2).broadcast_to([P, H, n, HD])
                    ins = pool.tensor_copy(out, src)
                ins.then_inc(s_stq, 1)
            norm2.gpsimd_rstd(pool)

        @block.scalar
        def _(act):
            act.preload_act_table_set(EXP_LN)
            act.dma_start(x[:], x_dram[bass.ts(it, NB)].rearrange("b (c p) d -> p (b c) d", p=P)).then_inc(s_x, 16)
            act.dma_start(ctx[:], ctx_dram[bass.ts(it, NB)].rearrange("b (c p) d -> p (b c) d", p=P)).then_inc(s_ctx, 16)
            act.wait_ge(s_xTp, 1)
            act.activation(xT[:], G0[:, :], ACT.Copy).then_inc(s_xT, 1)
            act.wait_ge(s_init, 3)
            for t in range(TT):
                act.wait_ge(s_split, t + 1)
                v = EBK[t % 2][:, 2 * D:3 * D].rearrange("p (h d) -> p h d", h=H)
                act.activation(vals[:, t, :, 0:HD], v, ACT.Copy)
                act.activation(vals[:, t, :, 48:48 + HD], v, ACT.Copy).then_inc(s_v, 1)
                if t >= 2:
                    act.wait_ge(s_stT, 4 * (t - 1))
                for part, i, n in split_columns(K_PARTS):
                    ins = act.activation(stack[:, t % 2, 1, :, i * HD:(i + n) * HD],
                                         sp_[:, t % 2, part, D:2 * D].rearrange("p (h d) -> p h d", h=H), ACT.Copy)
                ins.then_inc(s_stk, 1)
            for n in range(U + 2):
                if n < U:
                    a.scalar_exp(act, n, EBK[n % 2])
                if n % Q4 == 1 and n > 1:
                    g = n // Q4 - 1
                    act.wait_ge(a.s_sum, g + 1)
                    if g >= 2:
                        act.wait_ge(s_ob, g - 1)
                    act.activation(osb[:, g % 2, :], OBK[g % 2][:, 0:S], ACT.Copy).then_inc(a.s_og, 1)
            act.wait_ge(s_ctx, 16)

        @block.vector
        def _(dve):
            link = Chain(dve, s_chain)
            dve.wait_ge(s_x, 16)
            norm.vector_stats(dve, link, x)
            w.loaded(dve, "l0a")
            dve.memset(vals[:], 0.0).then_inc(s_init, 1)
            dve.wait_ge(s_init, 2)
            dve.memset(vals[:, :, :, HD:HD + 1], 1.0).then_inc(s_init, 1)
            norm.vector_apply(dve, xn, x, s_xn)
            for t in range(TT):
                dve.wait_ge(s_qkv, t + 1)
                if t >= 2:
                    dve.wait_ge(s_stq, t - 1)
                    dve.wait_ge(s_stk, t - 1)
                qk = EBK[t % 2][:, 0:2 * D]
                hi, mid, lo = (sp_[:, t % 2, i, :] for i in range(3))
                link(dve.tensor_copy(hi, qk))
                link(dve.tensor_tensor(sr[:, t % 2, :], qk, hi, ALU.subtract))
                link(dve.tensor_copy(mid, sr[:, t % 2, :]))
                dve.tensor_tensor(lo, sr[:, t % 2, :], mid, ALU.subtract).then_inc(s_split, 1)
                if t:
                    copy_stack(dve, t - 1)
            copy_stack(dve, TT - 1)
            for u in range(H):
                a.vector_max(dve, u, SBK[u % 2])
            a.vector_parts(dve, link, 0)
            a.vector_shiftT(dve, 0, G0)
            for n in range(U + LAG + 1):
                b, h = divmod(n, H)
                if h == H - 1 and b + 1 < NB:
                    a.vector_shiftT(dve, b + 1, G0)
                for u in ahead(n, H, EARLY):
                    a.vector_max(dve, u, SBK[u % 2])
                if h == H - 1 - EARLY and b + 1 < NB:
                    a.vector_parts(dve, link, b + 1)
                if n >= Q4 + LAG and (n - LAG) % Q4 == 0:
                    g = (n - LAG) // Q4 - 1
                    b2, hg = divmod(g, H // Q4)
                    dve.wait_ge(s_ob, g + 1)
                    if g:
                        dve.wait_ge(s_fin, g)
                    o = G1[:, 0:SB * P].rearrange("p (c r) -> p c r", r=32)
                    link(dve.reciprocal(rz[:], o[:, :, HD]))
                    link(dve.tensor_tensor(tmp[:], o[:, :, 0:HD], bcast(rz[:], 2 * Q4, HD), ALU.mult))
                    dst = y[:, b2 * SB:(b2 + 1) * SB, hg * 32:(hg + 1) * 32].rearrange("p c (j d) -> p c j d", d=HD)
                    for c in range(SB):
                        ins = dve.tensor_tensor(dst[:, c], o[:, c * Q4:(c + 1) * Q4, 16:16 + HD],
                                                tmp[:, c * Q4:(c + 1) * Q4, :], ALU.add)
                    ins.then_inc(s_fin, 1)
            dve.wait_ge(s_fin, GROUPS)
            norm2.vector_stats(dve, link, y)
            norm2.vector_apply(dve, xn, y, s_y)
            dve.wait_ge(s_y, TT)
            dve.wait_ge(s_xb, 1)
            link(dve.tensor_tensor(y[:], xn[:], w["gamma"][:].unsqueeze(1).broadcast_to([P, TT, D]), ALU.mult))
            link(dve.tensor_tensor(x[:], y[:], xb[:], ALU.add))

        @block.tensor
        def _(pe):
            tensor_transpose_tiles(pe, w, G0, xn, s_xn, s_xTp)
            w.loaded(pe, "l0a")
            pe.wait_ge(s_xT, 1)
            for t in range(TT + 1):
                if t < TT:
                    if t >= 2:
                        pe.wait_ge(s_split, t - 1)
                        pe.wait_ge(s_v, t - 1)
                    pe.matmul(EBK[t % 2][:, 0:3 * D], xT[:, t * P:(t + 1) * P], w["l0a_qkv"][:], start=True, stop=True).then_inc(s_qkv, 1)
                if t:
                    pe.wait_ge(s_stq, t)
                    pe.wait_ge(s_stk, t)
                    for i in range(4):
                        n = 4 * (t - 1) + i
                        if n >= 2:
                            pe.wait_ge(s_qkT, n - 1)
                        out = bank[6 + n % 2][:, 0:256].bitcast(BF16)
                        for hp in (2 * i, 2 * i + 1):
                            for part in range(2):
                                c = ((hp % 2) * 2 + part) * P
                                ins = pe.transpose(out[:, c:c + P], stack[:, (t - 1) % 2, part, 2 * hp:2 * hp + 2, :], w["ident_bf"][:])
                        ins.then_inc(s_stT, 1)
            pe.wait_ge(s_qkT, 4 * TT)
            w.loaded(pe, "toeplitz")
            for u in range(H):
                a.tensor_S(pe, u, SBK[u % 2])
            a.tensor_shift(pe, 0, G0)
            for n in range(U + LAG + 1):
                b, h = divmod(n, H)
                if h == H - 1 and b + 1 < NB:
                    a.tensor_shift(pe, b + 1, G0)
                if n < U:
                    a.tensor_E(pe, n, EBK[n % 2])
                for u in ahead(n, H, EARLY):
                    a.tensor_S(pe, u, SBK[u % 2])
                if n >= Q4 and n % Q4 == 0:
                    a.tensor_PV(pe, n // Q4 - 1, OBK[(n // Q4 - 1) % 2], extra=bias_term)
                if n >= Q4 + LAG and (n - LAG) % Q4 == 0:
                    g = (n - LAG) // Q4 - 1
                    pe.wait_ge(a.s_og, g + 1)
                    if g:
                        pe.wait_ge(s_fin, g)
                    for c in range(SB):
                        ins = pe.transpose(G1[:, c * P:(c + 1) * P], osb[:, g % 2, c * P:(c + 1) * P], w["ident"][:])
                    ins.then_inc(s_ob, 1)
    st.close()

def cross_attention(nc, w, x, ctx, dram, it):
    st = Stage(nc, "l0x")
    HD = 64
    HP = H // 2
    xn = st.sb("xn", [P, TT, D])
    xT = st.sb("xT", [P, 2, TOK])
    qT = st.sb("qT", [P, HP, TOK])
    kT = st.sb("kT", [P, HP, TOK])
    vals = st.sb("vals", [P, TT, H * HD])
    oT = st.sb("oT", [P, HP, TOK])
    xb = st.sb("x_bias", [P, TT, D])
    pad8 = st.sb("padded_bytes", [P, NB, S // 4], U32)
    padk8 = st.sb("padded_key_bytes", [P, 1], U32)
    pad = st.sb("padded", [P, NB, S])
    padk = st.sb("padded_keys", [P, NB, SB])
    mask_q = st.sb("mask_q", [P, NB, 3 * P], BF16)
    mask_k = st.sb("mask_k", [P, NB, 3 * P], BF16)
    csum = st.sb("ctx_sum", [P, NB])
    csumB = st.sb("ctx_sum_by_token", [P, NB, P])
    closed = st.sb("no_open_key", [P, NB, SB])
    norm = Norm(st, w)
    s_chain = st.sem("dve_chain")
    s_xn = st.sem("xn_ready")
    s_tp = st.sem("transposed")
    s_xT = st.sem("xT_ready")
    s_xb = st.sem("x_bias_ready")
    s_pr = st.sem("projected")
    s_pa = st.sem("projection_by_scalar")
    s_pv = st.sem("projection_by_vector")
    s_wo = st.sem("product_ready")
    s_pad = st.sem("padding_loaded")
    s_neg = st.sem("padding_scaled")
    s_mask = st.sem("masks_ready")
    s_cs = st.sem("ctx_sum_ready")
    s_cb = st.sem("ctx_sum_spread")
    s_mean = st.sem("mean_product_ready")
    s_x = st.sem("x_updated")
    bank = st.psum_banks()
    SBK, EBK, OBK, G0, G1 = bank[0:2], bank[2:4], bank[4:6], bank[6], bank[7]

    def at(buf, b, h, t0, n):
        r = HD * (h % 2)
        return buf[r:r + HD, h // 2, b * S + t0:b * S + t0 + n]

    a = Attention(st, w, causal=True, lse=True, scale=1.0, heads_per_out=2,
                  q=lambda b, h, t0, n: at(qT, b, h, t0, n), k=lambda b, h, t0, n: at(kT, b, h, t0, n),
                  values=lambda b, h, c: vals[:, b * SB + c, h * HD:(h + 1) * HD], out_rows=HD, ring=6,
                  masks=(mask_q, mask_k))

    v_jobs = [("v", t, i) for t in range(TT) for i in range(2)]
    jobs = v_jobs[:4] + [(kind, c, 0) for c in range(HP) for kind in "kq"] + v_jobs[4:]
    FIRST = 4
    plan = [("project", n) for n in range(FIRST + 2)]
    for c in range(HP):
        if c + 1 < HP:
            plan += [("project", FIRST + 2 * c + 2), ("project", FIRST + 2 * c + 3)]
        plan += [("maximum", 2 * c), ("maximum", 2 * c + 1)]
    plan += [("project", n) for n in range(FIRST + 2 * HP, len(jobs))]
    JB = bank[2:6]
    GROUPS = U // 2

    def destination(job):
        kind, c, i = job
        if kind == "k":
            return kT[:, c, :], 1.0
        if kind == "q":
            return qT[:, c, :], float(HD) ** -0.5
        return vals[:, c, i * 512:(i + 1) * 512], 1.0

    with nc.Block() as block:

        @block.sync
        def _(sp):
            sp.dma_start(pad8[:], dram["padded"][bass.ts(it, NB)].unsqueeze(0).broadcast_to([P, NB, S // 4])).then_inc(s_pad, 16)
            sp.dma_start(padk8[:], dram["padded_keys"][bass.ts(it, 1)].rearrange("o p c -> (o p) c")).then_inc(s_pad, 16)
            sp.wait_ge(s_pad, 32)

        @block.gpsimd
        def _(pool):
            pool.memset(a.parts[:], 0.0).then_inc(a.s_zero, 1)
            norm.gpsimd_rstd(pool)
            w.loaded(pool, "l0x")
            pool.tensor_tensor(xb[:], x[:], w["l0x_bo"][:].unsqueeze(1).broadcast_to([P, TT, D]), ALU.add).then_inc(s_xb, 1)
            pool.wait_ge(s_pad, 32)
            pool.tensor_scalar(pad[:], pad8[:].bitcast(U8), -BIG, None, ALU.mult).then_inc(s_neg, 1)
            pool.tensor_scalar(padk[:].rearrange("p b c -> p (b c)"), padk8[:].bitcast(U8), -BIG, None, ALU.mult).then_inc(s_neg, 1)
            pool.wait_ge(s_neg, 2)
            for b in range(NB):
                pool.tensor_tensor(mask_q[:, b, 0:P], w["mask_q32"][:], pad[:, b, 0:P], ALU.add)
                pool.tensor_copy(mask_q[:, b, P:2 * P], pad[:, b, 0:P])
                pool.tensor_tensor(mask_q[:, b, 2 * P:3 * P], w["mask_q32"][:], pad[:, b, P:S], ALU.add)
                pool.tensor_tensor(mask_k[:, b, 0:P], w["mask_k32"][:], padk[:, b, 0:1].broadcast_to([P, P]), ALU.add)
                pool.tensor_copy(mask_k[:, b, P:2 * P], padk[:, b, 0:1].broadcast_to([P, P]))
                ins = pool.tensor_tensor(mask_k[:, b, 2 * P:3 * P], w["mask_k32"][:], padk[:, b, 1:2].broadcast_to([P, P]), ALU.add)
            ins.then_inc(s_mask, 1)
            pool.wait_ge(s_cs, 1)
            pool.tensor_copy(csumB[:], bcast(csum[:], NB, P)).then_inc(s_cb, 1)

        @block.scalar
        def _(act):
            act.wait_ge(s_tp, 1)
            act.activation(xT[:, 1, :], G0[:, :], ACT.Copy).then_inc(s_xT, 1)
            act.preload_act_table_set(EXP_LN)
            for what, n in plan:
                if what == "maximum":
                    a.scalar_sum(act, n, SBK[n % 2])
                elif n % 2 == 0:
                    out, scale = destination(jobs[n])
                    act.wait_ge(s_pr, n + 1)
                    act.activation(out, JB[n % 4][:, :], ACT.Copy, scale=scale).then_inc(s_pa, 1)
                    if n == FIRST:
                        act.wait_ge(s_tp, 2)
                        act.activation(xT[:, 0, :], G1[:, :], ACT.Copy).then_inc(s_xT, 1)
            a.scalar_log(act, 0)
            for n in range(U + 2):
                b, h = divmod(n, H)
                if n < U:
                    a.scalar_exp(act, n, EBK[n % 2])
                for u in ahead(n, H, EARLY):
                    a.scalar_sum(act, u, SBK[u % 2])
                if h == H - 1 - EARLY and b + 1 < NB:
                    a.scalar_log(act, b + 1)
                if n % 2 == 1 and n > 1:
                    g = n // 2 - 1
                    b2, c = divmod(g, HP)
                    act.wait_ge(a.s_pv, g + 1)
                    act.activation(oT[:, c, b2 * S:(b2 + 1) * S], OBK[g % 2][:, 0:S], ACT.Copy).then_inc(a.s_og, 1)

        @block.vector
        def _(dve):
            link = Chain(dve, s_chain)
            norm.vector_stats(dve, link, x)
            norm.vector_apply(dve, xn, x, s_xn)
            dve.wait_ge(s_xT, 1)
            dve.tensor_reduce(csum[:], xT[:, 1, :].rearrange("p (b s) -> p b s", b=NB), AX, ALU.add).then_inc(s_cs, 1)
            for what, n in plan:
                if what == "maximum":
                    a.vector_max(dve, n, SBK[n % 2])
                elif n % 2:
                    out, scale = destination(jobs[n])
                    dve.wait_ge(s_pr, n + 1)
                    if scale == 1.0:
                        ins = dve.tensor_copy(out, JB[n % 4][:, :])
                    else:
                        ins = dve.tensor_scalar(out, JB[n % 4][:, :], scale, None, ALU.mult)
                    ins.then_inc(s_pv, 1)
            a.vector_parts(dve, link, 0)
            a.vector_shiftT(dve, 0, G0)
            for n in range(U + 1):
                b, h = divmod(n, H)
                if h == H - 1 and b + 1 < NB:
                    a.vector_shiftT(dve, b + 1, G0)
                for u in ahead(n, H, EARLY):
                    a.vector_max(dve, u, SBK[u % 2])
                if h == H - 1 - EARLY and b + 1 < NB:
                    a.vector_parts(dve, link, b + 1)
            link(dve.tensor_scalar(closed[:], a.nmax[:, :, :, 0], BIG / 2, None, ALU.is_ge))
            dve.wait_ge(s_xb, 1)
            dve.wait_ge(s_mean, 1)
            for t in range(TT):
                b, c = divmod(t, SB)
                ins = dve.scalar_tensor_tensor(xb[:, t, :], G1[:, b * D:(b + 1) * D], closed[:, b, c:c + 1], xb[:, t, :], ALU.mult, ALU.add)
            link(ins)
            for t in range(TT):
                dve.wait_ge(s_wo, t + 1)
                dve.tensor_tensor(x[:, t, :], bank[t % 4][:, 0:D], xb[:, t, :], ALU.add).then_inc(s_x, 1)

        @block.tensor
        def _(pe):
            w.loaded(pe, "l0x_vo")
            w.loaded(pe, "l0x")
            for t in range(TT):
                ins = pe.transpose(G0[:, t * P:(t + 1) * P], ctx[:, t, :], w["ident"][:])
            ins.then_inc(s_tp, 1)
            pe.wait_ge(s_xT, 1)
            for what, n in plan:
                if what == "maximum":
                    if n == 0:
                        pe.wait_ge(s_mask, 1)
                    if n % 2 == 0:
                        job = FIRST + n
                        pe.wait_ge(s_pa, job // 2 + 1)
                        pe.wait_ge(s_pv, job // 2 + 1)
                    a.tensor_S(pe, n, SBK[n % 2])
                    continue
                kind, c, i = jobs[n]
                if n == FIRST + 1:
                    tensor_transpose_tiles(pe, w, G1, xn, s_xn, s_tp)
                    pe.wait_ge(s_xT, 2)
                if n >= 4:
                    pe.wait_ge(s_pv if n % 2 else s_pa, n // 2 - 1)
                out = JB[n % 4][:, :]
                if kind == "v":
                    ins = pe.matmul(out, xT[:, 1, c * P:(c + 1) * P], w["l0x_v"][:, i * 512:(i + 1) * 512], start=True, stop=True)
                else:
                    ins = pe.matmul(out, w[f"l0x_{kind}"][:, c * P:(c + 1) * P], xT[:, int(kind == "k"), :], start=True, stop=True)
                ins.then_inc(s_pr, 1)
            pe.wait_ge(s_cb, 1)
            for b in range(NB):
                ins = pe.matmul(G1[:, b * D:(b + 1) * D], csumB[:, b, :], w["l0x_vo"][:], start=(b == 0), stop=True, skip_group_check=True)
            ins.then_inc(s_mean, 1)
            a.tensor_shift(pe, 0, G0)
            pe.wait_ge(s_pa, len(jobs) // 2)
            pe.wait_ge(s_pv, len(jobs) // 2)
            for n in range(U + 1):
                b, h = divmod(n, H)
                if h == H - 1 and b + 1 < NB:
                    a.tensor_shift(pe, b + 1, G0)
                if n < U:
                    a.tensor_E(pe, n, EBK[n % 2])
                for u in ahead(n, H, EARLY):
                    a.tensor_S(pe, u, SBK[u % 2])
                if n >= 2 and n % 2 == 0:
                    a.tensor_PV(pe, n // 2 - 1, OBK[(n // 2 - 1) % 2])
            for t in range(TT):
                pe.wait_ge(a.s_og, HP * (t // SB + 1))
                pe.wait_ge(a.s_p, U)
                for c in range(HP):
                    ins = pe.matmul(bank[t % 4][:, 0:D], oT[:, c, t * P:(t + 1) * P], w["l0x_o"][:, c, :],
                                    start=(c == 0), stop=(c == HP - 1))
                ins.then_inc(s_wo, 1)
    st.close()


def weight_levels(nc, w, dram):
    st = Stage(nc, "wq")
    raw = st.sb("raw", [P, 2, HID])
    psum_bank = st.psum_banks()
    part = st.sb("part", [P, 2])
    scale = st.sb("scale", [P, 2])
    r = st.sb("r", [P, 2, HID])
    HP = H // 2
    vT = st.sb("vT", [P, HP, P])
    s_raw, s_part, s_sum, s_chain, s_done = (st.sem(n) for n in ("raw_loaded", "part_ready", "sum_ready", "dve_chain", "done"))
    s_vTp, s_vT, s_vo = (st.sem(n) for n in ("v_transposed", "vT_ready", "product_ready"))
    with nc.Block() as block:

        @block.vector
        def _(dve):
            link = Chain(dve, s_chain)
            dve.wait_ge(s_raw, 32)
            dve.tensor_reduce(part[:], raw[:], AX, ALU.add, apply_absolute_value=True).then_inc(s_part, 1)
            dve.wait_ge(s_sum, 1)
            mean = w["ffn_wmean"]
            link(dve.tensor_scalar(mean[:], psum_bank[0][:, 0:2], 1.0 / (HID * D), EPS, ALU.mult, ALU.max))
            link(dve.reciprocal(scale[:], mean[:]))
            for i in range(2):
                link(dve.tensor_scalar(r[:, i, :], raw[:, i, :], scale[:, i:i + 1], MAGIC, ALU.mult, ALU.add))
            link(dve.tensor_scalar(r[:], r[:], MAGIC, 1.0, ALU.subtract, ALU.min))
            dve.tensor_scalar(w["ffn_q"][:], r[:], -1.0, None, ALU.max).then_inc(s_done, 1)

        @block.tensor
        def _(pe):
            w.loaded(pe, "const")
            pe.wait_ge(s_part, 1)
            pe.matmul(psum_bank[0][:, 0:2], w["ones"][:], part[:], start=True, stop=True).then_inc(s_sum, 1)
            w.loaded(pe, "l0x_vo")
            for c in range(HP):
                ins = pe.transpose(psum_bank[1 + c // 4][:, c % 4 * P:(c % 4 + 1) * P], w["l0x_v"][:, c * P:(c + 1) * P], w["ident"][:])
            ins.then_inc(s_vTp, 1)
            pe.wait_ge(s_vT, 1)
            for c in range(HP):
                ins = pe.matmul(psum_bank[3][:, 0:D], vT[:, c, :], w["l0x_o"][:, c, :], start=(c == 0), stop=(c == HP - 1))
            ins.then_inc(s_vo, 1)

        @block.scalar
        def _(act):
            act.dma_start(raw[:, 0, :], dram["ffn_w1T"]).then_inc(s_raw, 16)
            act.dma_start(raw[:, 1, :], dram["ffn_w2T"]).then_inc(s_raw, 16)
            act.wait_ge(s_vTp, 1)
            for i in range(2):
                ins = act.activation(vT[:, 4 * i:4 * i + 4, :], psum_bank[1 + i][:, :].rearrange("p (c d) -> p c d", c=4), ACT.Copy)
            ins.then_inc(s_vT, 1)
            act.wait_ge(s_vo, 1)
            act.activation(w["l0x_vo"][:], psum_bank[3][:, 0:D], ACT.Copy, scale=1.0 / S)
    st.close()


def quantized_ffn(nc, w, x):
    st = Stage(nc, "ffn")
    xn = st.sb("xn", [P, TT, D])
    r = st.sb("r", [P, TT, HID])
    xq = st.sb("xq", [P, TT, D], BF16)
    xqT = st.sb("xqT", [P, TOK], BF16)
    amax = st.sb("amax", [P, 2, TT])
    inv = st.sb("inv", [P, 2, TT])
    scale = st.sb("scale", [P, 2, TT])
    dg = st.sb("diag", [P, TT, P])
    rowinv = st.sb("rowinv", [P, TOK])
    hp = st.sb("h", [P, HC, NB, S + 2])
    y = st.sb("conv", [P, HC, TOK])
    q2 = st.sb("q2", [P, TT, HID], BF16)
    q2T = st.sb("q2T", [P, HC, TOK], BF16)
    norm = Norm(st, w)
    names = ("dve_chain", "xn_ready", "diag_ready", "rowsum_ready", "rowinv_ready", "xq_ready", "xq_transposed", "xqT_ready",
             "hidden_ready", "hidden_scaled", "conv_ready", "act_ready", "act_transposed", "q2_ready", "q2_transposed", "q2T_ready",
             "product_ready", "x_updated", "inv_ready", "pads_zero", "act_read")
    (s_chain, s_xn, s_dg, s_rs, s_ri, s_xq, s_xqt, s_xqT, s_h, s_hs, s_cv, s_ac, s_act, s_q2, s_q2t, s_q2T,
     s_pr, s_x, s_inv, s_pad, s_rd) = (st.sem(n) for n in names)
    bank = st.psum_banks()

    def tokens(ap):
        return ap.rearrange("p (b s) -> p b s", b=NB)

    with nc.Block() as block:

        @block.gpsimd
        def _(pool):
            norm.gpsimd_rstd(pool)
            pool.memset(hp[:, :, :, 0:1], 0.0).then_inc(s_pad, 1)
            pool.memset(hp[:, :, :, S + 1:S + 2], 0.0).then_inc(s_pad, 1)
            pool.wait_ge(s_inv, 1)
            for t in range(TT):
                ins = pool.tensor_tensor(dg[:, t, :], w["ident"][:], inv[:, 0, t:t + 1].broadcast_to([P, P]), ALU.mult)
            ins.then_inc(s_dg, 1)

        @block.scalar
        def _(act):
            act.wait_ge(s_rs, 1)
            act.activation(rowinv[:], bank[0][:, :], ACT.Copy).then_inc(s_ri, 1)
            for c in range(HC):
                act.wait_ge(s_cv, c + 1)
                act.activation(y[:, c, :], y[:, c, :], ACT.Silu).then_inc(s_ac, 1)
            for c in range(HC):
                act.wait_ge(s_q2t, c + 1)
                act.activation(q2T[:, c, :], bank[c][:, 0:TOK // 2].bitcast(BF16), ACT.Copy).then_inc(s_q2T, 1)

        @block.vector
        def _(dve):
            link = Chain(dve, s_chain)

            def levels(i, t0, t1, src_of, out, width, s_done):
                a, n, s = amax[:, i, t0:t1], inv[:, i, t0:t1], scale[:, i, t0:t1]
                link(dve.tensor_scalar(a, a, EPS, None, ALU.max))
                link(dve.tensor_scalar(n, a, 1.0 / 127.0, None, ALU.mult))
                link(dve.reciprocal(s, a))
                link(dve.tensor_scalar(s, s, 127.0, None, ALU.mult))
                for t in range(t0, t1):
                    ins = dve.tensor_scalar(r[:, t, 0:width], src_of(t), scale[:, i, t:t + 1], 127.0, ALU.mult, ALU.min)
                    if i:
                        ins.then_inc(s_rd, 1)
                        dve.wait_ge(s_rd, t + 1)
                    else:
                        link(ins)
                link(dve.tensor_scalar(r[:, t0:t1, 0:width], r[:, t0:t1, 0:width], -128.0, MAGIC, ALU.max, ALU.add))
                dve.tensor_scalar(out, r[:, t0:t1, 0:width], MAGIC, None, ALU.subtract).then_inc(s_done, 1)

            norm.vector_stats(dve, link, x)
            norm.vector_apply(dve, xn, x, s_xn)
            dve.wait_ge(s_xn, TT)
            link(dve.tensor_reduce(amax[:, 0, :], xn[:], AX, ALU.max, apply_absolute_value=True))
            levels(0, 0, TT, lambda t: xn[:, t, :], xq[:], D, s_xq)
            dve.wait_ge(s_xq, 1)
            link(dve.tensor_scalar(inv[:, 0, :], inv[:, 0, :], w["ffn_wmean"][:, 0:1], None, ALU.mult))
            dve.tensor_copy(scale[:, 0, :], inv[:, 0, :]).then_inc(s_inv, 1)
            dve.wait_ge(s_xqt, 1)
            dve.tensor_copy(xqT[:], bank[1][:, 0:TOK // 2].bitcast(BF16)).then_inc(s_xqT, 1)
            dve.wait_ge(s_ri, 1)
            dve.wait_ge(s_pad, 2)
            w.loaded(dve, "ffn")
            cw = w["ffn_conv"]
            for c in range(HC):
                dve.wait_ge(s_h, c + 1)
                link(dve.tensor_tensor(hp[:, c, :, 1:S + 1], tokens(bank[2 + c][:, :]), tokens(rowinv[:]), ALU.mult))
                v = tokens(y[:, c, :])
                link(dve.tensor_scalar(v, hp[:, c, :, 1:S + 1], cw[:, c, 1:2], cw[:, c, 3:4], ALU.mult, ALU.add))
                link(dve.scalar_tensor_tensor(v, hp[:, c, :, 0:S], cw[:, c, 0:1], v, ALU.mult, ALU.add))
                dve.scalar_tensor_tensor(v, hp[:, c, :, 2:S + 2], cw[:, c, 2:3], v, ALU.mult, ALU.add).then_inc(s_cv, 1)
            for t in range(TT):
                dve.wait_ge(s_act, t + 1)
                link(dve.tensor_reduce(amax[:, 1, t:t + 1], bank[4 + t][:, :], AX, ALU.max, apply_absolute_value=True))
                levels(1, t, t + 1, lambda t: bank[4 + t][:, :], q2[:, t, :], HID, s_q2)
            dve.wait_ge(s_q2, TT)
            link(dve.tensor_scalar(inv[:, 1, :], inv[:, 1, :], w["ffn_wmean"][:, 1:2], None, ALU.mult))
            for t in range(TT):
                dve.wait_ge(s_pr, t + 1)
                dve.scalar_tensor_tensor(x[:, t, :], bank[4 + t][:, 0:D], inv[:, 1, t:t + 1], x[:, t, :], ALU.mult, ALU.add).then_inc(s_x, 1)

        @block.tensor
        def _(pe):
            pe.wait_ge(s_xq, 1)
            for t in range(TT):
                ins = pe.transpose(bank[1][:, 0:TOK // 2].bitcast(BF16)[:, t * P:(t + 1) * P], xq[:, t, :], w["ident_bf"][:])
            ins.then_inc(s_xqt, 1)
            pe.wait_ge(s_dg, 1)
            for t in range(TT):
                ins = pe.matmul(bank[0][:, t * P:(t + 1) * P], w["ones"][:], dg[:, t, :], start=(t == 0), stop=True, skip_group_check=True)
            ins.then_inc(s_rs, 1)
            pe.wait_ge(s_xqT, 1)
            for c in range(HC):
                pe.matmul(bank[2 + c][:, :], w["ffn_q"][:, 0, c * P:(c + 1) * P], xqT[:], start=True, stop=True).then_inc(s_h, 1)
            pe.wait_ge(s_ac, HC)
            for t in range(TT):
                for c in range(HC):
                    ins = pe.transpose(bank[4 + t][:, c * P:(c + 1) * P], y[:, c, t * P:(t + 1) * P], w["ident"][:])
                ins.then_inc(s_act, 1)
            pe.wait_ge(s_q2, TT)
            for c in range(HC):
                for t in range(TT):
                    ins = pe.transpose(bank[c][:, 0:TOK // 2].bitcast(BF16)[:, t * P:(t + 1) * P], q2[:, t, c * P:(c + 1) * P], w["ident_bf"][:])
                ins.then_inc(s_q2t, 1)
            pe.wait_ge(s_q2T, HC)
            for t in range(TT):
                for c in range(HC):
                    ins = pe.matmul(bank[4 + t][:, 0:D], q2T[:, c, t * P:(t + 1) * P], w["ffn_q"][:, 1, c * P:(c + 1) * P],
                                    start=(c == 0), stop=(c == HC - 1))
                ins.then_inc(s_pr, 1)
    st.close()


def alibi_attention(nc, w, x):
    st = Stage(nc, "l1a")
    HK, DQ, DV = 4, 4, 8
    NQ, NV = H * DQ, HK * DV
    W = NQ + HK * DQ + NV
    SW = 32
    xn = st.sb("xn", [P, TT, D])
    xT = st.sb("xT", [P, TOK])
    NQK = NQ + HK * DQ
    sp_ = st.sb("split", [P, 2, 3, NQK], BF16)
    sr = st.sb("rest_qk", [P, 2, NQK])
    stack = st.sb("stack", [P, TT, H + HK, SW], BF16)
    qkT = st.sb("qkT", [P, 5, TOK], BF16)
    vals = st.sb("vals", [P, TT, HK, 32])
    xb = st.sb("x_bias", [P, TT, D])
    y = st.sb("y", [P, TT, D])
    yT = st.sb("yT", [P, TOK])
    osb = st.sb("o", [P, 2, S])
    rz = st.sb("rz", [P, 2 * Q4])
    norm = Norm(st, w)
    s_chain = st.sem("dve_chain")
    s_xn = st.sem("xn_ready")
    s_xTp = st.sem("x_transposed")
    s_xT = st.sem("xT_ready")
    s_qkv = st.sem("qkv_ready")
    s_split = st.sem("parts_ready")
    s_v = st.sem("values_ready")
    s_stq = st.sem("q_stack_ready")
    s_stk = st.sem("k_stack_ready")
    s_init = st.sem("buffers_set")
    s_stT = st.sem("stack_transposed")
    s_qkT = st.sem("qkT_ready")
    s_ob = st.sem("o_transposed")
    s_fin = st.sem("o_finished")
    s_xb = st.sem("x_bias_ready")
    s_yT = st.sem("yT_ready")
    s_yTp = st.sem("y_transposed")
    s_wp = st.sem("product_ready")
    s_x = st.sem("x_updated")
    bank = st.psum_banks()
    SBK, EBK, OBK, G0, G1 = bank[0:2], bank[2:4], bank[4:6], bank[6], bank[7]

    def at(group, b, h, t0, n):
        r = SW * (h % HK)
        return qkT[r:r + SW, group, b * S + t0:b * S + t0 + n]

    a = Attention(st, w, causal=True, lse=False, scale=float(DQ) ** -0.5, heads_per_out=Q4,
                  q=lambda b, h, t0, n: at(h // HK, b, h, t0, n), k=lambda b, h, t0, n: at(4, b, h, t0, n),
                  values=lambda b, h, c: vals[:, b * SB + c, h % HK, :], out_rows=32, ring=8)
    GROUPS = U // Q4
    with nc.Block() as block:

        @block.gpsimd
        def _(pool):
            w.loaded(pool, "l1a")
            pool.memset(stack[:, :, :, 6 * DQ + 6:SW], 0.0).then_inc(s_init, 1)
            pool.memset(a.parts[:], 0.0).then_inc(a.s_zero, 1)
            for t in range(TT):
                pool.tensor_copy(stack[:, t, 0:H, 6 * DQ:6 * DQ + 6], w["alibi_q"][:, t % SB, :, :])
                ins = pool.tensor_copy(stack[:, t, H:H + HK, 6 * DQ:6 * DQ + 6],
                                       w["alibi_k"][:, t % SB, :].unsqueeze(1).broadcast_to([P, HK, 6]))
            ins.then_inc(s_init, 1)
            norm.gpsimd_rstd(pool)
            pool.tensor_tensor(xb[:], x[:], w["l1a_bp"][:].unsqueeze(1).broadcast_to([P, TT, D]), ALU.add).then_inc(s_xb, 1)
            for t in range(TT):
                pool.wait_ge(s_split, t + 1)
                for part, i, n in split_columns(Q_PARTS):
                    out = stack[:, t, 0:H, i * DQ:(i + n) * DQ].rearrange("p h (n d) -> p h n d", n=n)
                    src = sp_[:, t % 2, part, 0:NQ].rearrange("p (h d) -> p h d", h=H).unsqueeze(2).broadcast_to([P, H, n, DQ])
                    ins = pool.tensor_copy(out, src)
                ins.then_inc(s_stq, 1)

        @block.scalar
        def _(act):
            act.preload_act_table_set(EXP_LN)
            act.wait_ge(s_xTp, 1)
            act.activation(xT[:], G0[:, :], ACT.Copy).then_inc(s_xT, 1)
            act.wait_ge(s_init, 4)
            for t in range(TT):
                act.wait_ge(s_split, t + 1)
                act.activation(vals[:, t, :, 0:DV], EBK[t % 2][:, NQK:W].rearrange("p (h d) -> p h d", h=HK), ACT.Copy).then_inc(s_v, 1)
                for part, i, n in split_columns(K_PARTS):
                    ins = act.activation(stack[:, t, H:H + HK, i * DQ:(i + n) * DQ],
                                         sp_[:, t % 2, part, NQ:NQK].rearrange("p (h d) -> p h d", h=HK), ACT.Copy)
                ins.then_inc(s_stk, 1)
            for n in range(U + 2):
                if n < U:
                    a.scalar_exp(act, n, EBK[n % 2])
                if n % Q4 == 1 and n > 1:
                    g = n // Q4 - 1
                    act.wait_ge(a.s_sum, g + 1)
                    if g >= 2:
                        act.wait_ge(s_ob, g - 1)
                    act.activation(osb[:, g % 2, :], OBK[g % 2][:, 0:S], ACT.Copy).then_inc(a.s_og, 1)
            act.wait_ge(s_yTp, 1)
            act.activation(yT[:], G0[:, :], ACT.Copy).then_inc(s_yT, 1)

        @block.vector
        def _(dve):
            link = Chain(dve, s_chain)
            norm.vector_stats(dve, link, x)
            dve.memset(vals[:], 0.0).then_inc(s_init, 1)
            dve.wait_ge(s_init, 3)
            dve.memset(vals[:, :, :, DV:DV + 1], 1.0).then_inc(s_init, 1)
            norm.vector_apply(dve, xn, x, s_xn)
            for t in range(TT):
                dve.wait_ge(s_qkv, t + 1)
                if t >= 2:
                    dve.wait_ge(s_stq, t - 1)
                    dve.wait_ge(s_stk, t - 1)
                qk = EBK[t % 2][:, 0:NQK]
                hi, mid, lo = (sp_[:, t % 2, i, :] for i in range(3))
                link(dve.tensor_copy(hi, qk))
                link(dve.tensor_tensor(sr[:, t % 2, :], qk, hi, ALU.subtract))
                link(dve.tensor_copy(mid, sr[:, t % 2, :]))
                dve.tensor_tensor(lo, sr[:, t % 2, :], mid, ALU.subtract).then_inc(s_split, 1)
            for g in range(5):
                dve.wait_ge(s_stT, g + 1)
                dve.tensor_copy(qkT[:, g, :], bank[6 + g % 2][:, 0:TOK // 2].bitcast(BF16)).then_inc(s_qkT, 1)
            for u in range(H):
                a.vector_max(dve, u, SBK[u % 2])
            a.vector_parts(dve, link, 0)
            a.vector_shiftT(dve, 0, G0)
            for n in range(U + LAG + 1):
                b, h = divmod(n, H)
                if h == H - 1 and b + 1 < NB:
                    a.vector_shiftT(dve, b + 1, G0)
                for u in ahead(n, H, EARLY):
                    a.vector_max(dve, u, SBK[u % 2])
                if h == H - 1 - EARLY and b + 1 < NB:
                    a.vector_parts(dve, link, b + 1)
                if n >= Q4 + LAG and (n - LAG) % Q4 == 0:
                    g = (n - LAG) // Q4 - 1
                    b2, hg = divmod(g, H // Q4)
                    dve.wait_ge(s_ob, g + 1)
                    if g:
                        dve.wait_ge(s_fin, g)
                    o = G1[:, 0:SB * P].rearrange("p (c r) -> p c r", r=32)
                    link(dve.reciprocal(rz[:], o[:, :, DV]))
                    dst = y[:, b2 * SB:(b2 + 1) * SB, hg * 32:(hg + 1) * 32].rearrange("p c (j d) -> p c j d", d=DV)
                    for c in range(SB):
                        ins = dve.tensor_tensor(dst[:, c], o[:, c * Q4:(c + 1) * Q4, 0:DV],
                                                bcast(rz[:, c * Q4:(c + 1) * Q4], Q4, DV), ALU.mult)
                    ins.then_inc(s_fin, 1)
            dve.wait_ge(s_xb, 1)
            for t in range(TT):
                dve.wait_ge(s_wp, t + 1)
                dve.tensor_tensor(x[:, t, :], bank[t % 4][:, 0:D], xb[:, t, :], ALU.add).then_inc(s_x, 1)

        @block.tensor
        def _(pe):
            tensor_transpose_tiles(pe, w, G0, xn, s_xn, s_xTp)
            w.loaded(pe, "l1a")
            pe.wait_ge(s_xT, 1)
            for t in range(TT):
                if t >= 2:
                    pe.wait_ge(s_v, t - 1)
                pe.matmul(EBK[t % 2][:, 0:W], xT[:, t * P:(t + 1) * P], w["l1a_qkv"][:], start=True, stop=True).then_inc(s_qkv, 1)
            pe.wait_ge(s_init, 4)
            for g in range(5):
                if g >= 2:
                    pe.wait_ge(s_qkT, g - 1)
                for t in range(TT):
                    pe.wait_ge(s_stq, t + 1)
                    pe.wait_ge(s_stk, t + 1)
                    ins = pe.transpose(bank[6 + g % 2][:, 0:TOK // 2].bitcast(BF16)[:, t * P:(t + 1) * P],
                                       stack[:, t, g * HK:(g + 1) * HK, :], w["ident_bf"][:])
                ins.then_inc(s_stT, 1)
            pe.wait_ge(s_qkT, 5)
            for u in range(H):
                a.tensor_S(pe, u, SBK[u % 2])
            a.tensor_shift(pe, 0, G0)
            for n in range(U + LAG + 1):
                b, h = divmod(n, H)
                if h == H - 1 and b + 1 < NB:
                    a.tensor_shift(pe, b + 1, G0)
                if n < U:
                    a.tensor_E(pe, n, EBK[n % 2])
                for u in ahead(n, H, EARLY):
                    a.tensor_S(pe, u, SBK[u % 2])
                if n >= Q4 and n % Q4 == 0:
                    a.tensor_PV(pe, n // Q4 - 1, OBK[(n // Q4 - 1) % 2])
                if n >= Q4 + LAG and (n - LAG) % Q4 == 0:
                    g = (n - LAG) // Q4 - 1
                    pe.wait_ge(a.s_og, g + 1)
                    if g:
                        pe.wait_ge(s_fin, g)
                    for c in range(SB):
                        ins = pe.transpose(G1[:, c * P:(c + 1) * P], osb[:, g % 2, c * P:(c + 1) * P], w["ident"][:])
                    ins.then_inc(s_ob, 1)
            pe.wait_ge(s_fin, GROUPS)
            for t in range(TT):
                ins = pe.transpose(G0[:, t * P:(t + 1) * P], y[:, t, :], w["ident"][:])
            ins.then_inc(s_yTp, 1)
            pe.wait_ge(s_yT, 1)
            for t in range(TT):
                pe.matmul(bank[t % 4][:, 0:D], yT[:, t * P:(t + 1) * P], w["l1a_p"][:], start=True, stop=True).then_inc(s_wp, 1)
    st.close()


def head_attention(nc, w, x, ctx, v_dram):
    st = Stage(nc, "l1x")
    HD = 64
    assert NB == 2
    GT = P // H
    NG = S // GT
    GB = 4
    NU = NB * NG // GB
    UB = NU // NB
    J = 8
    xn = st.sb("xn", [P, TT, D])
    xT = st.sb("xT", [P, 2, TOK])
    qT = st.sb("qT", [P, S, H])
    kT = st.sb("kT", [P, S, H])
    vt = st.sb("v_tokens", [P, 2, H * HD])
    vg = st.sb("v_groups", [P, NB * NG, HD])
    oT = st.sb("oT", [P, NB, J, H, S // 16])
    xb = st.sb("x_bias", [P, TT, D])
    bq = st.sb("q_bias", [P, H])
    nmax = st.sb("nmax", [P, NB, NG])
    zsum = st.sb("zsum", [P, NB, NG])
    lnz = st.sb("lnz", [P, NG])
    shift = st.sb("shift", [P, NG])
    rest = st.sb("rest", [P, NG])
    parts = st.sb("parts", [P, NB, P], BF16)
    shiftT = st.sb("shiftT", [P, NB, P], BF16)
    expT = st.sb("expT", [P, 3, GB * P])
    norm = Norm(st, w)
    names = ("dve_chain", "xn_ready", "transposed", "xT_ready", "x_bias_ready", "v_projected", "v_biased", "v_stored", "v_regrouped",
             "heads_projected", "heads_by_scalar", "heads_by_vector", "max_scores_ready", "max_done", "sum_done", "log_ready",
             "parts_set", "parts_ready", "shift_transposed", "shiftT_ready", "exp_scores_ready", "exp_ready", "exp_used",
             "out_evicted", "product_ready", "x_updated", "q_bias_ready")
    (s_chain, s_xn, s_tp, s_xT, s_xb, s_vp, s_vb, s_vs, s_vg, s_pr, s_pa, s_pv, s_s, s_mx, s_lse, s_ln, s_ps, s_parts, s_shp, s_shT,
     s_e, s_p, s_used, s_og, s_wo, s_x, s_bq) = (st.sem(n) for n in names)
    bank = st.psum_banks()
    SBK, EBK, OBK, G0, G1 = bank[0:2], bank[2:4], bank[4:6], bank[6], bank[7]
    jobs = [(kind, c) for kind in "kq" for c in range(H // 2)]

    EARLY_U = 2
    plan = [x for i in range(4) for x in (("maximum", i), ("values", i))] + [("maximum", i) for i in range(4, UB)]
    plan += [("values", i) for i in range(4, 2 * TT)]

    def group(buf, n, i):
        u, q = divmod(n, UB)
        g = q * GB + i
        return buf[HD * u:HD * (u + 1), g * GT:(g + 1) * GT, :].rearrange("p t h -> p (t h)")

    with nc.Block() as block:

        @block.sync
        def _(sp):
            for t in range(TT):
                sp.wait_ge(s_vb, 2 * t + 2)
                sp.dma_start(v_dram[t * P:(t + 1) * P, :], vt[:, t % 2, :]).then_inc(s_vs, 16)
                sp.wait_ge(s_vs, 16 * (t + 1))
                src = v_dram[t * P:(t + 1) * P, :].rearrange("(g t) (h d) -> (t h) g d", t=GT, d=HD)
                sp.dma_start(vg[:, t * (P // GT):(t + 1) * (P // GT), :], src).then_inc(s_vg, 16)
            sp.wait_ge(s_vg, 16 * TT)

        @block.gpsimd
        def _(pool):
            w.loaded(pool, "l1x")
            pool.tensor_scalar(bq[:], w["l1x_bq"][:], float(HD) ** -0.5, None, ALU.mult).then_inc(s_bq, 1)
            pool.tensor_tensor(xb[:], x[:], w["l1x_bo"][:].unsqueeze(1).broadcast_to([P, TT, D]), ALU.add).then_inc(s_xb, 1)
            for u in range(NB):
                pool.memset(parts[:, u, 3 * NG + GT:P], 0.0)
                ins = pool.tensor_copy(parts[:, u, 3 * NG:3 * NG + GT], w["other_token"][:])
            ins.then_inc(s_ps, 1)
            norm.gpsimd_rstd(pool)

        @block.scalar
        def _(act):
            act.wait_ge(s_tp, 1)
            act.activation(xT[:, 1, :], G0[:, :], ACT.Copy).then_inc(s_xT, 1)
            act.preload_act_table_set(EXP_LN)
            w.loaded(act, "l1x")
            act.wait_ge(s_bq, 1)
            for n in range(0, len(jobs), 2):
                if jobs[n] == ("q", 0):
                    act.wait_ge(s_tp, 2)
                    act.activation(xT[:, 0, :], G1[:, :], ACT.Copy).then_inc(s_xT, 1)
                kind, c = jobs[n]
                buf, bias = (qT, bq) if kind == "q" else (kT, w["l1x_bk"])
                act.wait_ge(s_pr, n + 1)
                for i in range(2):
                    h = 2 * c + i
                    ins = act.activation(buf[:, :, h], bank[n % 4][:, i * S:(i + 1) * S], ACT.Identity,
                                         bias=bias[:, h:h + 1], scale=float(HD) ** -0.5 if kind == "q" else 1.0)
                ins.then_inc(s_pa, 1)

            def row_sums(n):
                u, q = divmod(n, UB)
                act.wait_ge(s_mx, n + 1)
                for i in range(GB):
                    part = SBK[n % 2][:, i * P:(i + 1) * P]
                    g = q * GB + i
                    ins = act.activation(part, part, ACT.Exp, bias=nmax[:, u, g:g + 1], accum_out=zsum[:, u, g:g + 1])
                ins.then_inc(s_lse, 1)

            def logs(u):
                act.wait_ge(s_lse, UB * (u + 1))
                if u:
                    act.wait_ge(s_parts, u)
                act.activation(lnz[:], zsum[:, u, :], ACT.Ln).then_inc(s_ln, 1)

            for n in range(UB):
                row_sums(n)
            logs(0)
            for n in range(NU + 1):
                if n < NU:
                    act.wait_ge(s_e, n + 1)
                    if n >= 3:
                        act.wait_ge(s_used, n - 2)
                    act.activation(expT[:, n % 3, :], EBK[n % 2][:, :], ACT.Exp).then_inc(s_p, 1)
                for m in ahead(n, UB, EARLY_U):
                    row_sums(m)
                if n % UB == UB - 1 - EARLY_U and n // UB + 1 < NB:
                    logs(n // UB + 1)

        @block.vector
        def _(dve):
            link = Chain(dve, s_chain)
            norm.vector_stats(dve, link, x)
            norm.vector_apply(dve, xn, x, s_xn)
            w.loaded(dve, "l1x")
            dve.wait_ge(s_bq, 1)
            for n in range(1, len(jobs), 2):
                kind, c = jobs[n]
                buf, bias = (qT, bq) if kind == "q" else (kT, w["l1x_bk"])
                dve.wait_ge(s_pr, n + 1)
                for i in range(2):
                    h = 2 * c + i
                    ins = dve.tensor_scalar(buf[:, :, h], bank[n % 4][:, i * S:(i + 1) * S],
                                            float(HD) ** -0.5 if kind == "q" else 1.0, bias[:, h:h + 1], ALU.mult, ALU.add)
                ins.then_inc(s_pv, 1)

            def maxima(n):
                u, q = divmod(n, UB)
                dve.wait_ge(s_s, n + 1)
                dve.tensor_reduce(nmax[:, u, q * GB:(q + 1) * GB], SBK[n % 2][:, :].rearrange("p (g k) -> p g k", g=GB), AX, ALU.max,
                                  negate=True).then_inc(s_mx, 1)

            def split(u):
                dve.wait_ge(s_ln, u + 1)
                link(dve.tensor_tensor(shift[:], nmax[:, u, :], lnz[:], ALU.subtract))
                hi, mid, lo = (parts[:, u, i * NG:(i + 1) * NG] for i in range(3))
                link(dve.tensor_copy(hi, shift[:]))
                link(dve.tensor_tensor(rest[:], shift[:], hi, ALU.subtract))
                link(dve.tensor_copy(mid, rest[:]))
                dve.tensor_tensor(lo, rest[:], mid, ALU.subtract).then_inc(s_parts, 1)

            def values(i):
                t, half = divmod(i, 2)
                dve.wait_ge(s_vp, i + 1)
                if t >= 2 and half == 0:
                    dve.wait_ge(s_vs, 16 * (t - 1))
                dve.tensor_tensor(vt[:, t % 2, half * 512:(half + 1) * 512], bank[4 + i % 2][:, :],
                                  w["l1x_bv"][:, half * 512:(half + 1) * 512], ALU.add).then_inc(s_vb, 1)

            def copy_shift(u):
                dve.wait_ge(s_shp, u + 1)
                dve.tensor_copy(shiftT[:, u, :], G0[:, 0:P // 2].bitcast(BF16)).then_inc(s_shT, 1)

            for what, i in plan:
                if what == "maximum":
                    maxima(i)
                else:
                    if i == 4:
                        split(0)
                        copy_shift(0)
                    values(i)
            for n in range(NU + 2):
                u = n // UB
                if n % UB == UB - 1 and u + 1 < NB:
                    copy_shift(u + 1)
                for m in ahead(n, UB, EARLY_U):
                    maxima(m)
                if n % UB == UB - 1 - EARLY_U and u + 1 < NB:
                    split(u + 1)
                if n >= 2:
                    m = n - 2
                    u2, q = divmod(m, UB)
                    dve.wait_ge(s_used, m + 1)
                    out = oT[:, u2, :, :, 2 * q:2 * q + 2].rearrange("p j h s -> p s j h")
                    for s in range(2):
                        ins = dve.tensor_copy(out[:, s], OBK[m % 2][:, s * P:(s + 1) * P].rearrange("p (j h) -> p j h", j=J))
                    ins.then_inc(s_og, 1)
            dve.wait_ge(s_xb, 1)
            for t in range(TT):
                dve.wait_ge(s_wo, t + 1)
                dve.tensor_tensor(x[:, t, :], bank[t % 4][:, 0:D], xb[:, t, :], ALU.add).then_inc(s_x, 1)

        @block.tensor
        def _(pe):
            w.loaded(pe, "l1x")
            for t in range(TT):
                ins = pe.transpose(G0[:, t * P:(t + 1) * P], ctx[:, t, :], w["ident"][:])
            ins.then_inc(s_tp, 1)
            pe.wait_ge(s_xT, 1)
            for n, (kind, c) in enumerate(jobs):
                if (kind, c) == ("q", 0):
                    tensor_transpose_tiles(pe, w, G1, xn, s_xn, s_tp)
                    pe.wait_ge(s_xT, 2)
                if n >= 4:
                    pe.wait_ge(s_pv if n % 2 else s_pa, n // 2 - 1)
                for i in range(2):
                    for u in range(NB):
                        h = 2 * c + i
                        ins = pe.matmul(bank[n % 4][HD * u:HD * (u + 1), i * S:(i + 1) * S], w[f"l1x_{kind}"][:, h * HD:(h + 1) * HD],
                                        xT[:, int(kind == "k"), u * S:(u + 1) * S], start=(i == 0), stop=True, skip_group_check=True)
                ins.then_inc(s_pr, 1)
            pe.wait_ge(s_pa, len(jobs) // 2)
            pe.wait_ge(s_pv, len(jobs) // 2)

            def scores_for_max(n):
                if n >= 2:
                    pe.wait_ge(s_lse, n - 1)
                out = SBK[n % 2]
                pe.matmul(out[:, :], w["same_token"][:], w["other_token4"][:], start=True, stop=False, skip_group_check=True)
                for i in range(GB):
                    ins = pe.matmul(out[:, i * P:(i + 1) * P], group(qT, n, i), group(kT, n, i), start=False, stop=True, skip_group_check=True)
                ins.then_inc(s_s, 1)

            def scores_for_exp(n):
                u, q = divmod(n, UB)
                if n >= 2:
                    pe.wait_ge(s_p, n - 1)
                out = EBK[n % 2]
                for i in range(GB):
                    pe.matmul(out[:, i * P:(i + 1) * P], w["sel_group"][:, q * GB + i, :], shiftT[:, u, :], start=(i == 0), stop=False,
                              skip_group_check=True)
                for i in range(GB):
                    ins = pe.matmul(out[:, i * P:(i + 1) * P], group(kT, n, i), group(qT, n, i), start=False, stop=True, skip_group_check=True)
                ins.then_inc(s_e, 1)

            def weighted_values(n):
                u, q = divmod(n, UB)
                pe.wait_ge(s_p, n + 1)
                if q == 0:
                    pe.wait_ge(s_vg, 16 * SB * (u + 1))
                    pe.wait_ge(s_vb, 2 * TT)
                if n >= 2:
                    pe.wait_ge(s_og, n - 1)
                for i in range(GB):
                    r = HD * (i % 2)
                    ins = pe.matmul(OBK[n % 2][r:r + HD, (i // 2) * P:(i // 2 + 1) * P], vg[:, u * NG + q * GB + i, :],
                                    expT[:, n % 3, i * P:(i + 1) * P], start=(i < 2), stop=True, skip_group_check=True)
                ins.then_inc(s_used, 1)

            def values(i):
                t, half = divmod(i, 2)
                if i >= 2:
                    pe.wait_ge(s_vb, i - 1)
                pe.matmul(bank[4 + i % 2][:, :], xT[:, 1, t * P:(t + 1) * P], w["l1x_v"][:, half * 512:(half + 1) * 512],
                          start=True, stop=True).then_inc(s_vp, 1)

            def transpose_shift(u):
                pe.wait_ge(s_ps, 1)
                pe.wait_ge(s_parts, u + 1)
                pe.transpose(G0[:, 0:P // 2].bitcast(BF16), parts[:, u, :], w["ident_bf"][:]).then_inc(s_shp, 1)

            for what, i in plan:
                if what == "maximum":
                    scores_for_max(i)
                elif i < 2 * TT - 2:
                    values(i)
            transpose_shift(0)
            for i in range(2 * TT - 2, 2 * TT):
                values(i)
            for n in range(NU + 1):
                u = n // UB
                if n % UB == UB - 1 and u + 1 < NB:
                    transpose_shift(u + 1)
                if n < NU:
                    if n % UB == 0:
                        pe.wait_ge(s_shT, u + 1)
                    scores_for_exp(n)
                for m in ahead(n, UB, EARLY_U):
                    scores_for_max(m)
                if n:
                    weighted_values(n - 1)
            pe.wait_ge(s_og, NU)
            for t in range(TT):
                u, c = divmod(t, SB)
                for j in range(J):
                    ins = pe.matmul(bank[t % 4][:, 0:D], oT[:, u, j, c * J:(c + 1) * J, :].rearrange("p h s -> p (h s)"),
                                    w["l1x_o"][:, j, :], start=(j == 0), stop=(j == J - 1))
                ins.then_inc(s_wo, 1)
    st.close()


def expert_ffn(nc, w, x):
    st = Stage(nc, "moe")
    NE = E + 1
    ALPHA, LIMIT = 1.702, 7.0
    xn = st.sb("xn", [P, TT, D])
    xT = st.sb("xT", [P, TOK])
    logit = st.sb("logit", [P, TT, E])
    small = st.sb("small", [P, 2, TT])
    score = st.sb("score", [P, TT, E])
    biased = st.sb("biased", [P, TT, E])
    above = st.sb("above", [P, TT, E, E])
    equal = st.sb("equal", [P, TT, E, E])
    rank = st.sb("rank", [P, TT, E])
    cw = st.sb("expert_weight", [P, TT, NE])
    cwT = st.sb("expert_weightT", [NE, TOK])
    h1 = st.sb("h1", [P, 2, TOK])
    hh = st.sb("h13", [P, 2, TOK])
    g = st.sb("gate", [P, 2, TOK])
    sg = st.sb("sigmoid", [P, 2, TOK])
    act_in = st.sb("l1g", [P, 2, TOK])
    a = st.sb("a", [P, 2, TOK])
    norm = Norm(st, w)
    names = ("dve_chain", "xn_ready", "transposed", "xT_ready", "logits_ready", "shifted_ready", "exp_ready", "cw_ready", "cw_transposed",
             "cwT_ready", "bias_ready", "x_seeded", "hidden_ready", "h1_ready", "h13_ready", "gate_ready", "sigmoid_ready", "lg_ready",
             "a_ready", "y_ready", "y_added")
    (s_chain, s_xn, s_tp, s_xT, s_lg, s_sh, s_ex, s_cw, s_cwp, s_cwT, s_b, s_xs, s_h, s_h1, s_hh, s_g, s_sg, s_l, s_a, s_y,
     s_ya) = (st.sem(n) for n in names)
    bank = st.psum_banks()
    G0, G1 = bank[6], bank[7]

    def pair(n):
        return bank[2 * (n % 3)], bank[2 * (n % 3) + 1]

    with nc.Block() as block:

        @block.gpsimd
        def _(pool):
            pool.memset(cw[:, :, E:NE], 1.0).then_inc(s_cw, 1)
            norm.gpsimd_rstd(pool)
            for e in range(NE):
                pool.wait_ge(s_l, e + 1)
                pool.wait_ge(s_sg, e + 1)
                if e >= 2:
                    pool.wait_ge(s_y, e - 1)
                pool.tensor_tensor(a[:, e % 2, :], act_in[:, e % 2, :], sg[:, e % 2, :], ALU.mult).then_inc(s_a, 1)

        @block.scalar
        def _(act):
            act.wait_ge(s_tp, 1)
            act.activation(xT[:], G0[:, :], ACT.Copy).then_inc(s_xT, 1)
            act.wait_ge(s_sh, 1)
            act.activation(score[:], logit[:], ACT.Exp).then_inc(s_ex, 1)
            w.loaded(act, "moe")

            def sigmoid(e):
                act.wait_ge(s_g, e + 1)
                if e >= 2:
                    act.wait_ge(s_a, e - 1)
                act.activation(sg[:, e % 2, :], g[:, e % 2, :], ACT.Sigmoid, scale=ALPHA).then_inc(s_sg, 1)

            for n in range(2 * NE):
                e, part = divmod(n, 2)
                act.wait_ge(s_h, n + 1)
                if n >= 2:
                    act.wait_ge(s_hh, n - 1)
                act.activation(h1[:, n % 2, :], pair(n)[0][:, :], ACT.Identity, bias=w["moe_b1"][:, e, part:part + 1]).then_inc(s_h1, 1)
                if part:
                    sigmoid(e)

        @block.vector
        def _(dve):
            link = Chain(dve, s_chain)
            norm.vector_stats(dve, link, x)
            norm.vector_apply(dve, xn, x, s_xn)
            dve.wait_ge(s_lg, 1)
            lg = G1[:, 0:TT * E].rearrange("p (t e) -> p t e", t=TT)
            link(dve.tensor_reduce(small[:, 0, :], lg, AX, ALU.max, negate=True))
            dve.tensor_tensor(logit[:], lg, bcast(small[:, 0, :], TT, E), ALU.add).then_inc(s_sh, 1)
            dve.wait_ge(s_ex, 1)
            w.loaded(dve, "moe")
            link(dve.tensor_reduce(small[:, 1, :], score[:], AX, ALU.add))
            link(dve.reciprocal(small[:, 0, :], small[:, 1, :]))
            link(dve.tensor_tensor(score[:], score[:], bcast(small[:, 0, :], TT, E), ALU.mult))
            link(dve.tensor_tensor(biased[:], score[:], w["moe_gate_b"][:].unsqueeze(1).broadcast_to([P, TT, E]), ALU.add))
            for t in range(TT):
                mine = bcast(biased[:, t, :], E, E)
                theirs = biased[:, t, :].unsqueeze(1).broadcast_to([P, E, E])
                dve.tensor_tensor(above[:, t], theirs, mine, ALU.is_gt)
                ins = dve.tensor_tensor(equal[:, t], theirs, mine, ALU.is_equal)
            link(ins)
            link(dve.tensor_tensor(equal[:], equal[:], w["before"][:].unsqueeze(1).broadcast_to([P, TT, E * E]).rearrange("p t (e f) -> p t e f", e=E), ALU.mult))
            link(dve.tensor_tensor(above[:], above[:], equal[:], ALU.add))
            link(dve.tensor_reduce(rank[:], above[:], AX, ALU.add))
            dve.wait_ge(s_cw, 1)
            dve.scalar_tensor_tensor(cw[:, :, 0:E], rank[:], 2.0, score[:], ALU.is_lt, ALU.mult).then_inc(s_cw, 1)
            dve.wait_ge(s_cwp, 1)
            dve.tensor_copy(cwT[:], G0[0:NE, :]).then_inc(s_cwT, 1)
            dve.wait_ge(s_b, 1)
            dve.tensor_tensor(x[:], x[:], G1[:, :].rearrange("p (t d) -> p t d", t=TT), ALU.add).then_inc(s_xs, 1)

            def add_expert(e):
                dve.wait_ge(s_y, e + 1)
                if e:
                    dve.wait_ge(s_ya, e)
                else:
                    dve.wait_ge(s_xs, 1)
                for t in range(TT):
                    ins = dve.scalar_tensor_tensor(x[:, t, :], bank[6 + e % 2][:, t * P:(t + 1) * P], cw[:, t, e:e + 1], x[:, t, :],
                                                   ALU.mult, ALU.add)
                ins.then_inc(s_ya, 1)

            for n in range(2 * NE):
                e, part = divmod(n, 2)
                dve.wait_ge(s_h1, n + 1)
                if n >= 2:
                    dve.wait_ge(s_g if part == 0 else s_l, n // 2)
                dve.scalar_tensor_tensor(hh[:, n % 2, :], pair(n)[1][:, :], w["moe_b3"][:, e, part:part + 1], h1[:, n % 2, :],
                                         ALU.add, ALU.mult).then_inc(s_hh, 1)
                dve.wait_ge(s_hh, n + 1)
                if part == 0:
                    if e >= 2:
                        dve.wait_ge(s_sg, e - 1)
                    dve.tensor_scalar(g[:, e % 2, :], hh[:, 0, :], LIMIT, None, ALU.min).then_inc(s_g, 1)
                else:
                    link(dve.tensor_scalar(hh[:, 1, :], hh[:, 1, :], LIMIT, -LIMIT, ALU.min, ALU.max))
                    if e >= 2:
                        dve.wait_ge(s_a, e - 1)
                    dve.scalar_tensor_tensor(act_in[:, e % 2, :], hh[:, 1, :], 1.0, g[:, e % 2, :], ALU.add, ALU.mult).then_inc(s_l, 1)
                    if e:
                        add_expert(e - 1)
            add_expert(NE - 1)

        @block.tensor
        def _(pe):
            tensor_transpose_tiles(pe, w, G0, xn, s_xn, s_tp)
            pe.wait_ge(s_xT, 1)
            w.loaded(pe, "moe")
            for t in range(TT):
                ins = pe.matmul(G1[:, t * E:(t + 1) * E], xT[:, t * P:(t + 1) * P], w["moe_gateT"][:], start=(t == 0), stop=True,
                                skip_group_check=True)
            ins.then_inc(s_lg, 1)

            def hidden(n):
                e, part = divmod(n, 2)
                if n >= 3:
                    pe.wait_ge(s_hh, n - 2)
                for out, name in zip(pair(n), ("moe_w1", "moe_w3")):
                    ins = pe.matmul(out[:, :], w[name][:, e, part, :], xT[:], start=True, stop=True)
                ins.then_inc(s_h, 1)

            def expert_out(e):
                pe.wait_ge(s_a, e + 1)
                if e >= 2:
                    pe.wait_ge(s_ya, e - 1)
                for t in range(TT):
                    ins = pe.matmul(bank[6 + e % 2][:, t * P:(t + 1) * P], a[:, e % 2, t * P:(t + 1) * P], w["moe_w2"][:, e, :],
                                    start=(t == 0), stop=True, skip_group_check=True)
                ins.then_inc(s_y, 1)

            for n in range(3):
                hidden(n)
            pe.wait_ge(s_cw, 2)
            for t in range(TT):
                ins = pe.transpose(G0[0:NE, t * P:(t + 1) * P], cw[:, t, :], w["ident"][:])
            ins.then_inc(s_cwp, 1)
            pe.wait_ge(s_cwT, 1)
            for t in range(TT):
                ins = pe.matmul(G1[:, t * P:(t + 1) * P], cwT[:, t * P:(t + 1) * P], w["moe_b2"][:], start=(t == 0), stop=True,
                                skip_group_check=True)
            ins.then_inc(s_b, 1)
            pe.wait_ge(s_xs, 1)
            for n in range(3, 2 * NE):
                hidden(n)
                if n % 2 and n >= 3:
                    expert_out((n - 3) // 2)
            expert_out(NE - 1)
    st.close()



class Weights(dict):

    def __init__(self):
        super().__init__()
        self.groups = {}

    def loaded(self, eng, group):
        sem, count = self.groups[group]
        eng.wait_ge(sem, count)


def setup(nc, ctx, dram):
    w = Weights()

    def sb(name, shape, dt=F32):
        t = ctx.enter_context(nc.sbuf_tensor(f"w_{name}", shape, dt))
        w[name] = t
        return t

    loads = {
        "const": [("ident", [P, P]), ("mask_q32", [P, P]), ("mask_k32", [P, P]), ("sel32", [P, H]), ("minus_half", [P, 8]), ("ones", [P, P]), ("group32", [P, 32]),
                  ("same_token32", [P, P]), ("other_rows32", [P, P]), ("other_token", [P, 8])],
        "l0a": [("l0a_qkv", [P, 3 * D]), ("gamma", [P, D]), ("beta", [P, D])],
        "l0x_vo": [("l0x_v", [P, H * 64]), ("l0x_o", [P, H // 2, D])],
        "toeplitz": [("toeplitz", [P, H, TW])],
        "l0x": [("l0x_k", [P, H * 64]), ("l0x_q", [P, H * 64]), ("l0x_bo", [P, D])],
        "ffn": [("ffn_conv", [P, HC, 4])],
        "l1a": [("l1a_qkv", [P, 112]), ("l1a_p", [P, D]), ("l1a_bp", [P, D]), ("alibi_q", [P, SB, H, 6]), ("alibi_k", [P, SB, 6])],
        "l1x": [("l1x_q", [P, H * 64]), ("l1x_k", [P, H * 64]), ("l1x_v", [P, H * 64]), ("l1x_o", [P, 8, D]), ("l1x_bq", [P, H]),
                ("l1x_bk", [P, H]), ("l1x_bv", [P, H * 64]), ("l1x_bo", [P, D])],
        "moe": [("moe_w1", [P, E + 1, 2, F]), ("moe_w3", [P, E + 1, 2, F]), ("moe_w2", [P, E + 1, D]), ("moe_b1", [P, E + 1, 2]),
                ("moe_b3", [P, E + 1, 2]), ("moe_b2", [E + 1, D]), ("moe_gateT", [P, E]), ("moe_gate_b", [P, E]), ("before", [P, E * E])],
    }
    todo = []
    for g, items in loads.items():
        sem = ctx.enter_context(nc.semaphore(f"loaded_{g}"))
        for name, shape in items:
            t = sb(name, shape)
            src = dram[name]
            if len(src.shape) == 1:
                src = src.unsqueeze(0).broadcast_to([P, src.shape[0]])
            todo.append((t, src, sem))
        w.groups[g] = (sem, 16 * len(items))
    sb("ident_bf", [P, P], BF16)
    sb("mask_q", [P, P], BF16)
    sb("mask_k", [P, P], BF16)
    sb("sel", [P, H, P], BF16)
    sb("same_token", [P, P], BF16)
    sb("other_token4", [P, 4 * P], BF16)
    sb("sel_group", [P, 32, P], BF16)
    sb("l0x_vo", [P, D])
    sb("ffn_q", [P, 2, HID], BF16)
    sb("ffn_wmean", [P, 2])
    with nc.Block() as block:

        @block.sync
        def _(sp):
            for t, src, sem in todo:
                sp.dma_start(t[:], src).then_inc(sem, 16)

        @block.vector
        def _(dve):
            w.loaded(dve, "const")
            dve.tensor_copy(w["ident_bf"][:], w["ident"][:])
            dve.tensor_copy(w["mask_q"][:], w["mask_q32"][:])
            dve.tensor_copy(w["mask_k"][:], w["mask_k32"][:])
            dve.tensor_copy(w["sel"][:], bcast(w["sel32"][:], H, P))
            dve.tensor_copy(w["same_token"][:], w["same_token32"][:])
            dve.tensor_copy(w["other_token4"][:].rearrange("p (a k) -> p a k", a=4), w["other_rows32"][:].unsqueeze(1).broadcast_to([P, 4, P]))
            dve.tensor_tensor(w["sel_group"][:], bcast(w["group32"][:], 32, P), w["same_token32"][:].unsqueeze(1).broadcast_to([P, 32, P]), ALU.add)
    return w


def decoder(nc, dram, out):
    with ExitStack() as ctx:
        x = ctx.enter_context(nc.sbuf_tensor("x", [P, TT, D], F32))
        c = ctx.enter_context(nc.sbuf_tensor("ctx", [P, TT, D], F32))
        v_dram = nc.dram_tensor("l1x_values", (TOK, H * 64), F32, kind="Internal").ap()
        w = setup(nc, ctx, dram)
        weight_levels(nc, w, dram)
        with nc.Fori(0, PASSES) as it:
            rel_attention(nc, w, x, c, dram["x"], dram["ctx_1024"], it)
            cross_attention(nc, w, x, c, dram, it)
            quantized_ffn(nc, w, x)
            alibi_attention(nc, w, x)
            head_attention(nc, w, x, c, v_dram)
            expert_ffn(nc, w, x)
            store(nc, w, x, out, it)


def store(nc, w, x, out, it):
    st = Stage(nc, "store")
    s_out = st.sem("out_stored")
    st.sem("unused")
    with nc.Block() as block:

        @block.sync
        def _(sp):
            w.loaded(sp, "moe")
            sp.dma_start(out[bass.ts(it, NB)].rearrange("b (c p) d -> p (b c) d", p=P), x[:]).then_inc(s_out, 16)
            sp.wait_ge(s_out, 16)
    st.close()



def _constants(np):
    r = np.arange(P)
    c = {"ident": np.eye(P), "mask_q32": np.where(r[None, :] > r[:, None], -BIG, 0.0),
         "mask_k32": np.where(r[:, None] > r[None, :], -BIG, 0.0), "minus_half": np.full((P, 8), -0.5), "ones": np.ones((P, P))}
    k = np.arange(P)
    c["sel32"] = (k[:, None] % H == np.arange(H)[None, :]) & (k[:, None] < 3 * H)
    c["group32"] = (k[:, None] % 32 == np.arange(32)[None, :]) & (k[:, None] < 96)
    c["same_token32"] = (k[:, None] - 96 == r[None, :] // H)
    c["other_rows32"] = np.where((k[:, None] >= 96) & (k[:, None] < 104) & (k[:, None] - 96 != r[None, :] // H), -BIG, 0.0)
    c["other_token"] = np.where(r[:, None] // H != np.arange(8)[None, :], -BIG, 0.0)
    c["before"] = np.broadcast_to((np.arange(E)[None, :] < np.arange(E)[:, None]).reshape(-1), (P, E * E))
    slopes = (2.0 ** (-8.0 * np.arange(1, H + 1) / H)).astype(np.float32)
    pos = np.arange(S).astype(np.float32).reshape(SB, P).T
    c["alibi_q"] = np.concatenate([np.broadcast_to(_parts(np, slopes), (P, SB, H, 3)), _parts(np, -slopes * pos[:, :, None])], -1)
    c["alibi_k"] = np.stack([pos] * 3 + [np.ones_like(pos)] * 3, -1)
    return {n: np.ascontiguousarray(v, np.float32) for n, v in c.items()}


def _parts(np, v):
    out = []
    for _ in range(3):
        m, e = np.frexp(v)
        h = np.ldexp(np.rint(m * 256.0) / 256.0, e).astype(np.float32)
        out.append(h)
        v = v - h
    return np.stack(out, -1)


def kernel(**inputs):
    import numpy as np
    import concourse.bacc as bacc
    from concourse.bass_utils import run_bass_kernel_spmd as run

    i = {k: np.asarray(v) for k, v in inputs.items()}
    a = {"x": i["x"], "ctx_1024": i["ctx_1024"]}
    a["l0a_qkv"] = np.concatenate([i["L0_attn_Wq"].T, i["L0_attn_Wk"].T, i["L0_attn_Wv"].T], 1)
    a["gamma"], a["beta"] = i["L0_attn_ln_gamma"], i["L0_attn_ln_beta"]
    a["toeplitz"] = i["L0_attn_rel_bias_table"][(np.arange(TW)[None, :] - np.arange(P)[:, None] + P - 1)].transpose(0, 2, 1)
    for n in "qkv":
        a[f"l0x_{n}"] = i[f"L0_xattn_W{n}"]
    a["l0x_o"] = i["L0_xattn_Wo"].reshape(H // 2, P, D).transpose(1, 0, 2)
    a["l0x_bo"] = i["L0_xattn_bo"]
    padded = i["mask_BxS2_bf0"].view(np.uint8)
    a["padded"] = padded.view(np.uint32)
    a["padded_keys"] = np.ascontiguousarray(padded.reshape(PASSES, NB, SB, P).transpose(0, 3, 1, 2)).reshape(PASSES, P, NB * SB).view(np.uint32)
    a["ffn_w1T"] = i["L0_ffn_w1"].T
    a["ffn_w2T"] = i["L0_ffn_w2"].T.reshape(HC, P, D).transpose(1, 0, 2).reshape(P, HID)
    a["ffn_conv"] = np.concatenate([i["L0_ffn_conv_w"][:, 0, :], i["L0_ffn_conv_b"][:, None]], 1).reshape(HC, P, 4).transpose(1, 0, 2)
    a["l1a_qkv"] = np.concatenate([i["L1_attn_Wq"], i["L1_attn_Wk"], i["L1_attn_Wv"]], 1)
    a["l1a_p"], a["l1a_bp"] = i["L1_attn_Wp"], i["L1_attn_bp"]
    for n in "qkv":
        a[f"l1x_{n}"] = i[f"L1_xattn_W{n}"].T
    for n in "qk":
        a[f"l1x_b{n}"] = np.tile(i[f"L1_xattn_b{n}"].reshape(H, 64).T, (2, 1))
    a["l1x_bv"], a["l1x_bo"] = i["L1_xattn_bv"], i["L1_xattn_bo"]
    a["l1x_o"] = i["L1_xattn_Wo"].reshape(D, 2, 8, 64).transpose(1, 3, 2, 0).reshape(P, 8, D)

    def experts(name):
        return np.concatenate([i["L1_ffn_" + name], i["L1_ffn_s" + name][None]], 0)

    for n in ("w1", "w3"):
        a["moe_" + n] = experts(n).reshape(E + 1, F, 2, D).transpose(3, 0, 2, 1)
    for n in ("b1", "b3"):
        a["moe_" + n] = experts(n).reshape(E + 1, F, 2).transpose(1, 0, 2)
    a["moe_w2"], a["moe_b2"] = experts("w2").transpose(2, 0, 1), experts("b2")
    a["moe_gateT"], a["moe_gate_b"] = i["L1_ffn_gate_w"].T, i["L1_ffn_gate_b"]
    a.update(_constants(np))
    a = {k: np.ascontiguousarray(v) for k, v in a.items()}

    nc = bacc.Bacc("TRN2", target_bir_lowering=False, num_devices=1)
    dram = {k: nc.dram_tensor(f"in_{k}", v.shape, mybir.dt.from_np(v.dtype), kind="ExternalInput").ap() for k, v in a.items()}
    out = nc.dram_tensor("out_x", (B, S, D), F32, kind="ExternalOutput").ap()
    decoder(nc, dram, out)
    r = run(nc, [{f"in_{k}": v for k, v in a.items()}], core_ids=[0])
    return r.results[0]["out_x"]
```

```python
from contextlib import ExitStack

import concourse.bass as bass
from concourse import mybir
from concourse.alu_op_type import AluOpType as ALU

ACT = mybir.ActivationFunctionType
AX = mybir.AxisListType.X
F32 = mybir.dt.float32
BF16 = mybir.dt.bfloat16
U8 = mybir.dt.uint8
U32 = mybir.dt.uint32

B, S, D = 4, 256, 128
P = 128
NB = 2
PASSES = B // NB
SB = S // P
TT = NB * SB
TOK = NB * S
H = 16
U = NB * H
HID = 512
HC = HID // P
E, F = 8, 128
EPS = 1e-5
BIG = 1e30
EXP_LN = "natural_log_exp_and_others"
MAGIC = 1.5 * 2.0 ** 23
Q4 = 4
EARLY = 4
TW = S + P


class Stage:

    def __init__(self, nc, name):
        self.nc, self.name, self.ctx, self.sems = nc, name, ExitStack(), []
        self.chained = 0

    def sb(self, name, shape, dt=F32):
        return self.ctx.enter_context(self.nc.sbuf_tensor(f"{self.name}_{name}", shape, dt))

    def psum_banks(self):
        return [self.ctx.enter_context(self.nc.psum_tensor(f"{self.name}_bank{i}", [P, 512], F32)) for i in range(8)]

    def sem(self, name):
        s = self.ctx.enter_context(self.nc.semaphore(f"{self.name}_{name}"))
        self.sems.append(s)
        return s

    def close(self):
        nums = sorted(s.num for s in self.sems)
        while nums:
            n = 1
            while n < len(nums) and nums[n] == nums[0] + n:
                n += 1
            self.nc.vector.sem_clear(range(nums[0], nums[0] + n))
            nums = nums[n:]
        self.nc.all_engine_barrier()
        self.ctx.close()


class Chain:

    def __init__(self, eng, sem):
        self.eng, self.sem, self.n = eng, sem, 0

    def __call__(self, ins):
        self.n += 1
        ins.then_inc(self.sem, 1)
        self.eng.wait_ge(self.sem, self.n)


def bcast(ap, n, width):
    return ap.unsqueeze(2).broadcast_to([ap.shape[0], n, width])



class Norm:

    def __init__(self, st, w, tag=""):
        self.w = w
        self.stats = st.sb(f"bn{tag}", [P, TT, 6])
        self.mv = st.sb(f"mv{tag}", [P, TT, 2])
        self.ve = st.sb(f"ve{tag}", [P, TT])
        self.rstd = st.sb(f"rstd{tag}", [P, TT])
        self.s_var = st.sem(f"var_ready{tag}")
        self.s_rstd = st.sem(f"rstd_ready{tag}")

    def vector_stats(self, dve, link, src):
        for t in range(TT):
            ins = dve.bn_stats(self.stats[:, t, :], src[:, t, :])
            if t == TT - 1:
                link(ins)
            else:
                ins.then_inc(link.sem, 1)
                link.n += 1
        for t in range(TT):
            ins = dve.bn_aggr(self.mv[:, t, :], self.stats[:, t, :])
            if t == TT - 1:
                link(ins)
            else:
                ins.then_inc(link.sem, 1)
                link.n += 1
        dve.tensor_scalar(self.ve[:], self.mv[:, :, 1], EPS, None, ALU.add).then_inc(self.s_var, 1)

    def gpsimd_rstd(self, pool):
        pool.wait_ge(self.s_var, 1)
        pool.tensor_tensor(self.rstd[:], self.ve[:], self.w["minus_half"][:, 0:TT], ALU.pow).then_inc(self.s_rstd, 1)

    def vector_apply(self, dve, out, src, s_done):
        dve.wait_ge(self.s_rstd, 1)
        for t in range(TT):
            dve.tensor_scalar(out[:, t, :], src[:, t, :], self.mv[:, t, 0:1], self.rstd[:, t:t + 1],
                              ALU.subtract, ALU.mult).then_inc(s_done, 1)


def tensor_transpose_tiles(pe, w, bank, src, s_src, s_done):
    for t in range(TT):
        pe.wait_ge(s_src, t + 1)
        ins = pe.transpose(bank[:, t * P:(t + 1) * P], src[:, t, :], w["ident"][:])
    ins.then_inc(s_done, 1)



class Attention:

    def __init__(self, st, w, *, causal, lse, scale, heads_per_out, q, k, values, out_rows, ring, masks=None, extra=False):
        self.st, self.w, self.causal, self.lse, self.scale = st, w, causal, lse, scale
        self.masks, self.ring = masks, ring
        self.HG, self.q, self.k, self.values, self.rows = heads_per_out, q, k, values, out_rows
        self.W = 3 * P if causal else 2 * S
        self.nmax = st.sb("nmax", [P, NB, SB, H])
        self.zsum = st.sb("zsum", [P, NB, SB, H]) if lse else None
        self.lnz = st.sb("lnz", [P, SB, H]) if lse else None
        self.shift = st.sb("shift", [P, SB, H])
        self.rest = st.sb("rest", [P, SB, H])
        self.parts = st.sb("parts", [P, NB, SB, P], BF16)
        self.shiftT = st.sb("shiftT", [P, NB, S], BF16)
        self.expT = st.sb("expT", [P, ring, self.W])
        self.s_s = st.sem("max_scores_ready")
        self.s_mx = st.sem("max_done")
        self.s_lse = st.sem("sum_done")
        self.s_ln = st.sem("log_ready")
        self.s_parts = st.sem("shift_parts_ready")
        self.s_tp = st.sem("shift_transposed")
        self.s_shT = st.sem("shiftT_ready")
        self.s_e = st.sem("exp_scores_ready")
        self.s_p = st.sem("exp_ready")
        self.s_pv = st.sem("exp_used")
        self.s_sum = st.sem("group_summed") if extra else self.s_pv
        self.s_og = st.sem("out_evicted")
        self.s_zero = st.sem("parts_zeroed")

    def tensor_S(self, pe, u, bank):
        b, h = divmod(u, H)
        if u >= 2:
            pe.wait_ge(self.s_lse if self.lse else self.s_mx, u - 1)
        if self.causal:
            pe.matmul(bank[:, 0:P], self.q(b, h, 0, P), self.k(b, h, 0, P), start=True, stop=False, skip_group_check=True)
            pe.matmul(bank[:, P:3 * P], self.q(b, h, P, P), self.k(b, h, 0, S), start=False, stop=False, skip_group_check=True)
            if self.masks:
                ins = pe.matmul(bank[:, 0:3 * P], self.w["ident_bf"][:], self.masks[0][:, b, :], start=False, stop=True, skip_group_check=True)
            else:
                for c in (0, 2 * P):
                    ins = pe.matmul(bank[:, c:c + P], self.w["ident_bf"][:], self.w["mask_q"][:], start=False, stop=True, skip_group_check=True)
        else:
            for c in range(SB):
                ins = pe.matmul(bank[:, c * S:(c + 1) * S], self.q(b, h, c * P, P), self.k(b, h, 0, S),
                                start=(c == 0), stop=True, skip_group_check=True)
        ins.then_inc(self.s_s, 1)

    def tensor_shift(self, pe, b, bank):
        pe.wait_ge(self.s_parts, b + 1)
        if b:
            pe.wait_ge(self.s_shT, b)
        view = bank[:, 0:P].bitcast(BF16)
        for c in range(SB):
            ins = pe.transpose(view[:, c * P:(c + 1) * P], self.parts[:, b, c, :], self.w["ident_bf"][:])
        ins.then_inc(self.s_tp, 1)

    def tensor_E(self, pe, u, bank):
        b, h = divmod(u, H)
        if h == 0:
            pe.wait_ge(self.s_shT, b + 1)
        if u >= 2:
            pe.wait_ge(self.s_p, u - 1)
        sel = self.w["sel"][:, h, :]
        sh = self.shiftT[:, b, :]
        second = P if self.causal else 0
        pe.matmul(bank[:, 0:S], sel, sh, start=True, stop=False, skip_group_check=True)
        pe.matmul(bank[:, S:self.W], sel, sh[:, second:S], start=False, stop=False, skip_group_check=True)
        pe.matmul(bank[:, 0:S], self.k(b, h, 0, P), self.q(b, h, 0, S), start=False, stop=not self.causal, skip_group_check=True)
        ins = pe.matmul(bank[:, S:self.W], self.k(b, h, P, P), self.q(b, h, second, S - second), start=False, stop=not self.causal, skip_group_check=True)
        if self.masks:
            ins = pe.matmul(bank[:, 0:self.W], self.w["ident_bf"][:], self.masks[1][:, b, :], start=False, stop=True, skip_group_check=True)
        elif self.causal:
            for c in (0, S):
                ins = pe.matmul(bank[:, c:c + P], self.w["ident_bf"][:], self.w["mask_k"][:], start=False, stop=True, skip_group_check=True)
        ins.then_inc(self.s_e, 1)

    def tensor_PV(self, pe, g, bank, part, extra=None):
        if part == 0:
            pe.wait_ge(self.s_p, self.HG * (g + 1))
            if g >= 2:
                pe.wait_ge(self.s_og, g - 1)
        second = P if self.causal and part == 1 else 0
        for u in range(self.HG * g, self.HG * (g + 1)):
            b, h = divmod(u, H)
            r = u % self.HG * self.rows
            e = self.expT[:, u % self.ring, :]
            if part < 2:
                lhsT, rhs = self.values(b, h, part), e[:, S:self.W] if part else e[:, 0:S]
            else:
                lhsT, rhs = extra(b, h, part - 2)
            ins = pe.matmul(bank[r:r + self.rows, second:S], lhsT, rhs, start=(part == 0), stop=(part == (3 if extra else 1)),
                            skip_group_check=True)
        if part == 1:
            ins.then_inc(self.s_pv, 1)
        if part == 3:
            ins.then_inc(self.s_sum, 1)

    def vector_max(self, dve, u, bank):
        b, h = divmod(u, H)
        dve.wait_ge(self.s_s, u + 1)
        if self.causal:
            dve.tensor_reduce(self.nmax[:, b, 0, h:h + 1], bank[:, 0:P], AX, ALU.max, negate=True)
            dve.tensor_reduce(self.nmax[:, b, 1, h:h + 1], bank[:, P:3 * P], AX, ALU.max, negate=True).then_inc(self.s_mx, 1)
        else:
            dve.tensor_reduce(self.nmax[:, b, :, h], bank[:, :].rearrange("p (c k) -> p c k", c=SB), AX, ALU.max,
                              negate=True).then_inc(self.s_mx, 1)

    def vector_parts(self, dve, link, b):
        dve.wait_ge(self.s_mx, H * (b + 1))
        src = self.nmax[:, b, :, :]
        if self.lse:
            dve.wait_ge(self.s_ln, b + 1)
            link(dve.scalar_tensor_tensor(self.shift[:], src, BIG / 2, src, ALU.is_lt, ALU.mult))
            link(dve.tensor_tensor(self.shift[:], self.shift[:], self.lnz[:], ALU.subtract))
            src = self.shift[:]
        if b == 0:
            dve.wait_ge(self.s_zero, 1)
        hi, mid, lo = (self.parts[:, b, :, i * H:(i + 1) * H] for i in range(3))
        link(dve.tensor_copy(hi, src))
        link(dve.tensor_tensor(self.rest[:], src, hi, ALU.subtract))
        link(dve.tensor_copy(mid, self.rest[:]))
        dve.tensor_tensor(lo, self.rest[:], mid, ALU.subtract).then_inc(self.s_parts, 1)

    def vector_shiftT(self, dve, b, bank):
        dve.wait_ge(self.s_tp, b + 1)
        dve.tensor_copy(self.shiftT[:, b, :], bank[:, 0:P].bitcast(BF16)).then_inc(self.s_shT, 1)

    def scalar_sum(self, act, u, bank):
        b, h = divmod(u, H)
        act.wait_ge(self.s_mx, u + 1)
        act.activation(bank[:, 0:P], bank[:, 0:P], ACT.Exp, bias=self.nmax[:, b, 0, h:h + 1], scale=self.scale,
                       accum_out=self.zsum[:, b, 0, h:h + 1])
        act.activation(bank[:, P:3 * P], bank[:, P:3 * P], ACT.Exp, bias=self.nmax[:, b, 1, h:h + 1], scale=self.scale,
                       accum_out=self.zsum[:, b, 1, h:h + 1]).then_inc(self.s_lse, 1)

    def scalar_log(self, act, b):
        act.wait_ge(self.s_lse, H * (b + 1))
        if b:
            act.wait_ge(self.s_parts, b)
        act.activation(self.lnz[:], self.zsum[:, b, :, :], ACT.Ln).then_inc(self.s_ln, 1)

    def scalar_exp(self, act, u, bank):
        act.wait_ge(self.s_e, u + 1)
        if u >= self.ring:
            act.wait_ge(self.s_pv, (u - self.ring) // self.HG + 1)
        act.activation(self.expT[:, u % self.ring, :], bank[:, 0:self.W], ACT.Exp, scale=self.scale).then_inc(self.s_p, 1)


def ahead(n, units, early):
    b, h = divmod(n, units)
    if b + 1 >= NB:
        return range(0)
    done, now = (min(units, k * units // (units - early)) for k in (h, h + 1))
    return range(units * (b + 1) + done, units * (b + 1) + now)


def split_columns(part_of):
    runs = []
    for i, x in enumerate(part_of):
        if runs and runs[-1][0] == x and runs[-1][1] + runs[-1][2] == i:
            runs[-1][2] += 1
        else:
            runs.append([x, i, 1])
    return runs


Q_PARTS = (0, 0, 0, 1, 1, 2)
K_PARTS = (0, 1, 2, 0, 1, 0)


def rel_attention(nc, w, x, x_in, ctx_in, cT):
    st = Stage(nc, "l0a")
    HD = D // H
    SW = 64
    xn = st.sb("xn", [P, TT, D])
    xT = st.sb("xT", [P, TOK])
    sp_ = st.sb("split", [P, 2, 3, 2 * D], BF16)
    sr = st.sb("rest_qk", [P, 2, 2 * D])
    stack = st.sb("stack", [P, 2, 2, H, SW], BF16)
    qkT = st.sb("qkT", [P, H // 2, 2, TOK], BF16)
    vals = st.sb("vals", [P, TT, H, 64])
    xb = st.sb("x_beta", [P, TT, D])
    y = st.sb("y", [P, TT, D])
    osb = st.sb("o", [P, 2, S])
    rz = st.sb("rz", [P, 2 * Q4])
    tmp = st.sb("tmp", [P, 2 * Q4, HD])
    norm, norm2 = Norm(st, w), Norm(st, w, "2")
    s_chain = st.sem("dve_chain")
    s_cTp, s_cT = st.sem("ctx_transposed"), st.sem("ctxT_ready")
    s_xn = st.sem("xn_ready")
    s_xTp = st.sem("x_transposed")
    s_xT = st.sem("xT_ready")
    s_qkv = st.sem("qkv_ready")
    s_split = st.sem("parts_ready")
    s_v = st.sem("values_ready")
    s_stq = st.sem("q_stack_ready")
    s_stk = st.sem("k_stack_ready")
    s_init = st.sem("buffers_set")
    s_stT = st.sem("stack_transposed")
    s_qkT = st.sem("qkT_ready")
    s_ob = st.sem("o_transposed")
    s_fin = st.sem("o_finished")
    s_y = st.sem("y_normalized")
    s_xb = st.sem("x_beta_ready")
    bank = st.psum_banks()
    SBK, EBK, OBK, G0, G1 = bank[0:2], bank[2:4], bank[4:6], bank[6], bank[7]

    def at(part, b, h, t0, n):
        r = SW * (h % 2)
        return qkT[r:r + SW, h // 2, part, b * S + t0:b * S + t0 + n]

    a = Attention(st, w, causal=False, lse=False, scale=float(D) ** -0.5, heads_per_out=Q4,
                  q=lambda b, h, t0, n: at(0, b, h, t0, n), k=lambda b, h, t0, n: at(1, b, h, t0, n),
                  values=lambda b, h, c: vals[:, b * SB + c, h, 0:32], out_rows=32,
                  ring=8, extra=True)

    def bias_term(b, h, c):
        return vals[:, b * SB + c, h, 32:64], w["toeplitz"][:, h, (1 - c) * P:(1 - c) * P + S]

    GROUPS = U // Q4
    LAG = 5
    def copy_stack(dve, t):
        for i in range(4):
            n = 4 * t + i
            dve.wait_ge(s_stT, n + 1)
            dve.tensor_copy(qkT[:, 2 * i:2 * i + 2, :, t * P:(t + 1) * P],
                            bank[6 + n % 2][:, 0:256].bitcast(BF16).rearrange("p (a q k) -> p a q k", a=2, q=2)
                            ).then_inc(s_qkT, 1)

    with nc.Block() as block:

        @block.gpsimd
        def _(pool):
            pool.memset(stack[:, :, :, :, 6 * HD:SW], 0.0).then_inc(s_init, 1)
            norm.gpsimd_rstd(pool)
            pool.memset(a.parts[:], 0.0).then_inc(a.s_zero, 1)
            pool.memset(vals[:, 2:TT], 0.0).then_inc(s_init, 1)
            w.loaded(pool, "l0a")
            w.loaded(pool, "x")
            pool.tensor_tensor(xb[:], x_in[:], w["beta"][:].unsqueeze(1).broadcast_to([P, TT, D]), ALU.add).then_inc(s_xb, 1)
            for t in range(TT):
                pool.wait_ge(s_split, t + 1)
                if t >= 2:
                    pool.wait_ge(s_stT, 4 * (t - 1))
                for part, i, n in split_columns(Q_PARTS):
                    out = stack[:, t % 2, 0, :, i * HD:(i + n) * HD].rearrange("p h (n d) -> p h n d", n=n)
                    src = sp_[:, t % 2, part, 0:D].rearrange("p (h d) -> p h d", h=H).unsqueeze(2).broadcast_to([P, H, n, HD])
                    ins = pool.tensor_copy(out, src)
                ins.then_inc(s_stq, 1)
            norm2.gpsimd_rstd(pool)

        @block.scalar
        def _(act):
            act.preload_act_table_set(EXP_LN)
            act.wait_ge(s_cTp, 1)
            act.activation(cT[:], bank[0][:, :], ACT.Copy).then_inc(s_cT, 1)
            act.wait_ge(s_xTp, 1)
            act.activation(xT[:], G0[:, :], ACT.Copy).then_inc(s_xT, 1)
            act.wait_ge(s_init, 4)
            for t in range(TT):
                act.wait_ge(s_split, t + 1)
                v = EBK[t % 2][:, 2 * D:3 * D].rearrange("p (h d) -> p h d", h=H)
                act.activation(vals[:, t, :, 0:HD], v, ACT.Copy)
                act.activation(vals[:, t, :, 48:48 + HD], v, ACT.Copy).then_inc(s_v, 1)
                if t >= 2:
                    act.wait_ge(s_stT, 4 * (t - 1))
                for part, i, n in split_columns(K_PARTS):
                    ins = act.activation(stack[:, t % 2, 1, :, i * HD:(i + n) * HD],
                                         sp_[:, t % 2, part, D:2 * D].rearrange("p (h d) -> p h d", h=H), ACT.Copy)
                ins.then_inc(s_stk, 1)
            for n in range(U + LAG):
                if n < U:
                    a.scalar_exp(act, n, EBK[n % 2])
                if n >= Q4 + LAG - 1 and (n - LAG + 1) % Q4 == 0:
                    g = (n - LAG + 1) // Q4 - 1
                    act.wait_ge(a.s_sum, g + 1)
                    if g >= 2:
                        act.wait_ge(s_ob, g - 1)
                    act.activation(osb[:, g % 2, :], OBK[g % 2][:, 0:S], ACT.Copy).then_inc(a.s_og, 1)

        @block.vector
        def _(dve):
            link = Chain(dve, s_chain)
            w.loaded(dve, "x")
            norm.vector_stats(dve, link, x_in)
            norm.vector_apply(dve, xn, x_in, s_xn)
            w.loaded(dve, "l0a")
            dve.memset(vals[:, 0:2], 0.0).then_inc(s_init, 1)
            dve.wait_ge(s_init, 3)
            dve.memset(vals[:, :, :, HD:HD + 1], 1.0).then_inc(s_init, 1)
            for t in range(TT):
                dve.wait_ge(s_qkv, t + 1)
                if t >= 2:
                    dve.wait_ge(s_stq, t - 1)
                    dve.wait_ge(s_stk, t - 1)
                qk = EBK[t % 2][:, 0:2 * D]
                hi, mid, lo = (sp_[:, t % 2, i, :] for i in range(3))
                link(dve.tensor_copy(hi, qk))
                link(dve.tensor_tensor(sr[:, t % 2, :], qk, hi, ALU.subtract))
                link(dve.tensor_copy(mid, sr[:, t % 2, :]))
                dve.tensor_tensor(lo, sr[:, t % 2, :], mid, ALU.subtract).then_inc(s_split, 1)
                if t:
                    copy_stack(dve, t - 1)
            copy_stack(dve, TT - 1)
            for u in range(H):
                a.vector_max(dve, u, SBK[u % 2])
            a.vector_parts(dve, link, 0)
            a.vector_shiftT(dve, 0, G0)
            for n in range(U + LAG + 1):
                b, h = divmod(n, H)
                if h == H - 1 and b + 1 < NB:
                    a.vector_shiftT(dve, b + 1, G0)
                for u in ahead(n, H, EARLY):
                    a.vector_max(dve, u, SBK[u % 2])
                if h == H - 1 - EARLY and b + 1 < NB:
                    a.vector_parts(dve, link, b + 1)
                if n >= Q4 + LAG and (n - LAG) % Q4 == 0:
                    g = (n - LAG) // Q4 - 1
                    b2, hg = divmod(g, H // Q4)
                    dve.wait_ge(s_ob, g + 1)
                    if g:
                        dve.wait_ge(s_fin, g)
                    o = G1[:, 0:SB * P].rearrange("p (c r) -> p c r", r=32)
                    link(dve.reciprocal(rz[:], o[:, :, HD]))
                    link(dve.tensor_tensor(tmp[:], o[:, :, 0:HD], bcast(rz[:], 2 * Q4, HD), ALU.mult))
                    dst = y[:, b2 * SB:(b2 + 1) * SB, hg * 32:(hg + 1) * 32].rearrange("p c (j d) -> p c j d", d=HD)
                    for c in range(SB):
                        ins = dve.tensor_tensor(dst[:, c], o[:, c * Q4:(c + 1) * Q4, 16:16 + HD],
                                                tmp[:, c * Q4:(c + 1) * Q4, :], ALU.add)
                    ins.then_inc(s_fin, 1)
            dve.wait_ge(s_fin, GROUPS)
            norm2.vector_stats(dve, link, y)
            norm2.vector_apply(dve, xn, y, s_y)
            dve.wait_ge(s_y, TT)
            dve.wait_ge(s_xb, 1)
            link(dve.tensor_tensor(y[:], xn[:], w["gamma"][:].unsqueeze(1).broadcast_to([P, TT, D]), ALU.mult))
            link(dve.tensor_tensor(x[:], y[:], xb[:], ALU.add))

        @block.tensor
        def _(pe):
            w.loaded(pe, "x")
            for t in range(TT):
                ins = pe.transpose(bank[0][:, t * P:(t + 1) * P], ctx_in[:, t, :], w["ident"][:])
            ins.then_inc(s_cTp, 1)
            tensor_transpose_tiles(pe, w, G0, xn, s_xn, s_xTp)
            w.loaded(pe, "l0a")
            pe.wait_ge(s_xT, 1)
            for t in range(TT + 1):
                if t < TT:
                    if t >= 2:
                        pe.wait_ge(s_split, t - 1)
                        pe.wait_ge(s_v, t - 1)
                    pe.matmul(EBK[t % 2][:, 0:3 * D], xT[:, t * P:(t + 1) * P], w["l0a_qkv"][:], start=True, stop=True).then_inc(s_qkv, 1)
                if t:
                    pe.wait_ge(s_stq, t)
                    pe.wait_ge(s_stk, t)
                    for i in range(4):
                        n = 4 * (t - 1) + i
                        if n >= 2:
                            pe.wait_ge(s_qkT, n - 1)
                        out = bank[6 + n % 2][:, 0:256].bitcast(BF16)
                        for hp in (2 * i, 2 * i + 1):
                            for part in range(2):
                                c = ((hp % 2) * 2 + part) * P
                                ins = pe.transpose(out[:, c:c + P], stack[:, (t - 1) % 2, part, 2 * hp:2 * hp + 2, :], w["ident_bf"][:])
                        ins.then_inc(s_stT, 1)
            pe.wait_ge(s_qkT, 4 * TT)
            w.loaded(pe, "toeplitz")
            pe.wait_ge(s_cT, 1)
            for u in range(H):
                a.tensor_S(pe, u, SBK[u % 2])
            a.tensor_shift(pe, 0, G0)
            for n in range(U + LAG + 1):
                b, h = divmod(n, H)
                if h == H - 1 and b + 1 < NB:
                    a.tensor_shift(pe, b + 1, G0)
                if n < U:
                    a.tensor_E(pe, n, EBK[n % 2])
                for u in ahead(n, H, EARLY):
                    a.tensor_S(pe, u, SBK[u % 2])
                if Q4 <= n < U + Q4:
                    a.tensor_PV(pe, n // Q4 - 1, OBK[(n // Q4 - 1) % 2], n % Q4, extra=bias_term)
                if n >= Q4 + LAG and (n - LAG) % Q4 == 0:
                    g = (n - LAG) // Q4 - 1
                    pe.wait_ge(a.s_og, g + 1)
                    if g:
                        pe.wait_ge(s_fin, g)
                    for c in range(SB):
                        ins = pe.transpose(G1[:, c * P:(c + 1) * P], osb[:, g % 2, c * P:(c + 1) * P], w["ident"][:])
                    ins.then_inc(s_ob, 1)
    st.close()

def cross_attention(nc, w, x, cT, x_in, ctx_in, dram, it):
    st = Stage(nc, "l0x")
    HD = 64
    HP = H // 2
    xn = st.sb("xn", [P, TT, D])
    xT = st.sb("xT", [P, TOK])
    qT = st.sb("qT", [P, HP, TOK])
    kT = st.sb("kT", [P, HP, TOK])
    vals = st.sb("vals", [P, TT, H * HD])
    oT = st.sb("oT", [P, HP, TOK])
    xb = st.sb("x_bias", [P, TT, D])
    pad8 = st.sb("padded_bytes", [P, NB, S // 4], U32)
    padk8 = st.sb("padded_key_bytes", [P, 1], U32)
    pad = st.sb("padded", [P, NB, S])
    padk = st.sb("padded_keys", [P, NB, SB])
    mask_q = st.sb("mask_q", [P, NB, 3 * P], BF16)
    mask_k = st.sb("mask_k", [P, NB, 3 * P], BF16)
    csum = st.sb("ctx_sum", [P, NB])
    csumB = st.sb("ctx_sum_by_token", [P, NB, P])
    closed = st.sb("no_open_key", [P, NB, SB])
    norm = Norm(st, w)
    s_chain = st.sem("dve_chain")
    s_xn = st.sem("xn_ready")
    s_tp = st.sem("transposed")
    s_xT = st.sem("xT_ready")
    s_xb = st.sem("x_bias_ready")
    s_pr = st.sem("projected")
    s_pa = st.sem("projection_by_scalar")
    s_pv = st.sem("projection_by_vector")
    s_wo = st.sem("product_ready")
    s_pad = st.sem("padding_loaded")
    s_neg = st.sem("padding_scaled")
    s_next = st.sem("next_inputs_loaded")
    s_mask = st.sem("masks_ready")
    s_cs = st.sem("ctx_sum_ready")
    s_cb = st.sem("ctx_sum_spread")
    s_mean = st.sem("mean_product_ready")
    s_x = st.sem("x_updated")
    bank = st.psum_banks()
    SBK, EBK, OBK, G0, G1 = bank[0:2], bank[2:4], bank[4:6], bank[6], bank[7]

    def at(buf, b, h, t0, n):
        r = HD * (h % 2)
        return buf[r:r + HD, h // 2, b * S + t0:b * S + t0 + n]

    a = Attention(st, w, causal=True, lse=True, scale=1.0, heads_per_out=2,
                  q=lambda b, h, t0, n: at(qT, b, h, t0, n), k=lambda b, h, t0, n: at(kT, b, h, t0, n),
                  values=lambda b, h, c: vals[:, b * SB + c, h * HD:(h + 1) * HD], out_rows=HD, ring=4,
                  masks=(mask_q, mask_k))

    v_jobs = [("v", t, i) for t in range(TT) for i in range(2)]
    jobs = v_jobs[:4] + [(kind, c, 0) for c in range(HP) for kind in "kq"] + v_jobs[4:]
    FIRST = 4
    plan = [("project", n) for n in range(FIRST + 2)]
    for c in range(HP):
        if c + 1 < HP:
            plan += [("project", FIRST + 2 * c + 2), ("project", FIRST + 2 * c + 3)]
        plan += [("maximum", 2 * c), ("maximum", 2 * c + 1)]
    plan += [("project", n) for n in range(FIRST + 2 * HP, len(jobs))]
    JB = bank[2:6]
    GROUPS = U // 2

    def destination(job):
        kind, c, i = job
        if kind == "k":
            return kT[:, c, :], 1.0
        if kind == "q":
            return qT[:, c, :], float(HD) ** -0.5
        return vals[:, c, i * 512:(i + 1) * 512], 1.0

    with nc.Block() as block:

        @block.sync
        def _(sp):
            sp.dma_start(pad8[:], dram["padded"][bass.ts(it, NB)].unsqueeze(0).broadcast_to([P, NB, S // 4])).then_inc(s_pad, 16)
            sp.dma_start(padk8[:], dram["padded_keys"][bass.ts(it, 1)].rearrange("o p c -> (o p) c")).then_inc(s_pad, 16)
            sp.dma_start(x_in[:], token_tiles(dram["x"][NB:][bass.ts(it, NB)])).then_inc(s_next, 16)
            sp.dma_start(ctx_in[:], token_tiles(dram["ctx_1024"][NB:][bass.ts(it, NB)])).then_inc(s_next, 16)
            sp.wait_ge(s_pad, 32)
            sp.wait_ge(s_next, 32)

        @block.gpsimd
        def _(pool):
            pool.memset(a.parts[:], 0.0).then_inc(a.s_zero, 1)
            norm.gpsimd_rstd(pool)
            w.loaded(pool, "l0x")
            pool.tensor_tensor(xb[:], x[:], w["l0x_bo"][:].unsqueeze(1).broadcast_to([P, TT, D]), ALU.add).then_inc(s_xb, 1)
            pool.wait_ge(s_pad, 32)
            pool.tensor_scalar(pad[:], pad8[:].bitcast(U8), -BIG, None, ALU.mult).then_inc(s_neg, 1)
            pool.tensor_scalar(padk[:].rearrange("p b c -> p (b c)"), padk8[:].bitcast(U8), -BIG, None, ALU.mult).then_inc(s_neg, 1)
            pool.wait_ge(s_neg, 2)
            for b in range(NB):
                pool.tensor_tensor(mask_q[:, b, 0:P], w["mask_q32"][:], pad[:, b, 0:P], ALU.add)
                pool.tensor_copy(mask_q[:, b, P:2 * P], pad[:, b, 0:P])
                pool.tensor_tensor(mask_q[:, b, 2 * P:3 * P], w["mask_q32"][:], pad[:, b, P:S], ALU.add)
                pool.tensor_tensor(mask_k[:, b, 0:P], w["mask_k32"][:], padk[:, b, 0:1].broadcast_to([P, P]), ALU.add)
                pool.tensor_copy(mask_k[:, b, P:2 * P], padk[:, b, 0:1].broadcast_to([P, P]))
                ins = pool.tensor_tensor(mask_k[:, b, 2 * P:3 * P], w["mask_k32"][:], padk[:, b, 1:2].broadcast_to([P, P]), ALU.add)
            ins.then_inc(s_mask, 1)
            pool.wait_ge(s_cs, 1)
            pool.tensor_copy(csumB[:], bcast(csum[:], NB, P)).then_inc(s_cb, 1)

        @block.scalar
        def _(act):
            act.preload_act_table_set(EXP_LN)
            for what, n in plan:
                if what == "maximum":
                    a.scalar_sum(act, n, SBK[n % 2])
                    if n == H - 1:
                        a.scalar_log(act, 0)
                elif n % 2 == 0:
                    out, scale = destination(jobs[n])
                    act.wait_ge(s_pr, n + 1)
                    act.activation(out, JB[n % 4][:, :], ACT.Copy, scale=scale).then_inc(s_pa, 1)
                    if n == FIRST:
                        act.wait_ge(s_tp, 1)
                        act.activation(xT[:], G1[:, :], ACT.Copy).then_inc(s_xT, 1)
            for n in range(U + 2):
                b, h = divmod(n, H)
                if n < U:
                    a.scalar_exp(act, n, EBK[n % 2])
                for u in ahead(n, H, EARLY):
                    a.scalar_sum(act, u, SBK[u % 2])
                if h == H - 1 - EARLY and b + 1 < NB:
                    a.scalar_log(act, b + 1)
                if n % 2 == 1 and n > 1:
                    g = n // 2 - 1
                    b2, c = divmod(g, HP)
                    act.wait_ge(a.s_pv, g + 1)
                    act.activation(oT[:, c, b2 * S:(b2 + 1) * S], OBK[g % 2][:, 0:S], ACT.Copy).then_inc(a.s_og, 1)

        @block.vector
        def _(dve):
            link = Chain(dve, s_chain)
            norm.vector_stats(dve, link, x)
            norm.vector_apply(dve, xn, x, s_xn)
            dve.tensor_reduce(csum[:], cT[:].rearrange("p (b s) -> p b s", b=NB), AX, ALU.add).then_inc(s_cs, 1)
            for what, n in plan:
                if what == "maximum":
                    a.vector_max(dve, n, SBK[n % 2])
                    if n == H - 1:
                        a.vector_parts(dve, link, 0)
                elif n % 2:
                    out, scale = destination(jobs[n])
                    dve.wait_ge(s_pr, n + 1)
                    if scale == 1.0:
                        ins = dve.tensor_copy(out, JB[n % 4][:, :])
                    else:
                        ins = dve.tensor_scalar(out, JB[n % 4][:, :], scale, None, ALU.mult)
                    ins.then_inc(s_pv, 1)
            a.vector_shiftT(dve, 0, G0)
            for n in range(U + 1):
                b, h = divmod(n, H)
                if h == H - 1 and b + 1 < NB:
                    a.vector_shiftT(dve, b + 1, G0)
                for u in ahead(n, H, EARLY):
                    a.vector_max(dve, u, SBK[u % 2])
                if h == H - 1 - EARLY and b + 1 < NB:
                    a.vector_parts(dve, link, b + 1)
            link(dve.tensor_scalar(closed[:], a.nmax[:, :, :, 0], BIG / 2, None, ALU.is_ge))
            dve.wait_ge(s_xb, 1)
            dve.wait_ge(s_mean, 1)
            for t in range(TT):
                b, c = divmod(t, SB)
                ins = dve.scalar_tensor_tensor(xb[:, t, :], G1[:, b * D:(b + 1) * D], closed[:, b, c:c + 1], xb[:, t, :], ALU.mult, ALU.add)
            link(ins)
            for t in range(TT):
                dve.wait_ge(s_wo, t + 1)
                dve.tensor_tensor(x[:, t, :], bank[t % 4][:, 0:D], xb[:, t, :], ALU.add).then_inc(s_x, 1)

        @block.tensor
        def _(pe):
            w.loaded(pe, "l0x_vo")
            w.loaded(pe, "l0x")
            for what, n in plan:
                if what == "maximum":
                    if n == 0:
                        pe.wait_ge(s_mask, 1)
                    if n % 2 == 0:
                        job = FIRST + n
                        pe.wait_ge(s_pa, job // 2 + 1)
                        pe.wait_ge(s_pv, job // 2 + 1)
                    a.tensor_S(pe, n, SBK[n % 2])
                    continue
                kind, c, i = jobs[n]
                if n == FIRST + 1:
                    tensor_transpose_tiles(pe, w, G1, xn, s_xn, s_tp)
                    pe.wait_ge(s_xT, 1)
                if n >= 4:
                    pe.wait_ge(s_pv if n % 2 else s_pa, n // 2 - 1)
                out = JB[n % 4][:, :]
                if kind == "v":
                    ins = pe.matmul(out, cT[:, c * P:(c + 1) * P], w["l0x_v"][:, i * 512:(i + 1) * 512], start=True, stop=True)
                else:
                    ins = pe.matmul(out, w[f"l0x_{kind}"][:, c * P:(c + 1) * P], (cT if kind == "k" else xT)[:], start=True, stop=True)
                ins.then_inc(s_pr, 1)
            pe.wait_ge(s_cb, 1)
            for b in range(NB):
                ins = pe.matmul(G1[:, b * D:(b + 1) * D], csumB[:, b, :], w["l0x_vo"][:], start=(b == 0), stop=True, skip_group_check=True)
            ins.then_inc(s_mean, 1)
            a.tensor_shift(pe, 0, G0)
            pe.wait_ge(s_pa, len(jobs) // 2)
            pe.wait_ge(s_pv, len(jobs) // 2)
            for n in range(U + 1):
                b, h = divmod(n, H)
                if h == H - 1 and b + 1 < NB:
                    a.tensor_shift(pe, b + 1, G0)
                if n < U:
                    a.tensor_E(pe, n, EBK[n % 2])
                for u in ahead(n, H, EARLY):
                    a.tensor_S(pe, u, SBK[u % 2])
                if n >= 2 and n % 2 == 0:
                    for part in range(2):
                        a.tensor_PV(pe, n // 2 - 1, OBK[(n // 2 - 1) % 2], part)
            for t in range(TT):
                pe.wait_ge(a.s_og, HP * (t // SB + 1))
                pe.wait_ge(a.s_p, U)
                for c in range(HP):
                    ins = pe.matmul(bank[t % 4][:, 0:D], oT[:, c, t * P:(t + 1) * P], w["l0x_o"][:, c, :],
                                    start=(c == 0), stop=(c == HP - 1))
                ins.then_inc(s_wo, 1)
    st.close()


def weight_levels(nc, w, raw):
    st = Stage(nc, "wq")
    psum_bank = st.psum_banks()
    part = st.sb("part", [P, 2])
    scale = st.sb("scale", [P, 2])
    r = st.sb("r", [P, 2, HID])
    HP = H // 2
    vT = st.sb("vT", [P, HP, P])
    s_sel, s_part, s_sum, s_chain, s_done = (st.sem(n) for n in ("groups_selected", "part_ready", "sum_ready", "dve_chain", "done"))
    s_vTp, s_vT, s_vo = (st.sem(n) for n in ("v_transposed", "vT_ready", "product_ready"))
    with nc.Block() as block:

        @block.gpsimd
        def _(pool):
            pool.tensor_tensor(w["sel_group"][:], bcast(w["group32"][:], 32, P), w["same_token32"][:].unsqueeze(1).broadcast_to([P, 32, P]),
                               ALU.add).then_inc(s_sel, 1)

        @block.vector
        def _(dve):
            link = Chain(dve, s_chain)
            w.loaded(dve, "ffn_raw")
            for i in range(2):
                ins = dve.tensor_reduce(part[:, i:i + 1], raw[i], AX, ALU.add, apply_absolute_value=True)
            ins.then_inc(s_part, 1)
            dve.wait_ge(s_sum, 1)
            mean = w["ffn_wmean"]
            link(dve.tensor_scalar(mean[:], psum_bank[0][:, 0:2], 1.0 / (HID * D), EPS, ALU.mult, ALU.max))
            link(dve.reciprocal(scale[:], mean[:]))
            for i in range(2):
                link(dve.tensor_scalar(r[:, i, :], raw[i], scale[:, i:i + 1], MAGIC, ALU.mult, ALU.add))
            link(dve.tensor_scalar(r[:], r[:], MAGIC, 1.0, ALU.subtract, ALU.min))
            dve.tensor_scalar(w["ffn_q"][:], r[:], -1.0, None, ALU.max).then_inc(s_done, 1)

        @block.tensor
        def _(pe):
            w.loaded(pe, "const")
            pe.wait_ge(s_part, 1)
            pe.matmul(psum_bank[0][:, 0:2], w["ones"][:], part[:], start=True, stop=True).then_inc(s_sum, 1)
            w.loaded(pe, "l0x_vo")
            for c in range(HP):
                ins = pe.transpose(psum_bank[1 + c // 4][:, c % 4 * P:(c % 4 + 1) * P], w["l0x_v"][:, c * P:(c + 1) * P], w["ident"][:])
            ins.then_inc(s_vTp, 1)
            pe.wait_ge(s_vT, 1)
            for c in range(HP):
                ins = pe.matmul(psum_bank[3][:, 0:D], vT[:, c, :], w["l0x_o"][:, c, :], start=(c == 0), stop=(c == HP - 1))
            ins.then_inc(s_vo, 1)

        @block.scalar
        def _(act):
            act.wait_ge(s_vTp, 1)
            for i in range(2):
                ins = act.activation(vT[:, 4 * i:4 * i + 4, :], psum_bank[1 + i][:, :].rearrange("p (c d) -> p c d", c=4), ACT.Copy)
            ins.then_inc(s_vT, 1)
            act.wait_ge(s_vo, 1)
            act.activation(w["l0x_vo"][:], psum_bank[3][:, 0:D], ACT.Copy, scale=1.0 / S)
    st.close()


def quantized_ffn(nc, w, x):
    st = Stage(nc, "ffn")
    xn = st.sb("xn", [P, TT, D])
    r = st.sb("r", [P, TT, HID])
    xq = st.sb("xq", [P, TT, D], BF16)
    xqT = st.sb("xqT", [P, TOK], BF16)
    amax = st.sb("amax", [P, 2, TT])
    inv = st.sb("inv", [P, 2, TT])
    scale = st.sb("scale", [P, 2, TT])
    dg = st.sb("diag", [P, TT, P])
    rowinv = st.sb("rowinv", [P, TOK])
    hp = st.sb("h", [P, HC, NB, S + 2])
    y = st.sb("conv", [P, HC, TOK])
    q2 = st.sb("q2", [P, TT, HID], BF16)
    q2T = st.sb("q2T", [P, HC, TOK], BF16)
    norm = Norm(st, w)
    names = ("dve_chain", "xn_ready", "diag_ready", "rowsum_ready", "rowinv_ready", "xq_ready", "xq_transposed", "xqT_ready",
             "hidden_ready", "hidden_scaled", "conv_ready", "act_ready", "act_transposed", "q2_ready", "q2_transposed", "q2T_ready",
             "product_ready", "x_updated", "inv_ready", "pads_zero", "act_scaled", "middle_tap_ready", "scales_ready")
    (s_chain, s_xn, s_dg, s_rs, s_ri, s_xq, s_xqt, s_xqT, s_h, s_hs, s_cv, s_ac, s_act, s_q2, s_q2t, s_q2T,
     s_pr, s_x, s_inv, s_pad, s_rd, s_mid, s_sc) = (st.sem(n) for n in names)
    bank = st.psum_banks()
    HB = [bank[2], bank[3], bank[0], bank[1]]

    def tokens(ap):
        return ap.rearrange("p (b s) -> p b s", b=NB)

    with nc.Block() as block:

        @block.gpsimd
        def _(pool):
            norm.gpsimd_rstd(pool)
            pool.memset(hp[:, :, :, 0:1], 0.0).then_inc(s_pad, 1)
            pool.memset(hp[:, :, :, S + 1:S + 2], 0.0).then_inc(s_pad, 1)
            pool.wait_ge(s_inv, 1)
            for t in range(TT):
                ins = pool.tensor_tensor(dg[:, t, :], w["ident"][:], inv[:, 0, t:t + 1].broadcast_to([P, P]), ALU.mult)
            ins.then_inc(s_dg, 1)

        @block.scalar
        def _(act):
            act.wait_ge(s_rs, 1)
            act.activation(rowinv[:], bank[0][:, :], ACT.Copy).then_inc(s_ri, 1)
            w.loaded(act, "ffn")
            cw = w["ffn_conv"]

            def silu(c):
                act.wait_ge(s_cv, c + 1)
                act.activation(y[:, c, :], y[:, c, :], ACT.Silu).then_inc(s_ac, 1)

            for c in range(HC):
                act.wait_ge(s_hs, c + 1)
                act.activation(tokens(y[:, c, :]), hp[:, c, :, 1:S + 1], ACT.Identity, scale=cw[:, c, 1:2], bias=cw[:, c, 3:4]).then_inc(s_mid, 1)
                if c:
                    silu(c - 1)
            silu(HC - 1)
            act.wait_ge(s_sc, 1)
            for t in range(TT):
                act.activation(r[:, t, :], bank[4 + t][:, :], ACT.Copy, scale=scale[:, 1, t:t + 1]).then_inc(s_rd, 1)
            for c in range(0, HC, 2):
                act.wait_ge(s_q2t, 1)
                act.activation(q2T[:, c, :], bank[c][:, 0:TOK // 2].bitcast(BF16), ACT.Copy).then_inc(s_q2T, 1)

        @block.vector
        def _(dve):
            link = Chain(dve, s_chain)

            def scales(i):
                a, n, s = amax[:, i, :], inv[:, i, :], scale[:, i, :]
                link(dve.tensor_scalar(a, a, EPS, None, ALU.max))
                link(dve.reciprocal(s, a))
                link(dve.tensor_scalar(n, a, 1.0 / 127.0, w["ffn_wmean"][:, i:i + 1], ALU.mult, ALU.mult))

            norm.vector_stats(dve, link, x)
            norm.vector_apply(dve, xn, x, s_xn)
            dve.wait_ge(s_xn, TT)
            link(dve.tensor_reduce(amax[:, 0, :], xn[:], AX, ALU.max, apply_absolute_value=True))
            scales(0)
            dve.tensor_scalar(scale[:, 0, :], scale[:, 0, :], 127.0, None, ALU.mult).then_inc(s_inv, 1)
            dve.wait_ge(s_inv, 1)
            for t in range(TT):
                ins = dve.tensor_scalar(r[:, t, 0:D], xn[:, t, :], scale[:, 0, t:t + 1], 127.0, ALU.mult, ALU.min)
            link(ins)
            link(dve.tensor_scalar(r[:, :, 0:D], r[:, :, 0:D], -128.0, MAGIC, ALU.max, ALU.add))
            dve.tensor_scalar(xq[:], r[:, :, 0:D], MAGIC, None, ALU.subtract).then_inc(s_xq, 1)
            dve.wait_ge(s_xqt, 1)
            dve.tensor_copy(xqT[:], bank[1][:, 0:TOK // 2].bitcast(BF16)).then_inc(s_xqT, 1)
            dve.wait_ge(s_ri, 1)
            dve.wait_ge(s_pad, 2)
            w.loaded(dve, "ffn")
            cw = w["ffn_conv"]
            for c in range(HC + 1):
                if c < HC:
                    dve.wait_ge(s_h, c + 1)
                    dve.tensor_tensor(hp[:, c, :, 1:S + 1], tokens(HB[c][:, :]), tokens(rowinv[:]), ALU.mult).then_inc(s_hs, 1)
                if c:
                    dve.wait_ge(s_mid, c)
                    v = tokens(y[:, c - 1, :])
                    link(dve.scalar_tensor_tensor(v, hp[:, c - 1, :, 0:S], cw[:, c - 1, 0:1], v, ALU.mult, ALU.add))
                    dve.scalar_tensor_tensor(v, hp[:, c - 1, :, 2:S + 2], cw[:, c - 1, 2:3], v, ALU.mult, ALU.add).then_inc(s_cv, 1)
            for t in range(TT):
                dve.wait_ge(s_act, t + 1)
                link(dve.tensor_reduce(amax[:, 1, t:t + 1], bank[4 + t][:, :], AX, ALU.max, apply_absolute_value=True))
            scales(1)
            dve.tensor_scalar(scale[:, 1, :], scale[:, 1, :], 127.0, None, ALU.mult).then_inc(s_sc, 1)
            for t in range(TT):
                dve.wait_ge(s_rd, t + 1)
                link(dve.tensor_scalar(r[:, t, :], r[:, t, :], 127.0, -128.0, ALU.min, ALU.max))
                link(dve.tensor_scalar(r[:, t, :], r[:, t, :], MAGIC, None, ALU.add))
                dve.tensor_scalar(q2[:, t, :], r[:, t, :], MAGIC, None, ALU.subtract).then_inc(s_q2, 1)
            for c in range(1, HC, 2):
                dve.wait_ge(s_q2t, 1)
                dve.tensor_copy(q2T[:, c, :], bank[c][:, 0:TOK // 2].bitcast(BF16)).then_inc(s_q2T, 1)
            for t in range(TT):
                dve.wait_ge(s_pr, t + 1)
                dve.scalar_tensor_tensor(x[:, t, :], bank[4 + t][:, 0:D], inv[:, 1, t:t + 1], x[:, t, :], ALU.mult, ALU.add).then_inc(s_x, 1)

        @block.tensor
        def _(pe):
            pe.wait_ge(s_dg, 1)
            for t in range(TT):
                ins = pe.matmul(bank[0][:, t * P:(t + 1) * P], w["ones"][:], dg[:, t, :], start=(t == 0), stop=True, skip_group_check=True)
            ins.then_inc(s_rs, 1)
            pe.wait_ge(s_xq, 1)
            for t in range(TT):
                ins = pe.transpose(bank[1][:, 0:TOK // 2].bitcast(BF16)[:, t * P:(t + 1) * P], xq[:, t, :], w["ident_bf"][:])
            ins.then_inc(s_xqt, 1)
            pe.wait_ge(s_xqT, 1)
            for c in range(HC):
                if c == 2:
                    pe.wait_ge(s_ri, 1)
                pe.matmul(HB[c][:, :], w["ffn_q"][:, 0, c * P:(c + 1) * P], xqT[:], start=True, stop=True).then_inc(s_h, 1)
            for c in range(HC):
                pe.wait_ge(s_ac, c + 1)
                for t in range(TT):
                    ins = pe.transpose(bank[4 + t][:, c * P:(c + 1) * P], y[:, c, t * P:(t + 1) * P], w["ident"][:])
                    if c == HC - 1:
                        ins.then_inc(s_act, 1)
            for t in range(TT):
                pe.wait_ge(s_q2, t + 1)
                for c in range(HC):
                    ins = pe.transpose(bank[c][:, 0:TOK // 2].bitcast(BF16)[:, t * P:(t + 1) * P], q2[:, t, c * P:(c + 1) * P], w["ident_bf"][:])
            ins.then_inc(s_q2t, 1)
            pe.wait_ge(s_q2T, HC)
            for t in range(TT):
                for c in range(HC):
                    ins = pe.matmul(bank[4 + t][:, 0:D], q2T[:, c, t * P:(t + 1) * P], w["ffn_q"][:, 1, c * P:(c + 1) * P],
                                    start=(c == 0), stop=(c == HC - 1))
                ins.then_inc(s_pr, 1)
    st.close()


class ContextHeads:

    HD = 64
    GT = P // H

    def __init__(self, st, w, cT, kT, vg, v_dram, order, vt):
        self.w, self.cT, self.kT, self.vg, self.v_dram = w, cT, kT, vg, v_dram
        self.order = order
        self.vt = vt
        self.s_pr = {"k": st.sem("ctx_keys_projected"), "v": st.sem("ctx_values_projected")}
        self.s_out = {"k": st.sem("ctx_keys_ready"), "v": st.sem("ctx_values_biased")}
        self.s_zero = st.sem("ctx_keys_zeroed")
        self.s_vs = st.sem("ctx_values_stored")
        self.s_vg = st.sem("ctx_values_regrouped")

    def gpsimd_zeros(self, pool):
        for u in range(NB):
            other = slice(self.HD * (1 - u), self.HD * (2 - u))
            pool.memset(self.kT[other, u, :, :], 0.0).then_inc(self.s_zero, 1)
            pool.wait_ge(self.s_zero, u + 1)

    def count(self, m):
        kind = self.order[m][0]
        return sum(k == kind for k, _ in self.order[:m + 1])

    def tensor_product(self, pe, m, banks):
        kind, i = self.order[m]
        if m >= len(banks):
            before = m - len(banks)
            pe.wait_ge(self.s_out[self.order[before][0]], self.count(before))
        out, HD = banks[m % len(banks)], self.HD
        if kind == "v":
            t, half = divmod(i, 2)
            ins = pe.matmul(out[:, :], self.cT[:, t * P:(t + 1) * P], self.w["l1x_v"][:, half * 512:(half + 1) * 512], start=True, stop=True)
        else:
            for j in range(2):
                for u in range(NB):
                    h = 2 * i + j
                    ins = pe.matmul(out[HD * u:HD * (u + 1), j * S:(j + 1) * S], self.w["l1x_k"][:, h * HD:(h + 1) * HD],
                                    self.cT[:, u * S:(u + 1) * S], start=(j == 0), stop=True, skip_group_check=True)
        ins.then_inc(self.s_pr[kind], 1)

    def tensor_done(self, pe):
        for kind, sem in self.s_out.items():
            n = sum(k == kind for k, _ in self.order)
            if n:
                pe.wait_ge(sem, n)

    def scalar_keys(self, act, m, banks):
        i = self.order[m][1]
        act.wait_ge(self.s_pr["k"], self.count(m))
        for j in range(2):
            h = 2 * i + j
            for u in range(NB):
                half = slice(self.HD * u, self.HD * (u + 1))
                ins = act.activation(self.kT[half, u, :, h], banks[m % len(banks)][half, j * S:(j + 1) * S], ACT.Identity,
                                     bias=self.w["l1x_bk"][half, h:h + 1])
        ins.then_inc(self.s_out["k"], 1)

    def vector_values(self, dve, m, banks):
        t, half = divmod(self.order[m][1], 2)
        dve.wait_ge(self.s_pr["v"], self.count(m))
        dve.tensor_tensor(self.vt[:, t % SB, half * 512:(half + 1) * 512], banks[m % len(banks)][:, :],
                          self.w["l1x_bv"][:, half * 512:(half + 1) * 512], ALU.add).then_inc(self.s_out["v"], 1)

    def sync_regroup(self, sp):
        tiles = [i // 2 for kind, i in self.order if kind == "v" and i % 2]
        for n, t in enumerate(tiles):
            sp.wait_ge(self.s_out["v"], 2 * n + 2)
            sp.dma_start(self.v_dram[t * P:(t + 1) * P, :], self.vt[:, t % SB, :]).then_inc(self.s_vs, 16)
            sp.wait_ge(self.s_vs, 16 * (n + 1))
            src = self.v_dram[t * P:(t + 1) * P, :].rearrange("(g t) (h d) -> (t h) g d", t=self.GT, d=self.HD)
            sp.dma_start(self.vg[:, t * (P // self.GT):(t + 1) * (P // self.GT), :], src).then_inc(self.s_vg, 16)
        sp.wait_ge(self.s_vg, 16 * len(tiles))


def alibi_attention(nc, w, x, cT, heads_kT, vg, v_dram):
    st = Stage(nc, "l1a")
    HK, DQ, DV = 4, 4, 8
    NQ, NV = H * DQ, HK * DV
    W = NQ + HK * DQ + NV
    SW = 32
    xn = st.sb("xn", [P, TT, D])
    xT = st.sb("xT", [P, TOK])
    NQK = NQ + HK * DQ
    sp_ = st.sb("split", [P, 2, 3, NQK], BF16)
    sr = st.sb("rest_qk", [P, 2, NQK])
    qT = st.sb("qT", [P, 4, TOK], BF16)
    kT = st.sb("kT", [P, HK, TOK], BF16)
    vals = st.sb("vals", [P, TT, HK, 32])
    xb = st.sb("x_bias", [P, TT, D])
    y, yT = xn, xT
    osb = st.sb("o", [P, 2, S])
    rz = st.sb("rz", [P, 2 * Q4])
    norm = Norm(st, w)
    s_chain = st.sem("dve_chain")
    s_xn = st.sem("xn_ready")
    s_xTp = st.sem("x_transposed")
    s_xT = st.sem("xT_ready")
    s_qkv = st.sem("qkv_ready")
    s_split = st.sem("parts_ready")
    s_v = st.sem("values_ready")
    s_stq = st.sem("q_stack_ready")
    s_stk = st.sem("k_stack_ready")
    s_init = st.sem("buffers_set")
    s_stT = st.sem("stack_transposed")
    s_qkT = st.sem("qkT_ready")
    s_ob = st.sem("o_transposed")
    s_fin = st.sem("o_finished")
    s_xb = st.sem("x_bias_ready")
    s_yT = st.sem("yT_ready")
    s_yTp = st.sem("y_transposed")
    s_wp = st.sem("product_ready")
    s_x = st.sem("x_updated")
    bank = st.psum_banks()
    SBK, EBK, OBK, G0, G1 = bank[0:2], bank[2:4], bank[4:6], bank[6], bank[7]

    def at(buf, i, b, t0, n):
        return buf[:, i, b * S + t0:b * S + t0 + n]

    a = Attention(st, w, causal=True, lse=False, scale=float(DQ) ** -0.5, heads_per_out=Q4,
                  q=lambda b, h, t0, n: at(qT, h // HK, b, t0, n), k=lambda b, h, t0, n: at(kT, h % HK, b, t0, n),
                  values=lambda b, h, c: vals[:, b * SB + c, h % HK, :], out_rows=32, ring=6)
    stack = a.expT[:].rearrange("p r w -> p (r w)").bitcast(BF16)[:, 0:TT * (H + HK) * SW].rearrange("p (t h s) -> p t h s", t=TT, h=H + HK)
    GROUPS = U // Q4
    LAG = 3
    heads = ContextHeads(st, w, cT, heads_kT, vg, v_dram,
                         [("k", i) for i in range(4)] + [x for i in range(4) for x in (("v", i), ("k", 4 + i))],
                         st.sb("v_tokens", [P, SB, H * 64]))
    CB = [bank[0], bank[1], bank[4], bank[5]]
    with nc.Block() as block:

        @block.sync
        def _(sp):
            heads.sync_regroup(sp)

        @block.gpsimd
        def _(pool):
            w.loaded(pool, "l1a")
            pool.memset(stack[:, :, :, 6 * DQ + 6:SW], 0.0).then_inc(s_init, 1)
            pool.memset(a.parts[:], 0.0).then_inc(a.s_zero, 1)
            for t in range(TT):
                pool.tensor_copy(stack[:, t, 0:H, 6 * DQ:6 * DQ + 6], w["alibi_q"][:, t % SB, :, :])
                ins = pool.tensor_copy(stack[:, t, H:H + HK, 6 * DQ:6 * DQ + 6],
                                       w["alibi_k"][:, t % SB, :].unsqueeze(1).broadcast_to([P, HK, 6]))
            ins.then_inc(s_init, 1)
            norm.gpsimd_rstd(pool)
            pool.tensor_tensor(xb[:], x[:], w["l1a_bp"][:].unsqueeze(1).broadcast_to([P, TT, D]), ALU.add).then_inc(s_xb, 1)
            for t in range(TT):
                pool.wait_ge(s_split, t + 1)
                for part, i, n in split_columns(Q_PARTS):
                    out = stack[:, t, 0:H, i * DQ:(i + n) * DQ].rearrange("p h (n d) -> p h n d", n=n)
                    src = sp_[:, t % 2, part, 0:NQ].rearrange("p (h d) -> p h d", h=H).unsqueeze(2).broadcast_to([P, H, n, DQ])
                    ins = pool.tensor_copy(out, src)
                ins.then_inc(s_stq, 1)
            pool.wait_ge(s_stq, TT)
            heads.gpsimd_zeros(pool)

        @block.scalar
        def _(act):
            act.preload_act_table_set(EXP_LN)
            w.loaded(act, "l1x")
            for m in range(4):
                heads.scalar_keys(act, m, CB)
            act.wait_ge(s_xTp, 1)
            act.activation(xT[:], G0[:, :], ACT.Copy).then_inc(s_xT, 1)
            act.wait_ge(s_init, 4)
            for t in range(TT):
                act.wait_ge(s_split, t + 1)
                act.activation(vals[:, t, :, 0:DV], EBK[t % 2][:, NQK:W].rearrange("p (h d) -> p h d", h=HK), ACT.Copy).then_inc(s_v, 1)
                for part, i, n in split_columns(K_PARTS):
                    ins = act.activation(stack[:, t, H:H + HK, i * DQ:(i + n) * DQ],
                                         sp_[:, t % 2, part, NQ:NQK].rearrange("p (h d) -> p h d", h=HK), ACT.Copy)
                ins.then_inc(s_stk, 1)
                heads.scalar_keys(act, 4 + 2 * t + 1, CB)
            for n in range(U + LAG):
                if n < U:
                    a.scalar_exp(act, n, EBK[n % 2])
                if n >= Q4 + LAG - 1 and (n - LAG + 1) % Q4 == 0:
                    g = (n - LAG + 1) // Q4 - 1
                    act.wait_ge(a.s_sum, g + 1)
                    if g >= 2:
                        act.wait_ge(s_ob, g - 1)
                    act.activation(osb[:, g % 2, :], OBK[g % 2][:, 0:S], ACT.Copy).then_inc(a.s_og, 1)
            act.wait_ge(s_yTp, 1)
            act.activation(yT[:], G0[:, :], ACT.Copy).then_inc(s_yT, 1)

        @block.vector
        def _(dve):
            link = Chain(dve, s_chain)
            norm.vector_stats(dve, link, x)
            dve.memset(kT[:], 0.0).then_inc(s_chain, 1)
            link.n += 1
            dve.memset(vals[:], 0.0).then_inc(s_init, 1)
            dve.wait_ge(s_init, 3)
            dve.memset(vals[:, :, :, DV:DV + 1], 1.0).then_inc(s_init, 1)
            norm.vector_apply(dve, xn, x, s_xn)
            for t in range(TT):
                dve.wait_ge(s_qkv, t + 1)
                if t >= 2:
                    dve.wait_ge(s_stq, t - 1)
                    dve.wait_ge(s_stk, t - 1)
                qk = EBK[t % 2][:, 0:NQK]
                hi, mid, lo = (sp_[:, t % 2, i, :] for i in range(3))
                link(dve.tensor_copy(hi, qk))
                link(dve.tensor_tensor(sr[:, t % 2, :], qk, hi, ALU.subtract))
                link(dve.tensor_copy(mid, sr[:, t % 2, :]))
                dve.tensor_tensor(lo, sr[:, t % 2, :], mid, ALU.subtract).then_inc(s_split, 1)
                if t == 0:
                    w.loaded(dve, "l1x")
                heads.vector_values(dve, 4 + 2 * t, CB)
            for g in range(5):
                dve.wait_ge(s_stT, g + 1)
                src = bank[6 + g % 2][:, 0:TOK // 2].bitcast(BF16)
                if g < 4:
                    ins = dve.tensor_copy(qT[:, g, :], src)
                else:
                    for j in range(HK):
                        r = slice(SW * j, SW * (j + 1))
                        ins = dve.tensor_copy(kT[r, j, :], src[r, :])
                ins.then_inc(s_qkT, 1)
            for u in range(H):
                a.vector_max(dve, u, SBK[u % 2])
            a.vector_parts(dve, link, 0)
            a.vector_shiftT(dve, 0, G0)
            for n in range(U + LAG + 1):
                b, h = divmod(n, H)
                if h == H - 1 and b + 1 < NB:
                    a.vector_shiftT(dve, b + 1, G0)
                for u in ahead(n, H, EARLY):
                    a.vector_max(dve, u, SBK[u % 2])
                if h == H - 1 - EARLY and b + 1 < NB:
                    a.vector_parts(dve, link, b + 1)
                if n >= Q4 + LAG and (n - LAG) % Q4 == 0:
                    g = (n - LAG) // Q4 - 1
                    b2, hg = divmod(g, H // Q4)
                    dve.wait_ge(s_ob, g + 1)
                    if g:
                        dve.wait_ge(s_fin, g)
                    o = G1[:, 0:SB * P].rearrange("p (c r) -> p c r", r=32)
                    link(dve.reciprocal(rz[:], o[:, :, DV]))
                    dst = y[:, b2 * SB:(b2 + 1) * SB, hg * 32:(hg + 1) * 32].rearrange("p c (j d) -> p c j d", d=DV)
                    for c in range(SB):
                        ins = dve.tensor_tensor(dst[:, c], o[:, c * Q4:(c + 1) * Q4, 0:DV],
                                                bcast(rz[:, c * Q4:(c + 1) * Q4], Q4, DV), ALU.mult)
                    ins.then_inc(s_fin, 1)
            dve.wait_ge(s_xb, 1)
            for t in range(TT):
                dve.wait_ge(s_wp, t + 1)
                dve.tensor_tensor(x[:, t, :], bank[t % 4][:, 0:D], xb[:, t, :], ALU.add).then_inc(s_x, 1)

        @block.tensor
        def _(pe):
            w.loaded(pe, "l1x")
            for m in range(4):
                heads.tensor_product(pe, m, CB)
            tensor_transpose_tiles(pe, w, G0, xn, s_xn, s_xTp)
            w.loaded(pe, "l1a")
            pe.wait_ge(s_xT, 1)
            for t in range(TT):
                if t >= 2:
                    pe.wait_ge(s_v, t - 1)
                pe.matmul(EBK[t % 2][:, 0:W], xT[:, t * P:(t + 1) * P], w["l1a_qkv"][:], start=True, stop=True).then_inc(s_qkv, 1)
                if t:
                    heads.tensor_product(pe, 2 + 2 * t, CB)
                    heads.tensor_product(pe, 3 + 2 * t, CB)
            for m in (10, 11):
                heads.tensor_product(pe, m, CB)
            pe.wait_ge(s_init, 4)
            for g in range(5):
                if g >= 2:
                    pe.wait_ge(s_qkT, g - 1)
                for t in range(TT):
                    pe.wait_ge(s_stq, t + 1)
                    pe.wait_ge(s_stk, t + 1)
                    ins = pe.transpose(bank[6 + g % 2][:, 0:TOK // 2].bitcast(BF16)[:, t * P:(t + 1) * P],
                                       stack[:, t, g * HK:(g + 1) * HK, :], w["ident_bf"][:])
                ins.then_inc(s_stT, 1)
            pe.wait_ge(s_qkT, 5)
            heads.tensor_done(pe)
            for u in range(H):
                a.tensor_S(pe, u, SBK[u % 2])
            a.tensor_shift(pe, 0, G0)
            for n in range(U + LAG + 1):
                b, h = divmod(n, H)
                if h == H - 1 and b + 1 < NB:
                    a.tensor_shift(pe, b + 1, G0)
                if n < U:
                    a.tensor_E(pe, n, EBK[n % 2])
                for u in ahead(n, H, EARLY):
                    a.tensor_S(pe, u, SBK[u % 2])
                if Q4 <= n < U + Q4 and n % Q4 < 2:
                    a.tensor_PV(pe, n // Q4 - 1, OBK[(n // Q4 - 1) % 2], n % Q4)
                if n >= Q4 + LAG and (n - LAG) % Q4 == 0:
                    g = (n - LAG) // Q4 - 1
                    pe.wait_ge(a.s_og, g + 1)
                    if g:
                        pe.wait_ge(s_fin, g)
                    for c in range(SB):
                        ins = pe.transpose(G1[:, c * P:(c + 1) * P], osb[:, g % 2, c * P:(c + 1) * P], w["ident"][:])
                    ins.then_inc(s_ob, 1)
            pe.wait_ge(s_fin, GROUPS)
            for t in range(TT):
                ins = pe.transpose(G0[:, t * P:(t + 1) * P], y[:, t, :], w["ident"][:])
            ins.then_inc(s_yTp, 1)
            pe.wait_ge(s_yT, 1)
            for t in range(TT):
                pe.matmul(bank[t % 4][:, 0:D], yT[:, t * P:(t + 1) * P], w["l1a_p"][:], start=True, stop=True).then_inc(s_wp, 1)
    st.close()


def head_attention(nc, w, x, cT, kT, vg, v_dram):
    st = Stage(nc, "l1x")
    HD = 64
    assert NB == 2
    GT = P // H
    NG = S // GT
    GB = 4
    NU = NB * NG // GB
    UB = NU // NB
    J = 8
    qT = st.sb("qT", [P, S, H])
    oT = st.sb("oT", [P, NB, J, H, S // 16])
    xb = st.sb("x_bias", [P, TT, D])
    bq = st.sb("q_bias", [P, H])
    nmax = st.sb("nmax", [P, NB, NG])
    zsum = st.sb("zsum", [P, NB, NG])
    lnz = st.sb("lnz", [P, NG])
    shift = st.sb("shift", [P, NG])
    rest = st.sb("rest", [P, NG])
    parts = st.sb("parts", [P, NB, P], BF16)
    shiftT = st.sb("shiftT", [P, NB, P], BF16)
    expT = st.sb("expT", [P, 3, GB * P])
    xn, xT = expT[:, 0, :].rearrange("p (t d) -> p t d", t=TT), expT[:, 1, :]
    norm = Norm(st, w)
    names = ("dve_chain", "xn_ready", "transposed", "xT_ready", "x_bias_ready", 
             "heads_projected", "heads_by_scalar", "heads_by_vector", "max_scores_ready", "max_done", "sum_done", "log_ready",
             "parts_set", "parts_ready", "shift_transposed", "shiftT_ready", "exp_scores_ready", "exp_ready", "exp_used",
             "out_evicted", "product_ready", "x_updated", "q_bias_ready")
    (s_chain, s_xn, s_tp, s_xT, s_xb, s_pr, s_pa, s_pv, s_s, s_mx, s_lse, s_ln, s_ps, s_parts, s_shp, s_shT,
     s_e, s_p, s_used, s_og, s_wo, s_x, s_bq) = (st.sem(n) for n in names)
    bank = st.psum_banks()
    SBK, EBK, OBK, G0, G1 = bank[0:2], bank[2:4], bank[4:6], bank[6], bank[7]
    PAIRS = H // 2
    EARLY_U = 3
    heads = ContextHeads(st, w, cT, kT, vg, v_dram, [("v", i) for i in range(2 * SB, 2 * TT)],
                         oT[:, 1].rearrange("p j h s -> p (j h s)").rearrange("p (c e) -> p c e", c=SB))

    def queries(n, i):
        g = n % UB * GB + i
        return qT[:, g * GT:(g + 1) * GT, :].rearrange("p t h -> p (t h)")

    def keys(n, i):
        u, q = divmod(n, UB)
        g = q * GB + i
        return kT[:, u, g * GT:(g + 1) * GT, :].rearrange("p t h -> p (t h)")

    with nc.Block() as block:

        @block.sync
        def _(sp):
            heads.sync_regroup(sp)

        @block.gpsimd
        def _(pool):
            w.loaded(pool, "l1x")
            pool.tensor_scalar(bq[:], w["l1x_bq"][:], float(HD) ** -0.5, None, ALU.mult).then_inc(s_bq, 1)
            pool.tensor_tensor(xb[:], x[:], w["l1x_bo"][:].unsqueeze(1).broadcast_to([P, TT, D]), ALU.add).then_inc(s_xb, 1)
            for u in range(NB):
                pool.memset(parts[:, u, 3 * NG + GT:P], 0.0)
                ins = pool.tensor_copy(parts[:, u, 3 * NG:3 * NG + GT], w["other_token"][:])
            ins.then_inc(s_ps, 1)
            norm.gpsimd_rstd(pool)

        @block.scalar
        def _(act):
            act.preload_act_table_set(EXP_LN)
            w.loaded(act, "l1x")
            act.wait_ge(s_bq, 1)
            act.wait_ge(s_tp, 1)
            act.activation(xT[:], G1[:, :], ACT.Copy).then_inc(s_xT, 1)
            for n in range(0, PAIRS, 2):
                act.wait_ge(s_pr, n + 1)
                for i in range(2):
                    h = 2 * n + i
                    ins = act.activation(qT[:, :, h], bank[n % 4][:, i * S:(i + 1) * S], ACT.Identity, bias=bq[:, h:h + 1],
                                         scale=float(HD) ** -0.5)
                ins.then_inc(s_pa, 1)

            def row_sums(n):
                u, q = divmod(n, UB)
                act.wait_ge(s_mx, n + 1)
                for i in range(GB):
                    part = SBK[n % 2][:, i * P:(i + 1) * P]
                    g = q * GB + i
                    ins = act.activation(part, part, ACT.Exp, bias=nmax[:, u, g:g + 1], accum_out=zsum[:, u, g:g + 1])
                ins.then_inc(s_lse, 1)

            def logs(u):
                act.wait_ge(s_lse, UB * (u + 1))
                if u:
                    act.wait_ge(s_parts, u)
                act.activation(lnz[:], zsum[:, u, :], ACT.Ln).then_inc(s_ln, 1)

            for n in range(UB):
                row_sums(n)
            logs(0)
            for n in range(NU + 1):
                if n < NU:
                    act.wait_ge(s_e, n + 1)
                    if n >= 3:
                        act.wait_ge(s_used, n - 2)
                    act.activation(expT[:, n % 3, :], EBK[n % 2][:, :], ACT.Exp).then_inc(s_p, 1)
                for m in ahead(n, UB, EARLY_U):
                    row_sums(m)
                if n % UB == UB - 1 - EARLY_U and n // UB + 1 < NB:
                    logs(n // UB + 1)

        @block.vector
        def _(dve):
            link = Chain(dve, s_chain)
            norm.vector_stats(dve, link, x)
            norm.vector_apply(dve, xn, x, s_xn)
            w.loaded(dve, "l1x")
            dve.wait_ge(s_bq, 1)
            for n in range(1, PAIRS, 2):
                dve.wait_ge(s_pr, n + 1)
                for i in range(2):
                    h = 2 * n + i
                    ins = dve.tensor_scalar(qT[:, :, h], bank[n % 4][:, i * S:(i + 1) * S], float(HD) ** -0.5, bq[:, h:h + 1],
                                            ALU.mult, ALU.add)
                ins.then_inc(s_pv, 1)

            def maxima(n):
                u, q = divmod(n, UB)
                dve.wait_ge(s_s, n + 1)
                dve.tensor_reduce(nmax[:, u, q * GB:(q + 1) * GB], SBK[n % 2][:, :].rearrange("p (g k) -> p g k", g=GB), AX, ALU.max,
                                  negate=True).then_inc(s_mx, 1)

            def split(u):
                dve.wait_ge(s_ln, u + 1)
                link(dve.tensor_tensor(shift[:], nmax[:, u, :], lnz[:], ALU.subtract))
                hi, mid, lo = (parts[:, u, i * NG:(i + 1) * NG] for i in range(3))
                link(dve.tensor_copy(hi, shift[:]))
                link(dve.tensor_tensor(rest[:], shift[:], hi, ALU.subtract))
                link(dve.tensor_copy(mid, rest[:]))
                dve.tensor_tensor(lo, rest[:], mid, ALU.subtract).then_inc(s_parts, 1)

            def copy_shift(u):
                dve.wait_ge(s_shp, u + 1)
                dve.tensor_copy(shiftT[:, u, :], G0[:, 0:P // 2].bitcast(BF16)).then_inc(s_shT, 1)

            for n in range(UB):
                maxima(n)
            split(0)
            for m in range(2):
                heads.vector_values(dve, m, OBK)
            copy_shift(0)
            for m in range(2, 4):
                heads.vector_values(dve, m, OBK)
            for n in range(NU + 2):
                u = n // UB
                if n % UB == UB - 1 and u + 1 < NB:
                    copy_shift(u + 1)
                for m in ahead(n, UB, EARLY_U):
                    maxima(m)
                if n % UB == UB - 1 - EARLY_U and u + 1 < NB:
                    split(u + 1)
                if n >= 2:
                    m = n - 2
                    u2, q = divmod(m, UB)
                    dve.wait_ge(s_used, m + 1)
                    if m == UB:
                        dve.wait_ge(heads.s_vs, 16 * SB)
                    out = oT[:, u2, :, :, 2 * q:2 * q + 2].rearrange("p j h s -> p s j h")
                    for s in range(2):
                        ins = dve.tensor_copy(out[:, s], OBK[m % 2][:, s * P:(s + 1) * P].rearrange("p (j h) -> p j h", j=J))
                    ins.then_inc(s_og, 1)
            dve.wait_ge(s_xb, 1)
            for t in range(TT):
                dve.wait_ge(s_wo, t + 1)
                dve.tensor_tensor(x[:, t, :], bank[t % 4][:, 0:D], xb[:, t, :], ALU.add).then_inc(s_x, 1)

        @block.tensor
        def _(pe):
            w.loaded(pe, "l1x")
            tensor_transpose_tiles(pe, w, G1, xn, s_xn, s_tp)
            pe.wait_ge(s_xT, 1)
            for n in range(PAIRS):
                if n >= 4:
                    pe.wait_ge(s_pv if n % 2 else s_pa, n // 2 - 1)
                for i in range(2):
                    for u in range(NB):
                        h = 2 * n + i
                        ins = pe.matmul(bank[n % 4][HD * u:HD * (u + 1), i * S:(i + 1) * S], w["l1x_q"][:, h * HD:(h + 1) * HD],
                                        xT[:, u * S:(u + 1) * S], start=(i == 0), stop=True, skip_group_check=True)
                ins.then_inc(s_pr, 1)
            pe.wait_ge(s_pa, PAIRS // 2)
            pe.wait_ge(s_pv, PAIRS // 2)

            def scores_for_max(n):
                if n >= 2:
                    pe.wait_ge(s_lse, n - 1)
                out = SBK[n % 2]
                pe.matmul(out[:, :], w["same_token"][:], w["other_token4"][:], start=True, stop=False, skip_group_check=True)
                for i in range(GB):
                    ins = pe.matmul(out[:, i * P:(i + 1) * P], queries(n, i), keys(n, i), start=False, stop=True, skip_group_check=True)
                ins.then_inc(s_s, 1)

            def scores_for_exp(n):
                u, q = divmod(n, UB)
                if n >= 2:
                    pe.wait_ge(s_p, n - 1)
                out = EBK[n % 2]
                for i in range(GB):
                    pe.matmul(out[:, i * P:(i + 1) * P], w["sel_group"][:, q * GB + i, :], shiftT[:, u, :], start=(i == 0), stop=False,
                              skip_group_check=True)
                for i in range(GB):
                    ins = pe.matmul(out[:, i * P:(i + 1) * P], keys(n, i), queries(n, i), start=False, stop=True, skip_group_check=True)
                ins.then_inc(s_e, 1)

            def weighted_values(n):
                u, q = divmod(n, UB)
                pe.wait_ge(s_p, n + 1)
                if n == 0:
                    heads.tensor_done(pe)
                if n == UB:
                    pe.wait_ge(heads.s_vg, 16 * SB)
                if n >= 2:
                    pe.wait_ge(s_og, n - 1)
                for i in range(GB):
                    r = HD * (i % 2)
                    ins = pe.matmul(OBK[n % 2][r:r + HD, (i // 2) * P:(i // 2 + 1) * P], vg[:, u * NG + q * GB + i, :],
                                    expT[:, n % 3, i * P:(i + 1) * P], start=(i < 2), stop=True, skip_group_check=True)
                ins.then_inc(s_used, 1)

            def transpose_shift(u):
                pe.wait_ge(s_ps, 1)
                pe.wait_ge(s_parts, u + 1)
                pe.transpose(G0[:, 0:P // 2].bitcast(BF16), parts[:, u, :], w["ident_bf"][:]).then_inc(s_shp, 1)

            for n in range(UB):
                scores_for_max(n)
            for m in range(2):
                heads.tensor_product(pe, m, OBK)
            transpose_shift(0)
            for m in range(2, 4):
                heads.tensor_product(pe, m, OBK)
            for n in range(NU + 1):
                u = n // UB
                if n % UB == UB - 1 and u + 1 < NB:
                    transpose_shift(u + 1)
                if n < NU:
                    if n % UB == 0:
                        pe.wait_ge(s_shT, u + 1)
                    scores_for_exp(n)
                for m in ahead(n, UB, EARLY_U):
                    scores_for_max(m)
                if n:
                    weighted_values(n - 1)
            pe.wait_ge(s_og, NU)
            for t in range(TT):
                u, c = divmod(t, SB)
                for j in range(J):
                    ins = pe.matmul(bank[t % 4][:, 0:D], oT[:, u, j, c * J:(c + 1) * J, :].rearrange("p h s -> p (h s)"),
                                    w["l1x_o"][:, j, :], start=(j == 0), stop=(j == J - 1))
                ins.then_inc(s_wo, 1)
    st.close()


def expert_ffn(nc, w, x):
    st = Stage(nc, "moe")
    NE = E + 1
    ALPHA, LIMIT = 1.702, 7.0
    xn = st.sb("xn", [P, TT, D])
    xT = st.sb("xT", [P, TOK])
    logit = st.sb("logit", [P, TT, E])
    small = st.sb("small", [P, 2, TT])
    score = st.sb("score", [P, TT, E])
    biased = st.sb("biased", [P, TT, E])
    above = st.sb("above", [P, TT, E, E])
    equal = st.sb("equal", [P, TT, E, E])
    rank = st.sb("rank", [P, TT, E])
    cw = st.sb("expert_weight", [P, TT, NE])
    cwT = st.sb("expert_weightT", [NE, TOK])
    h1 = st.sb("h1", [P, 2, TOK])
    hh = st.sb("h13", [P, 2, TOK])
    g = st.sb("gate", [P, 2, TOK])
    sg = st.sb("sigmoid", [P, 2, TOK])
    act_in = st.sb("l1g", [P, 2, TOK])
    a = st.sb("a", [P, 2, TOK])
    norm = Norm(st, w)
    names = ("dve_chain", "xn_ready", "transposed", "xT_ready", "logits_ready", "shifted_ready", "exp_ready", "cw_ready", "cw_transposed",
             "cwT_ready", "bias_ready", "x_seeded", "hidden_ready", "h1_ready", "h13_ready", "gate_ready", "sigmoid_ready", "lg_ready",
             "a_ready", "y_ready", "y_added")
    (s_chain, s_xn, s_tp, s_xT, s_lg, s_sh, s_ex, s_cw, s_cwp, s_cwT, s_b, s_xs, s_h, s_h1, s_hh, s_g, s_sg, s_l, s_a, s_y,
     s_ya) = (st.sem(n) for n in names)
    bank = st.psum_banks()
    G0, G1 = bank[6], bank[7]

    def pair(n):
        return bank[2 * (n % 3)], bank[2 * (n % 3) + 1]

    with nc.Block() as block:

        @block.gpsimd
        def _(pool):
            pool.memset(cw[:, :, E:NE], 1.0).then_inc(s_cw, 1)
            norm.gpsimd_rstd(pool)
            for e in range(NE):
                pool.wait_ge(s_l, e + 1)
                pool.wait_ge(s_sg, e + 1)
                if e >= 2:
                    pool.wait_ge(s_y, e - 1)
                pool.tensor_tensor(a[:, e % 2, :], act_in[:, e % 2, :], sg[:, e % 2, :], ALU.mult).then_inc(s_a, 1)

        @block.scalar
        def _(act):
            act.wait_ge(s_tp, 1)
            act.activation(xT[:], G0[:, :], ACT.Copy).then_inc(s_xT, 1)
            act.wait_ge(s_sh, 1)
            act.activation(score[:], logit[:], ACT.Exp).then_inc(s_ex, 1)
            w.loaded(act, "moe")

            def sigmoid(e):
                act.wait_ge(s_g, e + 1)
                if e >= 2:
                    act.wait_ge(s_a, e - 1)
                act.activation(sg[:, e % 2, :], g[:, e % 2, :], ACT.Sigmoid, scale=ALPHA).then_inc(s_sg, 1)

            for n in range(2 * NE):
                e, part = divmod(n, 2)
                act.wait_ge(s_h, n + 1)
                if n >= 2:
                    act.wait_ge(s_hh, n - 1)
                act.activation(h1[:, n % 2, :], pair(n)[0][:, :], ACT.Identity, bias=w["moe_b1"][:, e, part:part + 1]).then_inc(s_h1, 1)
                if part:
                    sigmoid(e)

        @block.vector
        def _(dve):
            link = Chain(dve, s_chain)
            norm.vector_stats(dve, link, x)
            norm.vector_apply(dve, xn, x, s_xn)
            dve.wait_ge(s_lg, 1)
            lg = G1[:, 0:TT * E].rearrange("p (t e) -> p t e", t=TT)
            link(dve.tensor_reduce(small[:, 0, :], lg, AX, ALU.max, negate=True))
            dve.tensor_tensor(logit[:], lg, bcast(small[:, 0, :], TT, E), ALU.add).then_inc(s_sh, 1)
            dve.wait_ge(s_ex, 1)
            w.loaded(dve, "moe")
            link(dve.tensor_reduce(small[:, 1, :], score[:], AX, ALU.add))
            link(dve.reciprocal(small[:, 0, :], small[:, 1, :]))
            link(dve.tensor_tensor(score[:], score[:], bcast(small[:, 0, :], TT, E), ALU.mult))
            link(dve.tensor_tensor(biased[:], score[:], w["moe_gate_b"][:].unsqueeze(1).broadcast_to([P, TT, E]), ALU.add))
            for t in range(TT):
                mine = bcast(biased[:, t, :], E, E)
                theirs = biased[:, t, :].unsqueeze(1).broadcast_to([P, E, E])
                dve.tensor_tensor(above[:, t], theirs, mine, ALU.is_gt)
                ins = dve.tensor_tensor(equal[:, t], theirs, mine, ALU.is_equal)
            link(ins)
            link(dve.tensor_tensor(equal[:], equal[:], w["before"][:].unsqueeze(1).broadcast_to([P, TT, E * E]).rearrange("p t (e f) -> p t e f", e=E), ALU.mult))
            link(dve.tensor_tensor(above[:], above[:], equal[:], ALU.add))
            link(dve.tensor_reduce(rank[:], above[:], AX, ALU.add))
            dve.wait_ge(s_cw, 1)
            dve.scalar_tensor_tensor(cw[:, :, 0:E], rank[:], 2.0, score[:], ALU.is_lt, ALU.mult).then_inc(s_cw, 1)
            dve.wait_ge(s_cwp, 1)
            dve.tensor_copy(cwT[:], G0[0:NE, :]).then_inc(s_cwT, 1)
            dve.wait_ge(s_b, 1)
            dve.tensor_tensor(x[:], x[:], G1[:, :].rearrange("p (t d) -> p t d", t=TT), ALU.add).then_inc(s_xs, 1)

            def add_expert(e):
                dve.wait_ge(s_y, e + 1)
                if e:
                    dve.wait_ge(s_ya, e)
                else:
                    dve.wait_ge(s_xs, 1)
                for t in range(TT):
                    ins = dve.scalar_tensor_tensor(x[:, t, :], bank[6 + e % 2][:, t * P:(t + 1) * P], cw[:, t, e:e + 1], x[:, t, :],
                                                   ALU.mult, ALU.add)
                ins.then_inc(s_ya, 1)

            for n in range(2 * NE):
                e, part = divmod(n, 2)
                dve.wait_ge(s_h1, n + 1)
                if n >= 2:
                    dve.wait_ge(s_g if part == 0 else s_l, n // 2)
                dve.scalar_tensor_tensor(hh[:, n % 2, :], pair(n)[1][:, :], w["moe_b3"][:, e, part:part + 1], h1[:, n % 2, :],
                                         ALU.add, ALU.mult).then_inc(s_hh, 1)
                dve.wait_ge(s_hh, n + 1)
                if part == 0:
                    if e >= 2:
                        dve.wait_ge(s_sg, e - 1)
                    dve.tensor_scalar(g[:, e % 2, :], hh[:, 0, :], LIMIT, None, ALU.min).then_inc(s_g, 1)
                else:
                    link(dve.tensor_scalar(hh[:, 1, :], hh[:, 1, :], LIMIT, -LIMIT, ALU.min, ALU.max))
                    if e >= 2:
                        dve.wait_ge(s_a, e - 1)
                    dve.scalar_tensor_tensor(act_in[:, e % 2, :], hh[:, 1, :], 1.0, g[:, e % 2, :], ALU.add, ALU.mult).then_inc(s_l, 1)
                    if e:
                        add_expert(e - 1)
            add_expert(NE - 1)

        @block.tensor
        def _(pe):
            tensor_transpose_tiles(pe, w, G0, xn, s_xn, s_tp)
            pe.wait_ge(s_xT, 1)
            w.loaded(pe, "moe")
            for t in range(TT):
                ins = pe.matmul(G1[:, t * E:(t + 1) * E], xT[:, t * P:(t + 1) * P], w["moe_gateT"][:], start=(t == 0), stop=True,
                                skip_group_check=True)
            ins.then_inc(s_lg, 1)

            def hidden(n):
                e, part = divmod(n, 2)
                if n >= 3:
                    pe.wait_ge(s_hh, n - 2)
                for out, name in zip(pair(n), ("moe_w1", "moe_w3")):
                    ins = pe.matmul(out[:, :], w[name][:, e, part, :], xT[:], start=True, stop=True)
                ins.then_inc(s_h, 1)

            def expert_out(e):
                pe.wait_ge(s_a, e + 1)
                if e >= 2:
                    pe.wait_ge(s_ya, e - 1)
                for t in range(TT):
                    ins = pe.matmul(bank[6 + e % 2][:, t * P:(t + 1) * P], a[:, e % 2, t * P:(t + 1) * P], w["moe_w2"][:, e, :],
                                    start=(t == 0), stop=True, skip_group_check=True)
                ins.then_inc(s_y, 1)

            for n in range(3):
                hidden(n)
            pe.wait_ge(s_cw, 2)
            for t in range(TT):
                ins = pe.transpose(G0[0:NE, t * P:(t + 1) * P], cw[:, t, :], w["ident"][:])
            ins.then_inc(s_cwp, 1)
            pe.wait_ge(s_cwT, 1)
            for t in range(TT):
                ins = pe.matmul(G1[:, t * P:(t + 1) * P], cwT[:, t * P:(t + 1) * P], w["moe_b2"][:], start=(t == 0), stop=True,
                                skip_group_check=True)
            ins.then_inc(s_b, 1)
            pe.wait_ge(s_xs, 1)
            for n in range(3, 2 * NE):
                hidden(n)
                if n % 2 and n >= 3:
                    expert_out((n - 3) // 2)
            expert_out(NE - 1)
    st.close()



class Weights(dict):

    def __init__(self):
        super().__init__()
        self.groups = {}

    def loaded(self, eng, group):
        sem, count = self.groups[group]
        eng.wait_ge(sem, count)


def setup(nc, ctx, dram, x_in, ctx_in, raw):
    w = Weights()

    def sb(name, shape, dt=F32):
        t = ctx.enter_context(nc.sbuf_tensor(f"w_{name}", shape, dt))
        w[name] = t
        return t

    loads = {
        "const": [("ident", [P, P]), ("mask_q32", [P, P]), ("mask_k32", [P, P]), ("sel32", [P, H]), ("minus_half", [P, 8]), ("ones", [P, P]), ("group32", [P, 32]),
                  ("same_token32", [P, P]), ("other_rows32", [P, P]), ("other_token", [P, 8])],
        "l0a": [("l0a_qkv", [P, 3 * D]), ("gamma", [P, D]), ("beta", [P, D])],
        "l0x_vo": [("l0x_v", [P, H * 64]), ("l0x_o", [P, H // 2, D])],
        "toeplitz": [("toeplitz", [P, H, TW])],
        "l0x": [("l0x_k", [P, H * 64]), ("l0x_q", [P, H * 64]), ("l0x_bo", [P, D])],
        "ffn": [("ffn_conv", [P, HC, 4])],
        "l1a": [("l1a_qkv", [P, 112]), ("l1a_p", [P, D]), ("l1a_bp", [P, D]), ("alibi_q", [P, SB, H, 6]), ("alibi_k", [P, SB, 6])],
        "l1x": [("l1x_q", [P, H * 64]), ("l1x_k", [P, H * 64]), ("l1x_v", [P, H * 64]), ("l1x_o", [P, 8, D]), ("l1x_bq", [P, H]),
                ("l1x_bk", [P, H]), ("l1x_bv", [P, H * 64]), ("l1x_bo", [P, D])],
        "moe": [("moe_w1", [P, E + 1, 2, F]), ("moe_w3", [P, E + 1, 2, F]), ("moe_w2", [P, E + 1, D]), ("moe_b1", [P, E + 1, 2]),
                ("moe_b3", [P, E + 1, 2]), ("moe_b2", [E + 1, D]), ("moe_gateT", [P, E]), ("moe_gate_b", [P, E]), ("before", [P, E * E])],
    }
    todo = []
    s_x = ctx.enter_context(nc.semaphore("loaded_x"))
    s_raw = ctx.enter_context(nc.semaphore("loaded_ffn_raw"))
    w.groups["x"], w.groups["ffn_raw"] = (s_x, 32), (s_raw, 32)
    for g, items in loads.items():
        sem = ctx.enter_context(nc.semaphore(f"loaded_{g}"))
        for name, shape in items:
            t = sb(name, shape)
            src = dram[name]
            if len(src.shape) == 1:
                src = src.unsqueeze(0).broadcast_to([P, src.shape[0]])
            todo.append((t, src, sem))
        w.groups[g] = (sem, 16 * len(items))
    sb("ident_bf", [P, P], BF16)
    sb("mask_q", [P, P], BF16)
    sb("mask_k", [P, P], BF16)
    sb("sel", [P, H, P], BF16)
    sb("same_token", [P, P], BF16)
    sb("other_token4", [P, 4 * P], BF16)
    sb("sel_group", [P, 32, P], BF16)
    sb("l0x_vo", [P, D])
    sb("ffn_q", [P, 2, HID], BF16)
    sb("ffn_wmean", [P, 2])
    with nc.Block() as block:

        @block.sync
        def _(sp):
            sp.dma_start(x_in[:], token_tiles(dram["x"][0:NB])).then_inc(s_x, 16)
            for n, (t, src, sem) in enumerate(todo):
                sp.dma_start(t[:], src).then_inc(sem, 16)
                if n + 1 == len(loads["const"]):
                    sp.dma_start(ctx_in[:], token_tiles(dram["ctx_1024"][0:NB])).then_inc(s_x, 16)
                    sp.dma_start(raw[0], dram["ffn_w1T"]).then_inc(s_raw, 16)
                    sp.dma_start(raw[1], dram["ffn_w2T"]).then_inc(s_raw, 16)

        @block.vector
        def _(dve):
            w.loaded(dve, "const")
            dve.tensor_copy(w["ident_bf"][:], w["ident"][:])
            dve.tensor_copy(w["mask_q"][:], w["mask_q32"][:])
            dve.tensor_copy(w["mask_k"][:], w["mask_k32"][:])
            dve.tensor_copy(w["sel"][:], bcast(w["sel32"][:], H, P))
            dve.tensor_copy(w["same_token"][:], w["same_token32"][:])

        @block.gpsimd
        def _(pool):
            w.loaded(pool, "const")
            pool.tensor_copy(w["other_token4"][:].rearrange("p (a k) -> p a k", a=4), w["other_rows32"][:].unsqueeze(1).broadcast_to([P, 4, P]))
    return w


def decoder(nc, dram, out):
    with ExitStack() as ctx:
        x = ctx.enter_context(nc.sbuf_tensor("x", [P, TT, D], F32))
        x_in = ctx.enter_context(nc.sbuf_tensor("x_in", [P, TT, D], F32))
        ctx_in = ctx.enter_context(nc.sbuf_tensor("ctx_in", [P, TT, D], F32))
        cT = ctx.enter_context(nc.sbuf_tensor("ctxT", [P, TOK], F32))
        v_dram = nc.dram_tensor("l1x_values", (TOK, H * 64), F32, kind="Internal").ap()
        raw = x[:].rearrange("p t d -> p (t d)"), cT[:]
        w = setup(nc, ctx, dram, x_in, ctx_in, raw)
        weight_levels(nc, w, raw)
        with nc.Fori(0, PASSES) as it:
            rel_attention(nc, w, x, x_in, ctx_in, cT)
            cross_attention(nc, w, x, cT, x_in, ctx_in, dram, it)
            quantized_ffn(nc, w, x)
            with nc.sbuf_tensor("l1x_keysT", [P, NB, S, H], F32) as kT, nc.sbuf_tensor("l1x_v_groups", [P, TOK // (P // H), 64], F32) as vg:
                alibi_attention(nc, w, x, cT, kT, vg, v_dram)
                head_attention(nc, w, x, cT, kT, vg, v_dram)
            expert_ffn(nc, w, x)
            store(nc, w, x, out, it)


def token_tiles(batches):
    return batches.rearrange("b (c p) d -> p (b c) d", p=P)


def store(nc, w, x, out, it):
    st = Stage(nc, "store")
    s_out = st.sem("out_stored")
    st.sem("unused")
    with nc.Block() as block:

        @block.sync
        def _(sp):
            w.loaded(sp, "moe")
            sp.dma_start(token_tiles(out[bass.ts(it, NB)]), x[:]).then_inc(s_out, 16)
            sp.wait_ge(s_out, 16)
    st.close()



def _constants(np):
    r = np.arange(P)
    c = {"ident": np.eye(P), "mask_q32": np.where(r[None, :] > r[:, None], -BIG, 0.0),
         "mask_k32": np.where(r[:, None] > r[None, :], -BIG, 0.0), "minus_half": np.full((P, 8), -0.5), "ones": np.ones((P, P))}
    k = np.arange(P)
    c["sel32"] = (k[:, None] % H == np.arange(H)[None, :]) & (k[:, None] < 3 * H)
    c["group32"] = (k[:, None] % 32 == np.arange(32)[None, :]) & (k[:, None] < 96)
    c["same_token32"] = (k[:, None] - 96 == r[None, :] // H)
    c["other_rows32"] = np.where((k[:, None] >= 96) & (k[:, None] < 104) & (k[:, None] - 96 != r[None, :] // H), -BIG, 0.0)
    c["other_token"] = np.where(r[:, None] // H != np.arange(8)[None, :], -BIG, 0.0)
    c["before"] = np.broadcast_to((np.arange(E)[None, :] < np.arange(E)[:, None]).reshape(-1), (P, E * E))
    slopes = (2.0 ** (-8.0 * np.arange(1, H + 1) / H)).astype(np.float32)
    pos = np.arange(S).astype(np.float32).reshape(SB, P).T
    c["alibi_q"] = np.concatenate([np.broadcast_to(_parts(np, slopes), (P, SB, H, 3)), _parts(np, -slopes * pos[:, :, None])], -1)
    c["alibi_k"] = np.stack([pos] * 3 + [np.ones_like(pos)] * 3, -1)
    return {n: np.ascontiguousarray(v, np.float32) for n, v in c.items()}


def _parts(np, v):
    out = []
    for _ in range(3):
        m, e = np.frexp(v)
        h = np.ldexp(np.rint(m * 256.0) / 256.0, e).astype(np.float32)
        out.append(h)
        v = v - h
    return np.stack(out, -1)


def kernel(**inputs):
    import numpy as np
    import concourse.bacc as bacc
    from concourse.bass_utils import run_bass_kernel_spmd as run

    i = {k: np.asarray(v) for k, v in inputs.items()}
    a = {n: np.concatenate([i[n], np.zeros((NB, S, D), i[n].dtype)]) for n in ("x", "ctx_1024")}
    a["l0a_qkv"] = np.concatenate([i["L0_attn_Wq"].T, i["L0_attn_Wk"].T, i["L0_attn_Wv"].T], 1)
    a["gamma"], a["beta"] = i["L0_attn_ln_gamma"], i["L0_attn_ln_beta"]
    a["toeplitz"] = i["L0_attn_rel_bias_table"][(np.arange(TW)[None, :] - np.arange(P)[:, None] + P - 1)].transpose(0, 2, 1)
    for n in "qkv":
        a[f"l0x_{n}"] = i[f"L0_xattn_W{n}"]
    a["l0x_o"] = i["L0_xattn_Wo"].reshape(H // 2, P, D).transpose(1, 0, 2)
    a["l0x_bo"] = i["L0_xattn_bo"]
    padded = i["mask_BxS2_bf0"].view(np.uint8)
    a["padded"] = padded.view(np.uint32)
    a["padded_keys"] = np.ascontiguousarray(padded.reshape(PASSES, NB, SB, P).transpose(0, 3, 1, 2)).reshape(PASSES, P, NB * SB).view(np.uint32)
    a["ffn_w1T"] = i["L0_ffn_w1"].T
    a["ffn_w2T"] = i["L0_ffn_w2"].T.reshape(HC, P, D).transpose(1, 0, 2).reshape(P, HID)
    a["ffn_conv"] = np.concatenate([i["L0_ffn_conv_w"][:, 0, :], i["L0_ffn_conv_b"][:, None]], 1).reshape(HC, P, 4).transpose(1, 0, 2)
    a["l1a_qkv"] = np.concatenate([i["L1_attn_Wq"], i["L1_attn_Wk"], i["L1_attn_Wv"]], 1)
    a["l1a_p"], a["l1a_bp"] = i["L1_attn_Wp"], i["L1_attn_bp"]
    for n in "qkv":
        a[f"l1x_{n}"] = i[f"L1_xattn_W{n}"].T
    for n in "qk":
        a[f"l1x_b{n}"] = np.tile(i[f"L1_xattn_b{n}"].reshape(H, 64).T, (2, 1))
    a["l1x_bv"], a["l1x_bo"] = i["L1_xattn_bv"], i["L1_xattn_bo"]
    a["l1x_o"] = i["L1_xattn_Wo"].reshape(D, 2, 8, 64).transpose(1, 3, 2, 0).reshape(P, 8, D)

    def experts(name):
        return np.concatenate([i["L1_ffn_" + name], i["L1_ffn_s" + name][None]], 0)

    for n in ("w1", "w3"):
        a["moe_" + n] = experts(n).reshape(E + 1, F, 2, D).transpose(3, 0, 2, 1)
    for n in ("b1", "b3"):
        a["moe_" + n] = experts(n).reshape(E + 1, F, 2).transpose(1, 0, 2)
    a["moe_w2"], a["moe_b2"] = experts("w2").transpose(2, 0, 1), experts("b2")
    a["moe_gateT"], a["moe_gate_b"] = i["L1_ffn_gate_w"].T, i["L1_ffn_gate_b"]
    a.update(_constants(np))
    a = {k: np.ascontiguousarray(v) for k, v in a.items()}

    nc = bacc.Bacc("TRN2", target_bir_lowering=False, num_devices=1)
    dram = {k: nc.dram_tensor(f"in_{k}", v.shape, mybir.dt.from_np(v.dtype), kind="ExternalInput").ap() for k, v in a.items()}
    out = nc.dram_tensor("out_x", (B, S, D), F32, kind="ExternalOutput").ap()
    decoder(nc, dram, out)
    r = run(nc, [{f"in_{k}": v for k, v in a.items()}], core_ids=[0])
    return r.results[0]["out_x"]
```
